# Optimizing a Trainium2 kernel written in Bass

```python
import numpy as np
import jax
import jax.numpy as jnp

def _softmax(x, axis=-1):
    return jax.nn.softmax(x, axis=axis)

def _gelu(x):
    return jax.nn.gelu(x, approximate=True)

def _silu(x):
    return jax.nn.silu(x)

def _sigmoid(x):
    return jax.nn.sigmoid(x)

def _layernorm(x, axis=-1, eps=1e-05):
    m = jnp.mean(x, axis=axis, keepdims=True)
    v = jnp.var(x, axis=axis, keepdims=True)
    return (x - m) / jnp.sqrt(v + eps)

def _scatter_add(tgt, idx, src, axis=0):
    return tgt.at[idx].add(src)

def _segment_sum(src, seg, n):
    return jax.ops.segment_sum(src, seg, n)
kernel_name = 'mk_decoder_preln_d1_seqx_r4_f0c10a'

def setup_inputs(seed: int=0):
    np.random.seed(seed)
    _w = jnp.asarray

    def _rec_inputs():
        import jax
        import jax.numpy as jnp
        _rk = jax.random.key(seed)
        x = -0.0002928 + 1 * jax.random.normal(jax.random.fold_in(_rk, 1), (8, 256, 512), jnp.float32)
        _lenS = 256 - jax.random.randint(jax.random.fold_in(_rk, 7), (8,), 0, max(1, 256 // 4) + 1, jnp.int32)
        _lenS2 = 256 - jax.random.randint(jax.random.fold_in(_rk, 8), (8,), 0, max(1, 256 // 4) + 1, jnp.int32)
        _ctx_2048P = jax.random.normal(jax.random.fold_in(_rk, 11), (8, 16, 512), jnp.float32)
        _ctx_2048c = jax.random.dirichlet(jax.random.fold_in(_rk, 511), 0.3 * jnp.ones((16,), jnp.float32), (8, 256))
        _ctx_2048t = jnp.einsum('bsk,bkd->bsd', _ctx_2048c, _ctx_2048P)
        _ctx_2048t = _ctx_2048t * jax.lax.rsqrt(jnp.mean(jnp.square(_ctx_2048t)) + 1e-12) * 0.953939
        ctx_2048 = -1.39393e-06 + 0.999914 * (_ctx_2048t + 0.3 * jax.random.normal(jax.random.fold_in(_rk, 611), (8, 256, 512), jnp.float32))
        _validS = jnp.arange(256)[None, :] < _lenS[:, None]
        _validS2 = jnp.arange(256)[None, :] < _lenS2[:, None]
        _causal = jnp.tril(jnp.ones((256, 256), dtype=bool))
        mask_BxS2_if1 = jnp.where(jnp.ones((8, 256), dtype=bool), 1, 0).astype(jnp.int32)
        return (x, ctx_2048, mask_BxS2_if1)
    x, ctx_2048, mask_BxS2_if1 = _rec_inputs()

    def _L0_attn_setup():
        import jax, jax.numpy as jnp
        import numpy as np
        EPS = 1.1920929e-07

        def _rms(x):
            return x * jax.lax.rsqrt(jnp.mean(x * x, axis=-1, keepdims=True) + EPS)
        key = jax.random.key(seed)
        k0, k1, k2, k3 = jax.random.split(key, 4)
        B, S, D, DFF = (4, 512, 512, 2048)
        x = jax.random.normal(k0, (B, S, D), dtype=jnp.float32)
        w_qkv = jax.random.normal(k1, (3 * D, D), dtype=jnp.float32) * 0.02
        w_swiglu = jax.random.normal(k2, (2 * DFF, D), dtype=jnp.float32) * 0.02
        w_out = jax.random.normal(k3, (D, DFF), dtype=jnp.float32) * 0.02
        return {'x': x, 'w_qkv': w_qkv, 'w_swiglu': w_swiglu, 'w_out': w_out}
    _L0_attn_all = _L0_attn_setup()
    _L0_attn_in = {k: v for k, v in _L0_attn_all.items() if k in ('w_qkv', 'w_swiglu', 'w_out')}
    del _L0_attn_all

    def _L0_xattn_setup():
        import jax, jax.numpy as jnp
        import numpy as np
        D_MODEL = 512
        N_HEADS = 32
        N_GROUPS = 8
        HEAD_DIM = D_MODEL // N_HEADS
        BATCH, SEQ = (2, 256)
        NEG_INF = float('-inf')
        key = jax.random.key(seed)
        ks = jax.random.split(key, 9)
        s = 0.02
        return {'Q': jax.random.normal(ks[0], (BATCH, SEQ, D_MODEL), jnp.float32), 'K': jax.random.normal(ks[1], (BATCH, SEQ, D_MODEL), jnp.float32), 'V': jax.random.normal(ks[2], (BATCH, SEQ, D_MODEL), jnp.float32), 'attention_mask': jnp.ones((BATCH, SEQ), jnp.int32), 'w_q': jax.random.normal(ks[3], (D_MODEL, D_MODEL), jnp.float32) * s, 'w_k': jax.random.normal(ks[4], (HEAD_DIM * N_GROUPS, D_MODEL), jnp.float32) * s, 'w_v': jax.random.normal(ks[5], (HEAD_DIM * N_GROUPS, D_MODEL), jnp.float32) * s, 'w_o': jax.random.normal(ks[6], (D_MODEL, D_MODEL), jnp.float32) * s, 'b_o': jnp.zeros((D_MODEL,), jnp.float32)}
    _L0_xattn_all = _L0_xattn_setup()
    _L0_xattn_in = {k: v for k, v in _L0_xattn_all.items() if k in ('w_q', 'w_k', 'w_v', 'w_o', 'b_o')}
    del _L0_xattn_all

    def _L0_ffn_setup():
        import jax, jax.numpy as jnp
        import numpy as np
        B, S, DIM = (2, 512, 512)
        INTER = 256
        E = 8
        K = 2
        N_SHARED = 1
        ROUTE_SCALE = 1.0
        key = jax.random.key(seed)
        ks = jax.random.split(key, 8)
        s_in = 1.0 / np.sqrt(DIM)
        s_hid = 1.0 / np.sqrt(INTER)
        return {'x': jax.random.normal(ks[0], (B, S, DIM), dtype=jnp.float32), 'gate_w': jax.random.normal(ks[1], (E, DIM), dtype=jnp.float32) * s_in, 'w1': jax.random.normal(ks[2], (E, INTER, DIM), dtype=jnp.float32) * s_in, 'w2': jax.random.normal(ks[3], (E, DIM, INTER), dtype=jnp.float32) * s_hid, 'w3': jax.random.normal(ks[4], (E, INTER, DIM), dtype=jnp.float32) * s_in, 'ws1': jax.random.normal(ks[5], (N_SHARED * INTER, DIM), dtype=jnp.float32) * s_in, 'ws2': jax.random.normal(ks[6], (DIM, N_SHARED * INTER), dtype=jnp.float32) * s_hid, 'ws3': jax.random.normal(ks[7], (N_SHARED * INTER, DIM), dtype=jnp.float32) * s_in}
    _L0_ffn_all = _L0_ffn_setup()
    _L0_ffn_in = {k: v for k, v in _L0_ffn_all.items() if k in ('gate_w', 'w1', 'w2', 'w3', 'ws1', 'ws2', 'ws3')}
    del _L0_ffn_all
    return {'x': x, 'ctx_2048': ctx_2048, 'mask_BxS2_if1': mask_BxS2_if1, 'L0_attn_w_qkv': _L0_attn_in['w_qkv'], 'L0_attn_w_swiglu': _L0_attn_in['w_swiglu'], 'L0_attn_w_out': _L0_attn_in['w_out'], 'L0_xattn_w_q': _L0_xattn_in['w_q'], 'L0_xattn_w_k': _L0_xattn_in['w_k'], 'L0_xattn_w_v': _L0_xattn_in['w_v'], 'L0_xattn_w_o': _L0_xattn_in['w_o'], 'L0_xattn_b_o': _L0_xattn_in['b_o'], 'L0_ffn_gate_w': _L0_ffn_in['gate_w'], 'L0_ffn_w1': _L0_ffn_in['w1'], 'L0_ffn_w2': _L0_ffn_in['w2'], 'L0_ffn_w3': _L0_ffn_in['w3'], 'L0_ffn_ws1': _L0_ffn_in['ws1'], 'L0_ffn_ws2': _L0_ffn_in['ws2'], 'L0_ffn_ws3': _L0_ffn_in['ws3']}

def reference(x, ctx_2048, mask_BxS2_if1, L0_attn_w_qkv, L0_attn_w_swiglu, L0_attn_w_out, L0_xattn_w_q, L0_xattn_w_k, L0_xattn_w_v, L0_xattn_w_o, L0_xattn_b_o, L0_ffn_gate_w, L0_ffn_w1, L0_ffn_w2, L0_ffn_w3, L0_ffn_ws1, L0_ffn_ws2, L0_ffn_ws3):
    import jax
    import jax.numpy as jnp

    def _L0_attn_ref(x, w_qkv, w_swiglu, w_out):
        import jax, jax.numpy as jnp
        import numpy as np
        EPS = 1.1920929e-07

        def _rms(x):
            return x * jax.lax.rsqrt(jnp.mean(x * x, axis=-1, keepdims=True) + EPS)
        qkv = _rms(x) @ w_qkv.T
        q, k, v = jnp.split(qkv, 3, axis=-1)
        q = _rms(q)
        k = _rms(k)
        w = jnp.exp(k)
        kv_cum = jnp.cumsum(w * v, axis=1)
        w_cum = jnp.cumsum(w, axis=1)
        y = jax.nn.sigmoid(q) * (kv_cum / (w_cum + 1e-06))
        uv = y @ w_swiglu.T
        u, g = jnp.split(uv, 2, axis=-1)
        return x + u * jax.nn.silu(g) @ w_out.T

    def _L0_xattn_ref(Q, K, V, attention_mask, w_q, w_k, w_v, w_o, b_o):
        import jax, jax.numpy as jnp
        import numpy as np
        D_MODEL = 512
        N_HEADS = 32
        N_GROUPS = 8
        HEAD_DIM = D_MODEL // N_HEADS
        BATCH, SEQ = (2, 256)
        NEG_INF = float('-inf')
        B, S, D = Q.shape
        G, HG, HD = (N_GROUPS, N_HEADS // N_GROUPS, HEAD_DIM)
        q = (Q @ w_q.T).reshape(B, S, G, HG, HD)
        k = (K @ w_k.T).reshape(B, S, G, HD)
        v = (V @ w_v.T).reshape(B, S, G, HD)
        scale = jnp.sqrt(jnp.float32(HD))
        scores = jnp.einsum('bnghd,bmgd->bnghm', q, k) / scale
        pad = (attention_mask == 0)[:, None, None, None, :]
        scores = jnp.where(pad, NEG_INF, scores)
        causal = jnp.tril(jnp.ones((S, S), bool))[None, :, None, None, :]
        scores = jnp.where(causal, scores, NEG_INF)
        attn = jax.nn.softmax(scores, axis=-1)
        out = jnp.einsum('bnghm,bmgd->bnghd', attn, v).reshape(B, S, D)
        return out @ w_o.T + b_o

    def _L0_ffn_ref(x, gate_w, w1, w2, w3, ws1, ws2, ws3):
        import jax, jax.numpy as jnp
        import numpy as np
        B, S, DIM = (2, 512, 512)
        INTER = 256
        E = 8
        K = 2
        N_SHARED = 1
        ROUTE_SCALE = 1.0
        shape = x.shape
        xf = x.reshape(-1, DIM)
        scores = jax.nn.softmax(xf @ gate_w.T, axis=-1)
        weights, idx = jax.lax.top_k(scores, K)
        weights = weights * ROUTE_SCALE
        h = jnp.einsum('td,eid->eti', xf, w1)
        g = jax.nn.silu(h) * jnp.einsum('td,eid->eti', xf, w3)
        eo = jnp.einsum('eti,edi->etd', g, w2)
        comb = jnp.einsum('tke,tk->te', jax.nn.one_hot(idx, E, dtype=xf.dtype), weights)
        y = jnp.einsum('etd,te->td', eo, comb)
        z = jax.nn.silu(xf @ ws1.T) * (xf @ ws3.T) @ ws2.T
        return (y + z).reshape(shape)
    x = x + _L0_attn_ref(_layernorm(x, axis=-1), L0_attn_w_qkv, L0_attn_w_swiglu, L0_attn_w_out)
    x = x + _L0_xattn_ref(_layernorm(x, axis=-1), ctx_2048, ctx_2048, mask_BxS2_if1, L0_xattn_w_q, L0_xattn_w_k, L0_xattn_w_v, L0_xattn_w_o, L0_xattn_b_o)
    x = x + _L0_ffn_ref(_layernorm(x, axis=-1), L0_ffn_gate_w, L0_ffn_w1, L0_ffn_w2, L0_ffn_w3, L0_ffn_ws1, L0_ffn_ws2, L0_ffn_ws3)
    return x

_drawn_inputs = setup_inputs


def setup_inputs(seed=0):
    import zlib

    import numpy as np

    out = dict(_drawn_inputs(seed))
    spreads = {'L0_xattn_b_o': (0.0, 2.0)}
    factors = {'L0_attn_w_qkv': 8.0,
     'L0_attn_w_swiglu': 8.0,
     'L0_attn_w_out': 8.0,
     'L0_xattn_w_q': 64.0,
     'L0_xattn_w_k': 64.0,
     'ctx_2048': 8.0,
     'L0_xattn_w_v': 8.0,
     'L0_xattn_w_o': 8.0,
     'L0_ffn_gate_w': 8.0,
     'L0_ffn_w1': 8.0,
     'L0_ffn_w2': 8.0,
     'L0_ffn_w3': 8.0,
     'L0_ffn_ws1': 5.836,
     'L0_ffn_ws2': 5.449,
     'L0_ffn_ws3': 5.476}
    for name, (base, spread) in spreads.items():
        noise = np.random.default_rng([zlib.crc32(name.encode()), seed]).standard_normal(out[name].shape)
        drawn = base * np.exp(spread * noise) if base else spread * noise
        out[name] = jnp.asarray(drawn.astype(out[name].dtype))
    for name, factor in factors.items():
        out[name] = (out[name] * factor).astype(out[name].dtype)
    return out
```

```python
from contextlib import ExitStack

import concourse.bass as bass
from concourse import mybir
from concourse.alu_op_type import AluOpType as ALU

ACT = mybir.ActivationFunctionType
AX = mybir.AxisListType
F32 = mybir.dt.float32
F32R = mybir.dt.float32r
U32 = mybir.dt.uint32
I32 = mybir.dt.int32

P = 128
D = 512
KB = D // P
BATCH, SEQ = 8, 256
TPB = SEQ // P
TILES = BATCH * TPB
DFF = 2048
GROUP = 256
JB = GROUP // P
MLP_GROUPS = DFF // GROUP
EXPERTS = 8
CHUNK = 512
CHUNKS = BATCH * SEQ // CHUNK
TPC = CHUNK // P
SLOT = (2 * JB * KB + JB * KB) * P
HEADS, KVG, HD = 32, 8, 16
PAIRS = KVG // 2
UNITS = 3 * PAIRS
LN_EPS = 1e-5
RMS_EPS = 1.1920929e-07
MASKED = -1e37

SLOT_QKV, SLOT_MLP, SLOT_X = 0, 2, 2 + MLP_GROUPS
SLOT_O = SLOT_X + 1
SLOT_MOE = SLOT_X + 2
SLOTS = SLOT_MOE + 1 + EXPERTS


def hold(eng, sem, value, settled):
    eng.wait_ge(sem, value)
    eng.sem_inc(settled, 1)


class Chain:

    def __init__(self, eng, sem, base=0, per=None, settled=None):
        self.eng, self.sem, self.base, self.n, self.per, self.settled = eng, sem, base, 0, per, settled

    def mark(self, ins):
        self.n += 1
        ins.then_inc(self.sem, 1)
        return self.n

    def wait(self, n):
        self.eng.wait_ge(self.sem, self.base + n)
        if self.settled is not None:
            self.eng.sem_inc(self.settled, 1)

    def link(self, ins):
        self.wait(self.mark(ins))

    def done(self):
        assert self.per is None or self.n == self.per, (self.n, self.per)


def decoder_layer(nc: bass.Bass, x, weights, ctx_t, mask, b_o, out):
    with ExitStack() as es:
        start = (nc.sbuf_base + 63) // 64 * 64
        place = [start]

        def at(name, shape, dt, off=None):
            size = 4
            for n in shape[1:]:
                size *= n
            if off is None:
                off = place[0]
                place[0] += (size + 31) // 32 * 32
            assert off + size <= nc.sbuf_usable_end, (name, off + size)
            return nc.alloc_sbuf_tensor_at(name, shape, dt, offset=off)

        acc = at("acc", [P, TILES, D], F32)
        feat_at = place[0]
        feat = at("feat", [P, 2, KB, BATCH * SEQ], F32R)
        wsplit = at("wsplit", [P, 2, 2, SLOT], F32R)
        wraw = at("wraw", [P, 2, SLOT], F32)
        ident = at("ident", [P, P], F32)
        tri_f = at("tri_f", [P, 2 * P], F32)
        tri = at("tri", [P, 2 * P], F32R)
        causal = at("causal", [P, SEQ], F32)
        half_neg = at("half_neg", [P, 4], F32)
        ones_row = at("ones_row", [1, P], F32R)
        iota8 = at("iota8", [P, EXPERTS], F32)
        comb = at("comb", [P, TILES, EXPERTS], F32)
        stats = at("stats", [P, TPB, 6], F32)
        mv = at("mv", [P, TPB, 2], F32)
        ln = at("ln", [P, TPB, 8], F32)
        rq = at("rq", [P, 8], F32)
        sums = at("sums", [P, 4], F32)
        temp_at = place[0]

        def region(first):
            place[0] = first

        ha = at("ha", [P, D], F32)
        hTa = at("hTa", [P, 2, KB, P], F32R)
        e_q = at("e_q", [P, TPB, D], F32)
        w_k = at("w_k", [P, D], F32)
        wv_f = at("wv_f", [P, D], F32)
        wv_s = at("wv_s", [P, TPB, 2, 2, D], F32R)
        wce = at("wce", [P, 2 * SEQ], F32)
        den = at("den", [P, 2 * SEQ], F32)
        region(temp_at)
        m_s = at("m_s", [P, 2, 2, JB, CHUNK], F32R)
        m_f = at("m_f", [P, JB, CHUNK], F32)
        sg = at("sg", [P, JB, CHUNK], F32)
        mlp_end = place[0]
        hd = at("hd", [P, 2, D], F32)
        gl = at("gl", [P, 8, EXPERTS], F32)
        gi = at("gi", [P, EXPERTS], U32)
        region(temp_at)
        q4 = at("q4", [P, HEADS, 4, HD], F32)
        k4 = at("k4", [P, TPB, KVG, 4, HD], F32)
        v17 = at("v17", [P, TPB, KVG, HD + 1], F32)
        sc = at("sc", [P, 2, 8, P], F32)
        pt = at("pt", [P, 2, 8, P], F32)
        mxs = at("mxs", [P, 2, 8], F32)
        nmx = at("nmx", [P, 2, 8], F32)
        rden = at("rden", [P, 2, 8], F32)
        region(feat_at)
        q4T = at("q4T", [P, HEADS // 2, SEQ], F32R)
        k4T = at("k4T", [P, PAIRS, SEQ], F32R)
        ctx_s = at("ctx_s", [P, 2, KB, SEQ], F32R)
        hTc = at("hTc", [P, TPB, 2, KB, P], F32R)
        oT = at("oT", [P, TPB, 2, KB, P], F32R)
        ctx_raw = at("ctx_raw", [P, KB, SEQ], F32)
        o_tok = at("o_tok", [P, TPB, D], F32)
        bo_raw = at("bo_raw", [1, D], F32)
        bo = at("bo", [1, 2, D], F32R)
        hc = at("hc", [P, D], F32)
        msk_i = at("msk_i", [P, SEQ], I32)
        msk = at("msk", [P, 3, P], F32)
        assert place[0] <= feat_at + 65536

        ps = es.enter_context(nc.psum_tensor("ps", [P, 8, 512], F32))

        names = set()

        def sem(name):
            assert name not in names
            names.add(name)
            return es.enter_context(nc.semaphore(name))

        raw_loaded = [sem(f"raw_loaded{p}") for p in range(2)]
        w_ready = [sem(f"w_ready{p}") for p in range(2)]
        w_free = [sem(f"w_free{p}") for p in range(2)]
        pool_self = sem("pool_self")
        pool_held = sem("pool_held")
        dve_held = sem("dve_held")
        consts = sem("consts")
        x_first = sem("x_first")
        x_rest = sem("x_rest")
        a = {n: sem("a_" + n) for n in (
            "stats", "rstd", "h", "acc", "hT_ps", "hT_hi", "hT", "q", "k", "v", "ssq", "rms", "e", "w",
            "wv", "split", "pool", "dve", "scan", "wce", "den", "y", "yhi", "yT")}
        c = {n: sem("c_" + n) for n in (
            "bo", "bo_s", "ctx", "ctx_s", "mask_i", "stats", "rstd", "h", "hT_ps", "hT_hi", "hT", "kv", "khi", "k4", "v17",
            "k4T_ps", "k4T", "q", "qhi", "q4", "q4T_ps", "q4T_e", "mask", "dve", "pool", "S", "mx", "nmx", "P",
            "PT_ps", "PT_act", "PT_dve", "O", "o", "oT_ps", "oT_hi", "oT", "wo", "acc", "ones")}
        d = {n: sem("d_" + n) for n in (
            "stats", "rstd", "h", "hT_ps", "hT_hi", "hT", "dve", "pool", "logit", "nmx", "ex", "comb", "iota")}
        mlp = [{n: sem(f"mlp{i}_{n}") for n in ("up", "silu", "m", "hi", "lo", "down", "acc")} for i in range(2)]
        stored = sem("stored")

        block = es.enter_context(nc.Block())

        def slot_block(p, part, at_, n):
            return wsplit[:, p, part, at_:at_ + n]

        @block.sync
        def _(sp):
            x_v = x.rearrange("(t p) d -> p t d", p=P)
            out_v = out.rearrange("(t p) d -> p t d", p=P)
            sp.dma_start(acc[:, 0:TPB, :], x_v[:, 0:TPB, :]).then_inc(x_first, 16)
            for s in range(2):
                sp.dma_start(wraw[:, s, :], weights[s]).then_inc(raw_loaded[s], 16)
            sp.dma_start(acc[:, TPB:TILES, :], x_v[:, TPB:TILES, :]).then_inc(x_rest, 16)
            with sp.Fori(1, SLOT_X // 2) as n:
                for p in range(2):
                    sp.wait_ge(w_ready[p], n)
                    sp.dma_start(wraw[:, p, :], weights[bass.ds(2 * n + p, 1)].rearrange("s p n -> (s p) n")).then_inc(raw_loaded[p], 16)
            n = SLOT_X // 2
            for p in range(2):
                sp.wait_ge(w_ready[p], n)
                sp.dma_start(wraw[:, p, :], weights[2 * n + p]).then_inc(raw_loaded[p], 16)

            def ctx_load(b):
                sp.dma_start(ctx_raw[:, :, :], ctx_t[bass.ds(b, 1)].rearrange("s p k n -> (s p) k n")).then_inc(c["ctx"], 16)

            sp.wait_ge(mlp[0]["down"], 4 * CHUNKS * MLP_GROUPS)
            sp.wait_ge(mlp[0]["acc"], 4 * CHUNKS * MLP_GROUPS)
            sp.dma_start(bo_raw[:, :], b_o).then_inc(c["bo"], 16)
            sp.dma_start(ctx_raw[:, :, :], ctx_t[0]).then_inc(c["ctx"], 16)
            sp.dma_start(msk_i[:, :], mask[0:1].broadcast_to([P, SEQ])).then_inc(c["mask_i"], 16)
            with sp.Fori(1, BATCH) as b:
                sp.wait_ge(c["ctx_s"], b)
                ctx_load(b)
                sp.wait_ge(c["mask"], b)
                sp.dma_start(msk_i[:, :], mask[bass.ds(b, 1)].broadcast_to([P, SEQ])).then_inc(c["mask_i"], 16)
            with sp.Fori(SLOT_MOE // 2, SLOTS // 2) as n:
                for p in range(2):
                    sp.wait_ge(w_ready[p], n)
                    sp.dma_start(wraw[:, p, :], weights[bass.ds(2 * n + p, 1)].rearrange("s p n -> (s p) n")).then_inc(raw_loaded[p], 16)
            sp.wait_ge(w_ready[0], SLOTS // 2)
            sp.dma_start(wraw[:, 0, :], weights[SLOTS - 1]).then_inc(raw_loaded[0], 16)
            total = 4 * CHUNKS * (1 + EXPERTS)
            for ch in range(CHUNKS):
                sp.wait_ge(mlp[1]["acc"], total - 4 * (CHUNKS - 1 - ch))
                t = slice(ch * TPC, (ch + 1) * TPC)
                sp.dma_start(out_v[:, t, :], acc[:, t, :]).then_inc(stored, 16)
            sp.wait_ge(stored, 16 * CHUNKS)

        @block.gpsimd
        def _(pool):
            nc.gpsimd.memset(half_neg[:, :], -0.5).then_inc(consts, 1)
            nc.gpsimd.memset(tri_f[:, :], 1.0).then_inc(pool_self, 1)
            nc.gpsimd.memset(ident[:, :], 0.0).then_inc(pool_self, 1)
            nc.gpsimd.memset(causal[:, :], 0.0).then_inc(pool_self, 1)
            pool.wait_ge(pool_self, 3)
            nc.gpsimd.affine_select(out=ident[:, :], in_=ident[:, :], compare_op=ALU.not_equal, fill=1.0,
                                    base=0, pattern=[[-1, P]], channel_multiplier=1).then_inc(consts, 1)
            nc.gpsimd.affine_select(out=tri_f[:, 0:P], in_=tri_f[:, 0:P], compare_op=ALU.is_ge, fill=0.0,
                                    base=0, pattern=[[1, P]], channel_multiplier=-1).then_inc(pool_self, 1)
            nc.gpsimd.affine_select(out=causal[:, P:SEQ], in_=causal[:, P:SEQ], compare_op=ALU.is_ge, fill=MASKED,
                                    base=0, pattern=[[-1, P]], channel_multiplier=1).then_inc(consts, 1)
            nc.gpsimd.iota(iota8[:, :], pattern=[[1, EXPERTS]], base=0, channel_multiplier=0,
                           allow_small_or_imprecise_dtypes=True).then_inc(d["iota"], 1)
            pool.wait_ge(pool_self, 4)
            nc.gpsimd.tensor_copy(tri[:, :], tri_f[:, :]).then_inc(consts, 1)
            nc.gpsimd.tensor_copy(ones_row[:, :], tri_f[0:1, P:2 * P]).then_inc(consts, 1)

            split_count = [0]
            split_self = sem("split_self")

            def split(p, n, base):
                hold(pool, raw_loaded[p], 16 * n + 16, pool_held)
                if not isinstance(n, int) or n >= 1:
                    hold(pool, w_free[p], n, pool_held)
                nc.gpsimd.tensor_copy(wsplit[:, p, 0, :], wraw[:, p, :]).then_inc(split_self, 1)
                hold(pool, split_self, base + 1, pool_held)
                nc.gpsimd.tensor_tensor(out=wsplit[:, p, 1, :], in0=wraw[:, p, :], in1=wsplit[:, p, 0, :],
                                        op=ALU.subtract).then_inc(w_ready[p], 1)

            split(1, 0, 0)

            PER_A = 2 * 11

            def rstd_a(b, ch):
                hold(pool, a["stats"], b + 1, pool_held)
                for t in range(TPB):
                    m, v = mv[:, t, 0:1], mv[:, t, 1:2]
                    L = [ln[:, t, i:i + 1] for i in range(8)]
                    ch.link(nc.gpsimd.tensor_scalar(L[4], v, 1.0, LN_EPS, ALU.mult, ALU.add))
                    ch.link(nc.gpsimd.tensor_tensor(out=L[0], in0=L[4], in1=half_neg[:, 0:1], op=ALU.pow))
                    ch.link(nc.gpsimd.tensor_tensor(out=L[5], in0=v, in1=L[0], op=ALU.mult))
                    ch.link(nc.gpsimd.tensor_tensor(out=L[5], in0=L[5], in1=L[0], op=ALU.mult))
                    ch.link(nc.gpsimd.tensor_scalar(L[5], L[5], 1.0, RMS_EPS, ALU.mult, ALU.add))
                    ch.link(nc.gpsimd.tensor_tensor(out=L[6], in0=L[5], in1=half_neg[:, 0:1], op=ALU.pow))
                    ch.link(nc.gpsimd.tensor_tensor(out=L[1], in0=L[6], in1=L[0], op=ALU.mult))
                    ch.link(nc.gpsimd.tensor_scalar(L[2], L[0], 1.0, 1.0, ALU.mult, ALU.add))
                    ch.link(nc.gpsimd.tensor_tensor(out=L[7], in0=m, in1=L[0], op=ALU.mult))
                    ch.link(nc.gpsimd.tensor_scalar(L[3], L[7], -1.0, 0.0, ALU.mult, ALU.add))
                    ins = nc.gpsimd.tensor_scalar(L[4], L[3], 1.0, 0.0, ALU.mult, ALU.add)
                    ch.mark(ins)
                ch.wait(ch.n)
                pool.sem_inc(a["rstd"], 1)

            PER_T = 14

            def rms_and_split(b, tt, ch):
                t = 2 * b + tt
                for i in range(2):
                    hold(pool, a["ssq"], 2 * t + i + 1, pool_held)
                    ch.link(nc.gpsimd.tensor_scalar(rq[:, 2 + i:3 + i], sums[:, i:i + 1], 1.0 / D, RMS_EPS, ALU.mult, ALU.add))
                    ch.link(nc.gpsimd.tensor_tensor(out=rq[:, 4 + i:5 + i], in0=rq[:, 2 + i:3 + i], in1=half_neg[:, 0:1], op=ALU.pow))
                    ch.link(nc.gpsimd.tensor_scalar(rq[:, i:i + 1], rq[:, 4 + i:5 + i], [-1.0, 1.0][i], 0.0, ALU.mult, ALU.add))
                    pool.sem_inc(a["rms"], 1)
                if not isinstance(b, int) or b >= 1:
                    hold(pool, a["scan"], 2 * b, pool_held)
                hold(pool, a["w"], t + 1, pool_held)
                ch.link(nc.gpsimd.tensor_copy(wv_s[:, tt, 0, 0, :], w_k[:, :]))
                ch.link(nc.gpsimd.tensor_tensor(out=wv_s[:, tt, 0, 1, :], in0=w_k[:, :], in1=wv_s[:, tt, 0, 0, :], op=ALU.subtract))
                hold(pool, a["wv"], t + 1, pool_held)
                ch.link(nc.gpsimd.tensor_copy(wv_s[:, tt, 1, 0, :], wv_f[:, :]))
                ch.link(nc.gpsimd.tensor_tensor(out=wv_s[:, tt, 1, 1, :], in0=wv_f[:, :], in1=wv_s[:, tt, 1, 0, :], op=ALU.subtract))
                pool.sem_inc(a["split"], 1)

            def batch_a(b, last):
                per = PER_A + 2 * 10
                ch = Chain(pool, a["pool"], b * per + PER_A, None, pool_held)
                for tt in range(TPB):
                    rms_and_split(b, tt, ch)
                if not last:
                    rstd_a(b + 1, ch)
                    assert ch.n == per, ch.n

            rstd_a(0, Chain(pool, a["pool"], 0))
            with pool.Fori(0, BATCH - 1) as b:
                batch_a(b, False)
            batch_a(BATCH - 1, True)

            with pool.Fori(0, SLOT_X // 2 - 1) as n:
                split(0, n + 1, 2 * n + 1)
                split(1, n + 1, 2 * n + 2)
            base = 1 + 2 * (SLOT_X // 2 - 1)
            split(0, SLOT_X // 2, base)
            split(1, SLOT_X // 2, base + 1)
            base += 2

            PER_C = 2 * 3 + 2

            def batch_c(b):
                ch = Chain(pool, c["pool"], b * PER_C, PER_C, pool_held)
                hold(pool, c["ctx"], 16 * b + 16, pool_held)
                if not isinstance(b, int) or b >= 1:
                    hold(pool, c["kv"], b, pool_held)
                ch.link(nc.gpsimd.tensor_copy(ctx_s[:, 0, :, :], ctx_raw[:, :, :]))
                ch.link(nc.gpsimd.tensor_tensor(out=ctx_s[:, 1, :, :], in0=ctx_raw[:, :, :], in1=ctx_s[:, 0, :, :], op=ALU.subtract))
                pool.sem_inc(c["ctx_s"], 1)
                hold(pool, c["stats"], b + 1, pool_held)
                for t in range(TPB):
                    L = [ln[:, t, i:i + 1] for i in range(8)]
                    ch.link(nc.gpsimd.tensor_scalar(L[4], mv[:, t, 1:2], 1.0, LN_EPS, ALU.mult, ALU.add))
                    ch.link(nc.gpsimd.tensor_tensor(out=L[0], in0=L[4], in1=half_neg[:, 0:1], op=ALU.pow))
                    ch.link(nc.gpsimd.tensor_scalar(L[1], L[0], 1.0, 0.0, ALU.mult, ALU.add))
                pool.sem_inc(c["rstd"], 1)
                ch.done()

            pool.wait_ge(c["bo"], 16)
            nc.gpsimd.tensor_copy(bo[:, 0, :], bo_raw[:, :]).then_inc(c["bo_s"], 1)
            hold(pool, c["bo_s"], 1, pool_held)
            nc.gpsimd.tensor_tensor(out=bo[:, 1, :], in0=bo_raw[:, :], in1=bo[:, 0, :], op=ALU.subtract).then_inc(c["bo_s"], 1)
            batch_c(0)
            with pool.Fori(1, BATCH) as b:
                batch_c(b)

            def batch_d(b):
                ch = Chain(pool, d["pool"], b * 4, 4, pool_held)
                hold(pool, d["stats"], b + 1, pool_held)
                for t in range(TPB):
                    L = [ln[:, t, i:i + 1] for i in range(8)]
                    ch.link(nc.gpsimd.tensor_scalar(L[4], mv[:, t, 1:2], 1.0, LN_EPS, ALU.mult, ALU.add))
                    ch.link(nc.gpsimd.tensor_tensor(out=L[0], in0=L[4], in1=half_neg[:, 0:1], op=ALU.pow))
                pool.sem_inc(d["rstd"], 1)
                ch.done()

            split(0, SLOT_MOE // 2, base)
            with pool.Fori(0, BATCH) as b:
                batch_d(b)
            split(1, SLOT_MOE // 2, base + 1)
            with pool.Fori(0, SLOTS // 2 - SLOT_MOE // 2 - 1) as n:
                split(0, n + (SLOT_MOE // 2 + 1), 2 * n + base + 2)
                split(1, n + (SLOT_MOE // 2 + 1), 2 * n + base + 3)
            split(0, SLOTS // 2, base + 2 + 2 * (SLOTS // 2 - SLOT_MOE // 2 - 1))

        def three(pe, out_, w_hi, w_lo, m_hi, m_lo, first, last):
            nc.tensor.matmul(out_, w_hi, m_hi, start=first, stop=False)
            nc.tensor.matmul(out_, w_lo, m_hi, start=False, stop=False)
            return nc.tensor.matmul(out_, w_hi, m_lo, start=False, stop=last)

        def mlp_pe(pe, s_, groups, slot0, input_ready):
            first_parity = slot0 % 2

            def weights_of(g_par, part):
                return lambda at_, n: slot_block(g_par, part, at_, n)

            def up(s, par, ch, first_of_group, wait_n, static0):
                if first_of_group:
                    pe.wait_ge(w_ready[par], wait_n)
                for j in range(JB):
                    if not static0:
                        pe.wait_ge(s_["m"], JB * s + j - 1)
                    if input_ready is not None and isinstance(s, int) and s < CHUNKS:
                        pe.wait_ge(*input_ready(s))
                    for kind in range(2):
                        for k in range(KB):
                            o = ((kind * JB + j) * KB + k) * P
                            mm = three(pe, ps[:, 2 * j + kind, :], slot_block(par, 0, o, P), slot_block(par, 1, o, P),
                                       feat[:, 0, k, ch * CHUNK:(ch + 1) * CHUNK], feat[:, 1, k, ch * CHUNK:(ch + 1) * CHUNK],
                                       k == 0, k == KB - 1)
                    mm.then_inc(s_["up"], 1)

            def down(s, par, ch, static0):
                sp_ = ch % 2
                pe.wait_ge(s_["lo"], JB * s + JB)
                for t in range(TPC):
                    if not static0:
                        pe.wait_ge(s_["acc"], TPC * s + t - 3)
                    for j in range(JB):
                        o = 2 * JB * KB * P + j * D
                        mm = three(pe, ps[:, 4 + t, :], m_s[:, sp_, 0, j, t * P:(t + 1) * P], m_s[:, sp_, 1, j, t * P:(t + 1) * P],
                                   slot_block(par, 0, o, D), slot_block(par, 1, o, D), j == 0, j == JB - 1)
                    mm.then_inc(s_["down"], 1)
                if ch == CHUNKS - 1:
                    pe.sem_inc(w_free[par], 1) if False else None

            return up, down

        @block.tensor
        def _(pe):
            pe.wait_ge(consts, 5)

            def qkv(b, tt):
                t = 2 * b + tt
                hb = 0 if tt == 0 else 7
                pe.wait_ge(a["h"], t + 1)
                for k in range(KB):
                    tr = nc.tensor.transpose(ps[:, hb, k * P:(k + 1) * P], ha[:, k * P:(k + 1) * P], ident[:, :])
                tr.then_inc(a["hT_ps"], 1)
                pe.wait_ge(a["hT"], t + 1)
                for i, (name, freed) in enumerate((("q", "e"), ("k", "w"), ("v", "wv"))):
                    if not isinstance(b, int) or b + tt >= 1:
                        pe.wait_ge(a[freed], t)
                    for k in range(KB):
                        col = (i * KB + k) * D
                        p, o = col // SLOT, col % SLOT
                        mm = three(pe, ps[:, 1 + i, :], hTa[:, 0, k, :], hTa[:, 1, k, :],
                                   slot_block(p, 0, o, D), slot_block(p, 1, o, D), k == 0, k == KB - 1)
                    mm.then_inc(a[name], 1)

            def scan(b, half):
                s = 2 * b + half
                if half == 0:
                    pe.wait_ge(a["split"], 2 * b + 2)
                if not (isinstance(b, int) and b == 0 and half == 0):
                    pe.wait_ge(a["y"], s)
                for bank, kind in ((4, 1), (5, 0)):
                    for i in range(2):
                        blk = slice((2 * half + i) * P, (2 * half + i + 1) * P)
                        o = ps[:, bank, i * SEQ:(i + 1) * SEQ]
                        nc.tensor.matmul(o, wv_s[:, 0, kind, 0, blk], tri[:, :], start=True, stop=False)
                        nc.tensor.matmul(o, wv_s[:, 0, kind, 1, blk], tri[:, :], start=False, stop=False)
                        o1 = ps[:, bank, i * SEQ + P:(i + 1) * SEQ]
                        nc.tensor.matmul(o1, wv_s[:, 1, kind, 0, blk], tri[:, 0:P], start=False, stop=False)
                        nc.tensor.matmul(o1, wv_s[:, 1, kind, 1, blk], tri[:, 0:P], start=False, stop=True)
                for i in range(2):
                    blk = slice((2 * half + i) * P, (2 * half + i + 1) * P)
                    for tt in range(TPB):
                        tr = nc.tensor.transpose(ps[:, 6, i * SEQ + tt * P:i * SEQ + (tt + 1) * P], e_q[:, tt, blk], ident[:, :])
                tr.then_inc(a["scan"], 1)

            pe.wait_ge(w_ready[0], 1)
            pe.wait_ge(w_ready[1], 1)
            qkv(0, 0)
            qkv(0, 1)
            with pe.Fori(0, BATCH - 1) as b:
                scan(b, 0)
                scan(b, 1)
                qkv(b + 1, 0)
                qkv(b + 1, 1)
            pe.sem_inc(w_free[0], 1)
            pe.sem_inc(w_free[1], 1)
            scan(BATCH - 1, 0)
            scan(BATCH - 1, 1)

            def run_mlp(s_, groups, slot0, before_up):
                up, down = mlp_pe(pe, s_, groups, slot0, None)
                last_group = groups - 1

                def pair(s, r, g_static, n_expr, parity, last):
                    pass

                par0 = slot0 % 2
                n0 = slot0 // 2

                def steps(s0, count, slot_half, par_first, last):
                    for g in range(count):
                        par = (par_first + g) % 2
                        for ch in range(CHUNKS):
                            s = s0 + (g * CHUNKS + ch)
                            final = last and g == count - 1 and ch == CHUNKS - 1
                            if not final:
                                nch = (ch + 1) % CHUNKS
                                npar = par if nch else 1 - par
                                turn = slot_half + ((par_first + g) // 2 if nch else (par_first + g + 1) // 2)
                                before_up(s, nch)
                                up(s + 1, npar, nch, nch == 0, turn + 1, False)
                            down(s, par, ch, isinstance(s, int) and s == 0)
                            if ch == CHUNKS - 1:
                                pe.wait_ge(s_["down"], TPC * s + TPC)
                                pe.sem_inc(w_free[par], 1)

                return up, down, steps

            def run_b():
                pe.wait_ge(a["yT"], 2 * BATCH)
                up, down, steps = run_mlp(mlp[0], MLP_GROUPS, SLOT_MLP, lambda s, ch: None)
                up(0, 0, 0, True, SLOT_MLP // 2 + 1, True)
                steps(0, 2, SLOT_MLP // 2, 0, False)
                with pe.Fori(1, MLP_GROUPS // 2 - 1) as i:
                    steps(i * (2 * CHUNKS), 2, i + SLOT_MLP // 2, 0, False)
                i = MLP_GROUPS // 2 - 1
                steps(i * 2 * CHUNKS, 2, i + SLOT_MLP // 2, 0, True)

            run_b()

            def batch_c(b):
                later = not isinstance(b, int) or b >= 1
                if later:
                    pe.wait_ge(c["acc"], 2 * b)
                for tt in range(TPB):
                    pe.wait_ge(c["h"], 2 * b + tt + 1)
                    for k in range(KB):
                        tr = nc.tensor.transpose(ps[:, tt, k * P:(k + 1) * P], hc[:, k * P:(k + 1) * P], ident[:, :])
                    tr.then_inc(c["hT_ps"], 1)
                pe.wait_ge(c["ctx_s"], b + 1)
                for tt in range(TPB):
                    for k in range(KB):
                        o = KB * D + k * 2 * P
                        mm = three(pe, ps[:, 2, tt * SEQ:tt * SEQ + 2 * P], ctx_s[:, 0, k, tt * P:(tt + 1) * P],
                                   ctx_s[:, 1, k, tt * P:(tt + 1) * P], slot_block(0, 0, o, 2 * P), slot_block(0, 1, o, 2 * P),
                                   k == 0, k == KB - 1)
                mm.then_inc(c["kv"], 1)
                for tt in range(TPB):
                    pe.wait_ge(c["hT"], 2 * b + tt + 1)
                    for k in range(KB):
                        mm = three(pe, ps[:, 4 + tt, :], hTc[:, tt, 0, k, :], hTc[:, tt, 1, k, :],
                                   slot_block(0, 0, k * D, D), slot_block(0, 1, k * D, D), k == 0, k == KB - 1)
                    mm.then_inc(c["q"], 1)
                pe.wait_ge(c["k4"], 2 * b + 2)
                for tt in range(TPB):
                    for p in range(PAIRS):
                        tr = nc.tensor.transpose(ps[:, 3, p * P:(p + 1) * P] if tt == 0 else ps[:, 6, p * P:(p + 1) * P],
                                                 k4[:, tt, 2 * p:2 * p + 2, :, :].rearrange("t g r d -> t (g r d)"), ident[:, :])
                    tr.then_inc(c["k4T_ps"], 1)
                for tt in range(TPB):
                    pe.wait_ge(c["q4"], 2 * b + tt + 1)
                    for r in range(4):
                        bank = (0, 1, 2, 7)[r]
                        if r < 2 and tt == 0:
                            pass
                        if tt == 1:
                            pe.wait_ge(c["q4T_e"], 8 * b + r + 1)
                        for i in range(4):
                            n = 4 * r + i
                            tr = nc.tensor.transpose(ps[:, bank, i * P:(i + 1) * P],
                                                     q4[:, 2 * n:2 * n + 2, :, :].rearrange("t h r d -> t (h r d)"), ident[:, :])
                        tr.then_inc(c["q4T_ps"], 1)
                pe.wait_ge(c["q4T_e"], 8 * b + 8)
                pe.wait_ge(c["k4T"], 2 * b + 2)
                pe.wait_ge(c["v17"], 2 * b + 2)

                def scores(u):
                    p, kind = divmod(u, 3)
                    if u >= 2:
                        pe.wait_ge(c["mx"], UNITS * b + u - 1)
                    for half in range(2):
                        rows = slice(64 * half, 64 * half + 64)
                        bank = 2 * (u % 2) + half
                        if kind == 0:
                            for i in range(4):
                                mm = nc.tensor.matmul(ps[:, bank, i * P:(i + 1) * P], q4T[rows, 4 * p + i, 0:P],
                                                      k4T[rows, p, 0:P], start=True, stop=True)
                        else:
                            for i2 in range(2):
                                i = 2 * (kind - 1) + i2
                                mm = nc.tensor.matmul(ps[:, bank, i2 * SEQ:(i2 + 1) * SEQ], q4T[rows, 4 * p + i, P:SEQ],
                                                      k4T[rows, p, :], start=True, stop=True)
                    mm.then_inc(c["S"], 1)

                def probs_t(u):
                    g = UNITS * b + u
                    pe.wait_ge(c["P"], g + 1)
                    for half in range(2):
                        if u >= 1:
                            pe.wait_ge(c[("PT_act", "PT_dve")[half]], g)
                        for i in range(4):
                            tr = nc.tensor.transpose(ps[:, 4 + half, i * P:(i + 1) * P], sc[:, u % 2, 4 * half + i, :], ident[:, :])
                        tr.then_inc(c["PT_ps"], 1)

                def attend(u):
                    p, kind = divmod(u, 3)
                    g = UNITS * b + u
                    pe.wait_ge(c["PT_act"], g + 1)
                    pe.wait_ge(c["PT_dve"], g + 1)
                    if u >= 2:
                        pe.wait_ge(c["o"], g - 1)
                    for half in range(2):
                        v = 2 * p + half
                        if kind == 0:
                            for i in range(4):
                                n = 2 * i + half
                                mm = nc.tensor.matmul(ps[:, 6 + u % 2, n * 17:n * 17 + 17], pt[:, u % 2, 4 * half + i, :],
                                                      v17[:, 0, v, :], start=True, stop=True)
                        else:
                            for i2 in range(2):
                                n = 2 * i2 + half
                                for m in range(2):
                                    mm = nc.tensor.matmul(ps[:, 6 + u % 2, n * 17:n * 17 + 17],
                                                          pt[:, u % 2, 4 * half + 2 * i2 + m, :],
                                                          v17[:, m, v, :], start=(m == 0), stop=(m == 1))
                    mm.then_inc(c["O"], 1)

                for u in range(UNITS + 2):
                    if u < UNITS:
                        scores(u)
                    if 1 <= u <= UNITS:
                        probs_t(u - 1)
                    if u >= 2:
                        attend(u - 2)
                for tt in range(TPB):
                    pe.wait_ge(c["o"], UNITS * b + UNITS)
                    for k in range(KB):
                        tr = nc.tensor.transpose(ps[:, tt, k * P:(k + 1) * P], o_tok[:, tt, k * P:(k + 1) * P], ident[:, :])
                    tr.then_inc(c["oT_ps"], 1)
                for tt in range(TPB):
                    pe.wait_ge(c["oT"], 2 * b + tt + 1)
                    o = ps[:, 2 + tt, :]
                    nc.tensor.matmul(o, ones_row[:, :], bo[:, 0, :], start=True, stop=False)
                    nc.tensor.matmul(o, ones_row[:, :], bo[:, 1, :], start=False, stop=False)
                    for k in range(KB):
                        mm = three(pe, o, oT[:, tt, 0, k, :], oT[:, tt, 1, k, :],
                                   slot_block(1, 0, k * D, D), slot_block(1, 1, k * D, D), False, k == KB - 1)
                    mm.then_inc(c["wo"], 1)

            pe.wait_ge(w_ready[0], SLOT_X // 2 + 1)
            pe.wait_ge(w_ready[1], SLOT_X // 2 + 1)
            pe.wait_ge(c["bo_s"], 2)
            pe.wait_ge(mlp[0]["acc"], TPC * CHUNKS * MLP_GROUPS)
            batch_c(0)
            with pe.Fori(1, BATCH) as b:
                batch_c(b)
            pe.sem_inc(w_free[0], 1)
            pe.wait_ge(c["acc"], TILES)

            def norm_d(t, par_bank):
                pe.wait_ge(d["h"], t + 1)
                if not isinstance(t, int) or t >= 2:
                    pe.wait_ge(d["comb"], t - 1)
                for k in range(KB):
                    tr = nc.tensor.transpose(ps[:, 4 + par_bank, k * P:(k + 1) * P], hd[:, par_bank, k * P:(k + 1) * P], ident[:, :])
                tr.then_inc(d["hT_ps"], 1)

            def logits(t, par_bank):
                pe.wait_ge(d["hT"], t + 1)
                n = 0
                for k in range(KB):
                    for hp in range(2):
                        for wp in range(2):
                            mm = nc.tensor.matmul(ps[:, 6 + par_bank, 0:EXPERTS], feat[:, hp, k, bass.ts(t, P)] if isinstance(t, int) else feat[:, hp, k, bass.ds(t * P, P)],
                                                  slot_block(1, wp, KB * D + k * EXPERTS, EXPERTS), start=(n == 0), stop=(n == 15))
                            n += 1
                mm.then_inc(d["logit"], 1)

            for t in range(TILES):
                norm_d(t, t % 2)
                logits(t, t % 2)
            pe.wait_ge(d["logit"], TILES)
            pe.sem_inc(w_free[1], 1)
            pe.wait_ge(d["comb"], TILES)
            s_ = mlp[1]
            up, down, steps = run_mlp(s_, 1 + EXPERTS, SLOT_MOE, lambda s, ch: None)
            up(0, 0, 0, True, SLOT_MOE // 2 + 1, True)
            steps(0, 1, SLOT_MOE // 2, 0, False)
            with pe.Fori(0, EXPERTS // 2 - 1) as i:
                steps(i * (2 * CHUNKS) + CHUNKS, 2, i + SLOT_MOE // 2, 1, False)
            i = EXPERTS // 2 - 1
            steps(i * 2 * CHUNKS + CHUNKS, 2, i + SLOT_MOE // 2, 1, True)

        def mlp_act(act, s_):
            def act_step(s, ch, static0):
                for j in range(JB):
                    act.wait_ge(s_["up"], JB * s + j + 1)
                    nc.scalar.activation(sg[:, j, :], ps[:, 2 * j + 1, :], ACT.Silu).then_inc(s_["silu"], 1)
                    act.wait_ge(s_["m"], JB * s + j + 1)
                    if not (isinstance(s, int) and s < 2):
                        act.wait_ge(s_["down"], TPC * s - TPC)
                    nc.scalar.copy(m_s[:, ch % 2, 0, j, :], m_f[:, j, :]).then_inc(s_["hi"], 1)
            return act_step

        @block.scalar
        def _(act):
            def tile_a(b, tt):
                t = 2 * b + tt
                hb = 0 if tt == 0 else 7
                act.wait_ge(a["hT_ps"], t + 1)
                if not isinstance(b, int) or b + tt >= 1:
                    act.wait_ge(a["v"], t)
                nc.scalar.copy(hTa[:, 0, :, :], ps[:, hb, :]).then_inc(a["hT_hi"], 1)
                act.wait_ge(a["q"], t + 1)
                if (not isinstance(b, int)) or b >= 1:
                    act.wait_ge(a["scan"], 2 * b)
                nc.scalar.activation(e_q[:, tt, :], ps[:, 1, :], ACT.Square, accum_out=sums[:, 0:1]).then_inc(a["ssq"], 1)
                act.wait_ge(a["rms"], 2 * t + 1)
                nc.scalar.activation(e_q[:, tt, :], ps[:, 1, :], ACT.Exp, scale=rq[:, 0:1]).then_inc(a["e"], 1)
                act.wait_ge(a["k"], t + 1)
                if not isinstance(b, int) or b + tt >= 1:
                    act.wait_ge(a["split"], t)
                nc.scalar.activation(w_k[:, :], ps[:, 2, :], ACT.Square, accum_out=sums[:, 1:2]).then_inc(a["ssq"], 1)
                act.wait_ge(a["rms"], 2 * t + 2)
                nc.scalar.activation(w_k[:, :], ps[:, 2, :], ACT.Exp, scale=rq[:, 1:2]).then_inc(a["w"], 1)

            def scan_a(b, half):
                s = 2 * b + half
                act.wait_ge(a["scan"], s + 1)
                if not (isinstance(b, int) and b == 0 and half == 0):
                    act.wait_ge(a["den"], s)
                nc.scalar.activation(wce[:, :], ps[:, 5, :], ACT.Copy, bias=1e-6).then_inc(a["wce"], 1)
                act.wait_ge(a["y"], s + 1)
                dst = feat[:, 0, 2 * half:2 * half + 2, bass.ds(b * SEQ, SEQ)] if not isinstance(b, int) else \
                    feat[:, 0, 2 * half:2 * half + 2, b * SEQ:(b + 1) * SEQ]
                nc.scalar.copy(dst, den[:, :].rearrange("p (k n) -> p k n", k=2)).then_inc(a["yhi"], 1)

            tile_a(0, 0)
            tile_a(0, 1)
            with act.Fori(0, BATCH - 1) as b:
                scan_a(b, 0)
                scan_a(b, 1)
                tile_a(b + 1, 0)
                tile_a(b + 1, 1)
            scan_a(BATCH - 1, 0)
            scan_a(BATCH - 1, 1)
            act.wait_ge(a["yT"], 2 * BATCH)

            step = mlp_act(act, mlp[0])
            for s in range(2 * CHUNKS):
                step(s, s % CHUNKS, s == 0)
            with act.Fori(1, MLP_GROUPS // 2) as i:
                for r in range(2 * CHUNKS):
                    step(i * (2 * CHUNKS) + r, r % CHUNKS, False)

            def batch_c(b):
                later = not isinstance(b, int) or b >= 1
                for tt in range(TPB):
                    act.wait_ge(c["hT_ps"], 2 * b + tt + 1)
                    nc.scalar.copy(hTc[:, tt, 0, :, :], ps[:, tt, :]).then_inc(c["hT_hi"], 1)
                act.wait_ge(c["kv"], b + 1)
                for tt in range(TPB):
                    kv = ps[:, 2, tt * SEQ:(tt + 1) * SEQ]
                    k_in = kv[:, 0:P].rearrange("p (g o d) -> p g o d", g=KVG, o=1).broadcast_to([P, KVG, 2, HD])
                    nc.scalar.copy(v17[:, tt, :, 0:HD], kv[:, P:2 * P].rearrange("p (g d) -> p g d", g=KVG)).then_inc(c["v17"], 1)
                    nc.scalar.copy(k4[:, tt, :, 0:2, :].bitcast(F32R), k_in).then_inc(c["khi"], 1)
                for tt in range(TPB):
                    act.wait_ge(c["q"], 2 * b + tt + 1)
                    if tt == 1 :
                        act.wait_ge(c["q4T_ps"], 8 * b + 4)
                    q_in = ps[:, 4 + tt, :].rearrange("p (h o d) -> p h o d", h=HEADS, o=1).broadcast_to([P, HEADS, 2, HD])
                    nc.scalar.copy(q4[:, :, 0:3:2, :].bitcast(F32R), q_in).then_inc(c["qhi"], 1)
                    if tt == 0:
                        for k2 in range(TPB):
                            act.wait_ge(c["k4T_ps"], 2 * b + k2 + 1)
                            nc.scalar.copy(k4T[:, :, k2 * P:(k2 + 1) * P],
                                           ps[:, (3, 6)[k2], :].rearrange("p (k n) -> p k n", k=PAIRS)).then_inc(c["k4T"], 1)
                    for r in range(4):
                        act.wait_ge(c["q4T_ps"], 8 * b + 4 * tt + r + 1)
                        nc.scalar.copy(q4T[:, 4 * r:4 * r + 4, tt * P:(tt + 1) * P],
                                       ps[:, (0, 1, 2, 7)[r], :].rearrange("p (k n) -> p k n", k=4)).then_inc(c["q4T_e"], 1)

                def exps(u):
                    g = UNITS * b + u
                    kind = u % 3
                    act.wait_ge(c["nmx"], g + 1)
                    n, w = (8, P) if kind == 0 else (4, SEQ)
                    flat = sc[:, u % 2, :, :].rearrange("p a n -> p (a n)")
                    for i in range(n):
                        ins = nc.scalar.activation(flat[:, i * w:(i + 1) * w], flat[:, i * w:(i + 1) * w], ACT.Exp,
                                                   bias=nmx[:, u % 2, i:i + 1], scale=0.25)
                    ins.then_inc(c["P"], 1)

                def pt_evac(u):
                    g = UNITS * b + u
                    act.wait_ge(c["PT_ps"], 2 * g + 1)
                    if u >= 2:
                        act.wait_ge(c["O"], g - 1)
                    nc.scalar.copy(pt[:, u % 2, 0:4, :], ps[:, 4, :].rearrange("p (k n) -> p k n", k=4)).then_inc(c["PT_act"], 1)

                for u in range(UNITS + 1):
                    if u < UNITS:
                        exps(u)
                    if u >= 1:
                        pt_evac(u - 1)
                for tt in range(TPB):
                    act.wait_ge(c["oT_ps"], 2 * b + tt + 1)
                    nc.scalar.copy(oT[:, tt, 0, :, :], ps[:, tt, :].rearrange("p (k n) -> p k n", k=KB)).then_inc(c["oT_hi"], 1)

            act.wait_ge(mlp[0]["acc"], TPC * CHUNKS * MLP_GROUPS)
            batch_c(0)
            with act.Fori(1, BATCH) as b:
                batch_c(b)

            act.wait_ge(c["acc"], TILES)
            for t in range(TILES):
                act.wait_ge(d["hT_ps"], t + 1)
                nc.scalar.copy(feat[:, 0, :, t * P:(t + 1) * P], ps[:, 4 + t % 2, :].rearrange("p (k n) -> p k n", k=KB)).then_inc(d["hT_hi"], 1)
                act.wait_ge(d["nmx"], t + 1)
                nc.scalar.activation(gl[:, 2, :], gl[:, 0, :], ACT.Exp, bias=gl[:, 1, 0:1], accum_out=gl[:, 1, 1:2]).then_inc(d["ex"], 1)
            step = mlp_act(act, mlp[1])
            for s in range(CHUNKS):
                step(s, s % CHUNKS, s == 0)
            with act.Fori(0, EXPERTS // 2) as i:
                for r in range(2 * CHUNKS):
                    step(i * (2 * CHUNKS) + (CHUNKS + r), r % CHUNKS, False)

        def mlp_dve(dve, s_, scale_of):
            def hidden(s, j, ch):
                dve.wait_ge(s_["silu"], JB * s + j + 1)
                nc.vector.tensor_tensor(m_f[:, j, :], ps[:, 2 * j, :], sg[:, j, :], ALU.mult).then_inc(s_["m"], 1)

            def low(s, j, ch):
                dve.wait_ge(s_["hi"], JB * s + j + 1)
                nc.vector.tensor_tensor(m_s[:, ch % 2, 1, j, :], m_f[:, j, :], m_s[:, ch % 2, 0, j, :], ALU.subtract).then_inc(s_["lo"], 1)

            def sums_(s, t, tile, scale):
                dve.wait_ge(s_["down"], TPC * s + t + 1)
                if scale is None:
                    nc.vector.tensor_tensor(acc[:, tile, :], ps[:, 4 + t, :], acc[:, tile, :], ALU.add).then_inc(s_["acc"], 1)
                else:
                    nc.vector.scalar_tensor_tensor(out=acc[:, tile, :], in0=ps[:, 4 + t, :], scalar=scale, in1=acc[:, tile, :],
                                                   op0=ALU.mult, op1=ALU.add).then_inc(s_["acc"], 1)

            def head(s, ch):
                for j in range(JB):
                    hidden(s, j, ch)
                    low(s, j, ch)

            def steps(s0, groups, last, expert):
                for g in range(groups):
                    for ch in range(CHUNKS):
                        s = s0 + (g * CHUNKS + ch)
                        if not (last and g == groups - 1 and ch == CHUNKS - 1):
                            head(s + 1, (ch + 1) % CHUNKS)
                        if not (isinstance(s, int) and s < CHUNKS):
                            dve.wait_ge(s_["acc"], TPC * s + TPC - TPC * CHUNKS)
                        for t in range(TPC):
                            tile = ch * TPC + t
                            scale = None
                            if expert is not None:
                                e = expert + g
                                scale = comb[:, tile, e:e + 1] if isinstance(e, int) else comb[:, tile, bass.ds(e, 1)]
                            sums_(s, t, tile, scale)
            return head, steps

        @block.vector
        def _(dve):
            dve.wait_ge(raw_loaded[0], 16)
            ch0 = Chain(dve, a["dve"], 0)
            ch0.link(nc.vector.tensor_copy(wsplit[:, 0, 0, :], wraw[:, 0, :]))
            nc.vector.tensor_tensor(wsplit[:, 0, 1, :], wraw[:, 0, :], wsplit[:, 0, 0, :], ALU.subtract).then_inc(w_ready[0], 1)
            DVE0 = 1

            def accs(b, tt):
                return acc[:, 2 * b + tt, :] if isinstance(b, int) else acc[:, bass.ds(2 * b + tt, 1), :].rearrange("p o d -> p (o d)")

            def norm_stats(b, s_, ch):
                for t in range(TPB):
                    ch.mark(nc.vector.bn_stats(stats[:, t, :], accs(b, t)))
                hold(dve, ch.sem, ch.base + ch.n, dve_held)
                for t in range(TPB):
                    ins = nc.vector.bn_aggr(mv[:, t, :], stats[:, t, :])
                    ch.mark(ins)
                ch.wait(ch.n)
                dve.sem_inc(s_, 1)

            def norm_a(b, ch):
                norm_stats(b, a["stats"], ch)
                dve.wait_ge(a["rstd"], b + 1)

            def tile_a(b, tt, ch):
                t = 2 * b + tt
                first = isinstance(b, int) and b + tt == 0
                if not first:
                    dve.wait_ge(a["hT_ps"], t)
                nc.vector.tensor_scalar(ha[:, :], accs(b, tt), mv[:, tt, 0:1], ln[:, tt, 1:2], ALU.subtract, ALU.mult).then_inc(a["h"], 1)
                dve.wait_ge(a["h"], t + 1)
                nc.vector.tensor_scalar(accs(b, tt), accs(b, tt), ln[:, tt, 2:3], ln[:, tt, 3:4], ALU.mult, ALU.add).then_inc(a["acc"], 1)
                hb = 0 if tt == 0 else 7
                dve.wait_ge(a["hT_hi"], t + 1)
                nc.vector.tensor_tensor(hTa[:, 1, :, :].rearrange("p k n -> p (k n)"), ps[:, hb, :],
                                        hTa[:, 0, :, :].rearrange("p k n -> p (k n)"), ALU.subtract).then_inc(a["hT"], 1)
                dve.wait_ge(a["v"], t + 1)
                dve.wait_ge(a["w"], t + 1)
                if not first:
                    dve.wait_ge(a["split"], t)
                nc.vector.tensor_tensor(wv_f[:, :], ps[:, 3, :], w_k[:, :], ALU.mult).then_inc(a["wv"], 1)

            def scan_a(b, half):
                s = 2 * b + half
                dve.wait_ge(a["wce"], s + 1)
                if not (isinstance(b, int) and b == 0 and half == 0):
                    dve.wait_ge(a["yT"], s)
                nc.vector.scalar_tensor_tensor(out=den[:, :], in0=ps[:, 6, :], scalar=1.0, in1=wce[:, :], op0=ALU.add,
                                               op1=ALU.mult).then_inc(a["den"], 1)
                dve.wait_ge(a["den"], s + 1)
                nc.vector.reciprocal(den[:, :], den[:, :]).then_inc(rec_done, 1)
                dve.wait_ge(rec_done, s + 1)
                nc.vector.tensor_tensor(den[:, :], ps[:, 4, :], den[:, :], ALU.mult).then_inc(a["y"], 1)
                dve.wait_ge(a["yhi"], s + 1)
                cols = slice(b * SEQ, (b + 1) * SEQ) if isinstance(b, int) else bass.ds(b * SEQ, SEQ)
                nc.vector.tensor_tensor(feat[:, 1, 2 * half:2 * half + 2, cols], den[:, :].rearrange("p (k n) -> p k n", k=2),
                                        feat[:, 0, 2 * half:2 * half + 2, cols], ALU.subtract).then_inc(a["yT"], 1)

            rec_done = sem("a_rec")
            dve.wait_ge(x_first, 16)
            norm_a(0, Chain(dve, a["dve"], DVE0))
            tile_a(0, 0, None)
            tile_a(0, 1, None)
            dve.wait_ge(x_rest, 16)
            with dve.Fori(0, BATCH - 1) as b:
                norm_a(b + 1, Chain(dve, a["dve"], b * 4 + (DVE0 + 4)))
                scan_a(b, 0)
                scan_a(b, 1)
                tile_a(b + 1, 0, None)
                tile_a(b + 1, 1, None)
            scan_a(BATCH - 1, 0)
            scan_a(BATCH - 1, 1)
            dve.wait_ge(a["yT"], 2 * BATCH)
            dve.wait_ge(a["acc"], TILES)

            head, steps = mlp_dve(dve, mlp[0], None)
            head(0, 0)
            steps(0, 2, False, None)
            with dve.Fori(1, MLP_GROUPS // 2 - 1) as i:
                steps(i * (2 * CHUNKS), 2, False, None)
            steps((MLP_GROUPS // 2 - 1) * 2 * CHUNKS, 2, True, None)
            dve.wait_ge(mlp[0]["acc"], TPC * CHUNKS * MLP_GROUPS)

            nc.vector.memset(v17[:, :, :, HD:HD + 1], 1.0).then_inc(c["ones"], 1)
            dve.wait_ge(consts, 5)
            PER_C = 4 + 1 + 12

            def batch_c(b):
                later = not isinstance(b, int) or b >= 1
                ch = Chain(dve, c["dve"], b * PER_C, PER_C)
                dve.wait_ge(c["mask_i"], 16 * b + 16)
                ch.link(nc.vector.tensor_scalar(sc[:, 0, 0:2, :].rearrange("p a n -> p (a n)"), msk_i[:, :], 0.0, MASKED, ALU.is_equal, ALU.mult))
                nc.vector.tensor_tensor(msk[:, 0, :], sc[:, 0, 0, :], causal[:, P:SEQ], ALU.add).then_inc(msk_self, 1)
                nc.vector.tensor_tensor(msk[:, 1:3, :].rearrange("p a n -> p (a n)"), sc[:, 0, 0:2, :].rearrange("p a n -> p (a n)"),
                                        causal[:, :], ALU.add).then_inc(c["mask"], 1)
                norm_stats(b, c["stats"], ch)
                dve.wait_ge(c["rstd"], b + 1)
                for tt in range(TPB):
                    t = 2 * b + tt
                    if later or tt == 1:
                        dve.wait_ge(c["hT_ps"], t)
                    nc.vector.tensor_scalar(hc[:, :], accs(b, tt), mv[:, tt, 0:1], ln[:, tt, 0:1], ALU.subtract, ALU.mult).then_inc(c["h"], 1)
                    dve.wait_ge(c["hT_hi"], t + 1)
                    nc.vector.tensor_tensor(hTc[:, tt, 1, :, :].rearrange("p k n -> p (k n)"), ps[:, tt, :],
                                            hTc[:, tt, 0, :, :].rearrange("p k n -> p (k n)"), ALU.subtract).then_inc(c["hT"], 1)
                for tt in range(TPB):
                    t = 2 * b + tt
                    dve.wait_ge(c["khi"], 2 * b + 2)
                    k_in = ps[:, 2, tt * SEQ:tt * SEQ + P].rearrange("p (g o d) -> p g o d", g=KVG, o=1).broadcast_to([P, KVG, 2, HD])
                    nc.vector.tensor_tensor(k4[:, tt, :, 2:4, :].bitcast(F32R), k_in, k4[:, tt, :, 0:2, :], ALU.subtract).then_inc(c["k4"], 1)
                for tt in range(TPB):
                    dve.wait_ge(c["qhi"], 2 * b + tt + 1)
                    q_in = ps[:, 4 + tt, :].rearrange("p (h o d) -> p h o d", h=HEADS, o=1).broadcast_to([P, HEADS, 2, HD])
                    nc.vector.tensor_tensor(q4[:, :, 1:4:2, :].bitcast(F32R), q_in, q4[:, :, 0:3:2, :], ALU.subtract).then_inc(c["q4"], 1)
                dve.wait_ge(msk_self, b + 1)
                dve.wait_ge(c["mask"], b + 1)

                def maxes(u):
                    kind = u % 3
                    g = UNITS * b + u
                    hold(dve, c["S"], g + 1, dve_held)
                    if u >= 2:
                        hold(dve, c["PT_ps"], 2 * g - 2, dve_held)
                    n, w = (8, P) if kind == 0 else (4, SEQ)
                    flat = sc[:, u % 2, :, :].rearrange("p a n -> p (a n)")
                    m_in = msk[:, 0, :] if kind == 0 else msk[:, 1:3, :].rearrange("p a n -> p (a n)")
                    for i in range(n):
                        src = ps[:, 2 * (u % 2) + i * w // 512, i * w % 512:i * w % 512 + w]
                        ins = nc.vector.tensor_tensor_reduce(flat[:, i * w:(i + 1) * w], src, m_in, 1.0, -3e38, ALU.add, ALU.max,
                                                             mxs[:, u % 2, i:i + 1])
                    ins.then_inc(c["mx"], 1)
                    dve.wait_ge(c["mx"], g + 1)
                    nc.vector.tensor_scalar(nmx[:, u % 2, 0:n], mxs[:, u % 2, 0:n], -0.25, None, ALU.mult).then_inc(c["nmx"], 1)

                def pt_evac(u):
                    g = UNITS * b + u
                    dve.wait_ge(c["PT_ps"], 2 * g + 2)
                    if u >= 2:
                        dve.wait_ge(c["O"], g - 1)
                    nc.vector.tensor_copy(pt[:, u % 2, 4:8, :].rearrange("p k n -> p (k n)"), ps[:, 5, :]).then_inc(c["PT_dve"], 1)

                def normed(u):
                    p, kind = divmod(u, 3)
                    g = UNITS * b + u
                    n, tt, at_ = (8, 0, 8 * p) if kind == 0 else (4, 1, 8 * p + 4 * (kind - 1))
                    dve.wait_ge(c["O"], g + 1)
                    o17 = ps[:, 6 + u % 2, 0:n * 17].rearrange("p (h d) -> p h d", d=17)
                    ch.link(nc.vector.reciprocal(rden[:, u % 2, 0:n].rearrange("p (h o) -> p h o", o=1), o17[:, :, HD:HD + 1]))
                    nc.vector.tensor_tensor(o_tok[:, tt, at_ * HD:(at_ + n) * HD].rearrange("p (h d) -> p h d", d=HD), o17[:, :, 0:HD],
                                            rden[:, u % 2, 0:n].rearrange("p (h o) -> p h o", o=1).broadcast_to([P, n, HD]),
                                            ALU.mult).then_inc(c["o"], 1)

                for u in range(UNITS + 2):
                    if u < UNITS:
                        maxes(u)
                    if 1 <= u <= UNITS:
                        pt_evac(u - 1)
                    if u >= 2:
                        normed(u - 2)
                for tt in range(TPB):
                    dve.wait_ge(c["oT_hi"], 2 * b + tt + 1)
                    nc.vector.tensor_tensor(oT[:, tt, 1, :, :].rearrange("p k n -> p (k n)"), ps[:, tt, :],
                                            oT[:, tt, 0, :, :].rearrange("p k n -> p (k n)"), ALU.subtract).then_inc(c["oT"], 1)
                for tt in range(TPB):
                    dve.wait_ge(c["wo"], 2 * b + tt + 1)
                    nc.vector.tensor_tensor(accs(b, tt), ps[:, 2 + tt, :], accs(b, tt), ALU.add).then_inc(c["acc"], 1)
                ch.done()

            msk_self = sem("c_msk_self")
            batch_c(0)
            with dve.Fori(1, BATCH) as b:
                batch_c(b)
            dve.wait_ge(c["acc"], TILES)

            PER_R = 10
            dve.wait_ge(d["iota"], 1)
            for b in range(BATCH):
                ch = Chain(dve, d["dve"], b * (4 + 2 * PER_R), 4 + 2 * PER_R)
                norm_stats(b, d["stats"], ch)
                dve.wait_ge(d["rstd"], b + 1)
                for tt in range(TPB):
                    t = 2 * b + tt
                    if t >= 2:
                        dve.wait_ge(d["hT_ps"], t - 1)
                    nc.vector.tensor_scalar(hd[:, tt, :], accs(b, tt), mv[:, tt, 0:1], ln[:, tt, 0:1], ALU.subtract, ALU.mult).then_inc(d["h"], 1)
                    dve.wait_ge(d["hT_hi"], t + 1)
                    cols = slice(t * P, (t + 1) * P)
                    nc.vector.tensor_tensor(feat[:, 1, :, cols], ps[:, 4 + tt, :].rearrange("p (k n) -> p k n", k=KB), feat[:, 0, :, cols],
                                            ALU.subtract).then_inc(d["hT"], 1)
                    dve.wait_ge(d["logit"], t + 1)
                    ch.link(nc.vector.tensor_copy(gl[:, 0, :], ps[:, 6 + tt, 0:EXPERTS]))
                    ch.link(nc.vector.tensor_reduce(gl[:, 7, 0:1], gl[:, 0, :], AX.X, ALU.max))
                    nc.vector.tensor_scalar(gl[:, 1, 0:1], gl[:, 7, 0:1], -1.0, None, ALU.mult).then_inc(d["nmx"], 1)
                    dve.wait_ge(d["ex"], t + 1)
                    ch.link(nc.vector.reciprocal(gl[:, 1, 2:3], gl[:, 1, 1:2]))
                    ch.link(nc.vector.tensor_scalar(gl[:, 3, :], gl[:, 2, :], gl[:, 1, 2:3], None, ALU.mult))
                    ch.link(nc.vector.max(gl[:, 4, :], gl[:, 3, :]))
                    ch.link(nc.vector.max_index(gi[:, :], gl[:, 4, :], gl[:, 3, :]))
                    ch.link(nc.vector.tensor_copy(gl[:, 5, :], gi[:, :]))
                    ch.link(nc.vector.tensor_scalar(gl[:, 6, :], iota8[:, :], gl[:, 5, 0:1], gl[:, 4, 0:1], ALU.is_equal, ALU.mult))
                    ch.link(nc.vector.tensor_scalar(gl[:, 7, :], iota8[:, :], gl[:, 5, 1:2], gl[:, 4, 1:2], ALU.is_equal, ALU.mult))
                    ch.link(nc.vector.tensor_tensor(comb[:, t, :], gl[:, 6, :], gl[:, 7, :], ALU.add))
                    dve.sem_inc(d["comb"], 1)
                ch.done()
            head, steps = mlp_dve(dve, mlp[1], comb)
            head(0, 0)
            steps(0, 1, False, None)
            with dve.Fori(0, EXPERTS // 2 - 1) as i:
                steps(i * (2 * CHUNKS) + CHUNKS, 2, False, 2 * i)
            i = EXPERTS // 2 - 1
            steps(i * 2 * CHUNKS + CHUNKS, 2, True, 2 * i)


def blocks(w_t):
    k, n = w_t.shape
    return w_t.reshape(k // P, P, n).transpose(1, 0, 2).reshape(P, k // P * n)


def group_slot(up, gate, down):
    import numpy as np

    cols = []
    for w in (up, gate):
        t = w.T.reshape(KB, P, JB, P)
        cols.append(t.transpose(1, 2, 0, 3).reshape(P, JB * KB * P))
    cols.append(blocks(down.T))
    return np.concatenate(cols, axis=1)


def kernel(**inputs):
    import numpy as np
    import concourse.bacc as bacc
    from concourse.bass_utils import run_bass_kernel_spmd

    f = {k: np.asarray(v) for k, v in inputs.items()}
    qkv = f["L0_attn_w_qkv"]
    a_w = np.concatenate([blocks(qkv[i * D:(i + 1) * D].T) for i in range(3)], axis=1)
    slots = [a_w[:, :SLOT], a_w[:, SLOT:]]
    sw, wo = f["L0_attn_w_swiglu"], f["L0_attn_w_out"]
    for g in range(MLP_GROUPS):
        u = slice(g * GROUP, (g + 1) * GROUP)
        slots.append(group_slot(sw[:DFF][u], sw[DFF:][u], wo[:, u]))
    order = [(2 * p + half) * (HEADS // KVG) + i for p in range(PAIRS) for i in range(HEADS // KVG) for half in range(2)]
    rows = np.concatenate([np.arange(h * HD, (h + 1) * HD) for h in order])
    kv = np.concatenate([f["L0_xattn_w_k"], f["L0_xattn_w_v"]])
    slots.append(np.concatenate([blocks(f["L0_xattn_w_q"][rows].T), blocks(kv.T)], axis=1))
    o_slot = np.zeros((P, SLOT), np.float32)
    o_slot[:, :KB * D] = blocks(f["L0_xattn_w_o"][:, rows].T)
    o_slot[:, KB * D:KB * (D + EXPERTS)] = blocks(f["L0_ffn_gate_w"].T)
    slots.append(o_slot)
    slots.append(group_slot(f["L0_ffn_ws3"], f["L0_ffn_ws1"], f["L0_ffn_ws2"]))
    for e in range(EXPERTS):
        slots.append(group_slot(f["L0_ffn_w3"][e], f["L0_ffn_w1"][e], f["L0_ffn_w2"][e]))
    arrays = {
        "x": np.ascontiguousarray(f["x"].reshape(BATCH * SEQ, D)),
        "weights": np.ascontiguousarray(np.stack(slots)),
        "ctx_t": np.ascontiguousarray(f["ctx_2048"].reshape(BATCH, SEQ, KB, P).transpose(0, 3, 2, 1)),
        "mask": np.ascontiguousarray(f["mask_BxS2_if1"]),
        "b_o": np.ascontiguousarray(f["L0_xattn_b_o"].reshape(1, D)),
    }
    nc = bacc.Bacc("TRN2", target_bir_lowering=False, num_devices=1)
    args = [nc.dram_tensor(n, v.shape, mybir.dt.from_np(v.dtype), kind="ExternalInput").ap() for n, v in arrays.items()]
    out = nc.dram_tensor("out", (BATCH * SEQ, D), F32, kind="ExternalOutput").ap()
    decoder_layer(nc, *args, out)
    r = run_bass_kernel_spmd(nc, [arrays], core_ids=[0])
    return r.results[0]["out"].reshape(BATCH, SEQ, D)
```

```python
from contextlib import ExitStack

import concourse.bass as bass
from concourse import mybir
from concourse.alu_op_type import AluOpType as ALU

ACT = mybir.ActivationFunctionType
AX = mybir.AxisListType
F32 = mybir.dt.float32
F32R = mybir.dt.float32r
U32 = mybir.dt.uint32
I32 = mybir.dt.int32

P = 128
D = 512
KB = D // P
BATCH, SEQ = 8, 256
TPB = SEQ // P
TILES = BATCH * TPB
DFF = 2048
GROUP = 256
JB = GROUP // P
MLP_GROUPS = DFF // GROUP
EXPERTS = 8
CHUNK = 512
CHUNKS = BATCH * SEQ // CHUNK
TPC = CHUNK // P
SLOT = (2 * JB * KB + JB * KB) * P
HEADS, KVG, HD = 32, 8, 16
PAIRS = KVG // 2
UNITS = 3 * KVG
LN_EPS = 1e-5
RMS_EPS = 1.1920929e-07
MASKED = -1e37

SLOT_QKV, SLOT_MLP, SLOT_X = 0, 2, 2 + MLP_GROUPS
SLOT_O = SLOT_X + 1
SLOT_MOE = SLOT_X + 2
SLOTS = SLOT_MOE + 1 + EXPERTS


def after(eng, sem, value):
    if not (isinstance(value, int) and value <= 0):
        eng.wait_ge(sem, value)


PIECES = {1: "n10", 2: "kv", 3: "hT0", 4: "k4T0", 5: "n11", 6: "hT1", 7: "k4T1", 8: "q0", 9: "n00",
          10: "oT0", 11: "oT1", 12: "q4T00", 13: "q4T01", 14: "q4T02", 15: "q4T03", 16: "q1", 17: "wo0",
          18: "n01", 19: "wo1", 20: "q4T10", 21: "q4T11", 22: "q4T12", 23: "q4T13"}


def piece_side(name):
    if name[0] == "n":
        return "own" if name[1] == "0" else "out"
    return "out" if name[:2] in ("oT", "wo") else "in"


ORDER = list(PIECES.values())
PIECE_BANKS = 2
IN_BANK = [len(ORDER[k::PIECE_BANKS]) for k in range(PIECE_BANKS)]


def piece_turn(name, b):
    at = ORDER.index(name)
    return at % PIECE_BANKS, IN_BANK[at % PIECE_BANKS] * (b + 1) + at // PIECE_BANKS


def unit_of(u):
    quad, r = divmod(u, UNITS // 2)
    if r < 4:
        return 4 * quad + r, range(4), 0
    j, part = divmod(r - 4, 2)
    return 4 * quad + j, range(2 * part, 2 * part + 2), 1


QUAD_ENDS = (3, 11, 15, 23)


def hold(eng, sem, value, settled):
    eng.wait_ge(sem, value)
    eng.sem_inc(settled, 1)


class Chain:

    def __init__(self, eng, sem, base=0, per=None, settled=None):
        self.eng, self.sem, self.base, self.n, self.per, self.settled = eng, sem, base, 0, per, settled

    def mark(self, ins):
        self.n += 1
        ins.then_inc(self.sem, 1)
        return self.n

    def wait(self, n):
        self.eng.wait_ge(self.sem, self.base + n)
        if self.settled is not None:
            self.eng.sem_inc(self.settled, 1)

    def link(self, ins):
        self.wait(self.mark(ins))

    def done(self):
        assert self.per is None or self.n == self.per, (self.n, self.per)


def decoder_layer(nc: bass.Bass, x, weights, ctx_t, mask, out):
    with ExitStack() as es:
        start = (nc.sbuf_base + 63) // 64 * 64
        place = [start]

        def at(name, shape, dt, off=None):
            size = 4
            for n in shape[1:]:
                size *= n
            if off is None:
                off = place[0]
                place[0] += (size + 31) // 32 * 32
            assert off + size <= nc.sbuf_usable_end, (name, off + size)
            return nc.alloc_sbuf_tensor_at(name, shape, dt, offset=off)

        acc = at("acc", [P, TILES, D], F32)
        feat_at = place[0]
        feat = at("feat", [P, 2, KB, BATCH * SEQ], F32R)
        wsplit = at("wsplit", [P, 2, 2, SLOT], F32R)
        raw0_at = place[0]
        wraw = at("wraw", [P, 2, SLOT], F32)
        raw1_at = raw0_at + 4 * SLOT
        ident = at("ident", [P, P], F32)
        tri = at("tri", [P, 2 * P], F32R)
        causal = at("causal", [P, SEQ], F32)
        half_neg = at("half_neg", [P, 4], F32)
        ones_row = at("ones_row", [1, P], F32R)
        stats_d = at("stats_d", [P, TPC, 6], F32)
        mv_d = at("mv_d", [P, TPC, 2], F32)
        ln_d = at("ln_d", [P, TPC, 2], F32)
        iota8 = at("iota8", [P, EXPERTS], F32)
        comb = at("comb", [P, TILES, EXPERTS], F32)
        stats = at("stats", [P, TPB, 6], F32)
        mv = at("mv", [P, TPB, 2], F32)
        ln = at("ln", [P, TPB, 8], F32)
        rq = at("rq", [P, 8], F32)
        sums = at("sums", [P, 4], F32)
        temp_at = place[0]

        def region(first):
            place[0] = first

        ha = at("ha", [P, D], F32)
        hTa = at("hTa", [P, 2, KB, P], F32R)
        e_q = at("e_q", [P, TPB, D], F32)
        w_k = at("w_k", [P, D], F32)
        wv_f = at("wv_f", [P, D], F32)
        wv_s = at("wv_s", [P, TPB, 2, 2, D], F32R)
        wce = at("wce", [P, 2 * SEQ], F32)
        tri_f = at("tri_f", [P, 2 * P], F32, off=place[0])
        den = at("den", [P, 2 * SEQ], F32)
        region(temp_at)
        m_s = at("m_s", [P, 2, 2, JB, CHUNK], F32R)
        m_f = at("m_f", [P, JB, CHUNK], F32)
        sg = at("sg", [P, JB, CHUNK], F32)
        mlp_end = place[0]
        hd = at("hd", [P, TPC, D], F32)
        gl = at("gl", [P, 8, TPC, EXPERTS], F32)
        gs = at("gs", [P, 4, TPC], F32)
        gi = at("gi", [P, TPC, EXPERTS], U32)
        region(temp_at)
        q4 = at("q4", [P, HEADS, 4, HD], F32)
        v32 = at("v32", [P, 2, TPB, KVG, 2 * HD], F32)
        msk = at("msk", [P, 2, 3, P], F32)
        sc = at("sc", [P, 4, 512], F32)
        pt = at("pt", [P, 3, 512], F32)
        mxs = at("mxs", [P, 4, 4], F32)
        rden = at("rden", [P, 16], F32)
        region(raw0_at)
        ctx_raw = at("ctx_raw", [P, KB, SEQ], F32)
        hc = at("hc", [P, D], F32)
        msk_i = at("msk_i", [P, SEQ], I32)
        pad = at("pad", [P, SEQ], F32)
        k4 = at("k4", [P, TPB, KVG, 4, HD], F32)
        assert place[0] <= raw1_at
        region(raw1_at)
        o_tok0 = at("o_tok0", [P, TPB, D], F32)
        o_tok1 = at("o_tok1", [P, TPB, D], F32)
        o_raw = at("o_raw", [P, 2, 512], F32)
        assert place[0] <= raw1_at + 4 * SLOT
        o_tok = [o_tok0, o_tok1]
        region(feat_at)
        q4T = at("q4T", [P, 2, HEADS // 2, SEQ], F32R)
        k4T = at("k4T", [P, 2, PAIRS, SEQ], F32R)
        ctx_s = at("ctx_s", [P, 2, KB, SEQ], F32R)
        hTc = at("hTc", [P, TPB, 2, KB, P], F32R)
        oT = at("oT", [P, TPB, 2, KB, P], F32R)
        assert place[0] <= feat_at + 65536

        ps = es.enter_context(nc.psum_tensor("ps", [P, 8, 512], F32))

        names = set()

        def sem(name):
            assert name not in names
            names.add(name)
            return es.enter_context(nc.semaphore(name))

        raw_loaded = [sem(f"raw_loaded{p}") for p in range(2)]
        w_ready = [sem(f"w_ready{p}") for p in range(2)]
        w_free = [sem(f"w_free{p}") for p in range(2)]
        pool_self = sem("pool_self")
        pool_held = sem("pool_held")
        dve_held = sem("dve_held")
        consts = sem("consts")
        x_first = sem("x_first")
        x_rest = sem("x_rest")
        a = {n: sem("a_" + n) for n in (
            "stats", "rstd", "h", "acc", "hT_ps", "hT_hi", "hT", "q", "k", "v", "ssq", "rms", "e", "w",
            "wv", "split", "pool", "dve", "scan", "wce", "den", "y", "yhi", "yT")}
        c = {n: sem("c_" + n) for n in (
            "ones", "ctx", "ctx_s", "mask_i", "pad", "mask", "dve", "pool", "stats", "rstd", "h", "hT_ps", "hT_hi",
            "kv_ps", "kv_hi", "k4T_ps", "q_ps", "q_hi", "q4", "q4T_ps", "oT_ps", "oT_hi", "wo_ps",
            "S", "mx", "P", "PT_ps", "O", "o_raw", "n_ps", "rden")}
        piece_read = [sem(f"c_piece_read{k}") for k in range(PIECE_BANKS)]
        PT_read = [sem(f"c_PT_read{k}") for k in range(2)]
        d = {n: sem("d_" + n) for n in (
            "iota", "stats", "rstd", "h", "hT_ps", "hT_hi", "hT", "dve", "pool", "logit", "copied", "shifted", "ex")}
        mlp = [{n: sem(f"mlp{i}_{n}") for n in ("up", "silu", "m", "hi", "lo", "down", "acc")} for i in range(2)]
        stored = sem("stored")

        block = es.enter_context(nc.Block())

        def slot_block(p, part, at_, n):
            return wsplit[:, p, part, at_:at_ + n]

        @block.sync
        def _(sp):
            x_v = x.rearrange("(t p) d -> p t d", p=P)
            out_v = out.rearrange("(t p) d -> p t d", p=P)
            sp.dma_start(acc[:, 0:TPB, :], x_v[:, 0:TPB, :]).then_inc(x_first, 16)
            for s in range(2):
                sp.dma_start(wraw[:, s, :], weights[s]).then_inc(raw_loaded[s], 16)
            sp.dma_start(acc[:, TPB:TILES, :], x_v[:, TPB:TILES, :]).then_inc(x_rest, 16)
            with sp.Fori(1, SLOT_X // 2) as n:
                for p in range(2):
                    sp.wait_ge(w_ready[p], n)
                    sp.dma_start(wraw[:, p, :], weights[bass.ds(2 * n + p, 1)].rearrange("s p n -> (s p) n")).then_inc(raw_loaded[p], 16)
            n = SLOT_X // 2
            for p in range(2):
                sp.wait_ge(w_ready[p], n)
                sp.dma_start(wraw[:, p, :], weights[2 * n + p]).then_inc(raw_loaded[p], 16)

            sp.wait_ge(w_ready[0], SLOT_X // 2 + 1)
            for b in range(BATCH):
                after(sp, c["ctx_s"], b)
                sp.dma_start(ctx_raw[:, :, :], ctx_t[b]).then_inc(c["ctx"], 16)
                after(sp, c["mask"], b)
                sp.dma_start(msk_i[:, :], mask[b:b + 1].broadcast_to([P, SEQ])).then_inc(c["mask_i"], 16)
            sp.wait_ge(c["ctx_s"], BATCH)
            sp.wait_ge(c["mask"], BATCH)
            k, n = piece_turn("k4T1", BATCH - 2)
            sp.wait_ge(piece_read[k], n + 1)
            sp.dma_start(wraw[:, 0, :], weights[SLOT_MOE]).then_inc(raw_loaded[0], 16)
            k, n = piece_turn("oT1", BATCH)
            sp.wait_ge(piece_read[k], n + 1)
            sp.dma_start(wraw[:, 1, :], weights[SLOT_MOE + 1]).then_inc(raw_loaded[1], 16)
            with sp.Fori(SLOT_MOE // 2 + 1, SLOTS // 2) as n:
                for p in range(2):
                    sp.wait_ge(w_ready[p], n)
                    sp.dma_start(wraw[:, p, :], weights[bass.ds(2 * n + p, 1)].rearrange("s p n -> (s p) n")).then_inc(raw_loaded[p], 16)
            sp.wait_ge(w_ready[0], SLOTS // 2)
            sp.dma_start(wraw[:, 0, :], weights[SLOTS - 1]).then_inc(raw_loaded[0], 16)
            total = 4 * CHUNKS * (1 + EXPERTS)
            for ch in range(CHUNKS):
                sp.wait_ge(mlp[1]["acc"], total - 4 * (CHUNKS - 1 - ch))
                t = slice(ch * TPC, (ch + 1) * TPC)
                sp.dma_start(out_v[:, t, :], acc[:, t, :]).then_inc(stored, 16)
            sp.wait_ge(stored, 16 * CHUNKS)

        @block.gpsimd
        def _(pool):
            nc.gpsimd.memset(half_neg[:, :], -0.5).then_inc(consts, 1)
            nc.gpsimd.memset(tri_f[:, :], 1.0).then_inc(pool_self, 1)
            nc.gpsimd.memset(ident[:, :], 0.0).then_inc(pool_self, 1)
            nc.gpsimd.memset(causal[:, :], 0.0).then_inc(pool_self, 1)
            pool.wait_ge(pool_self, 3)
            nc.gpsimd.affine_select(out=ident[:, :], in_=ident[:, :], compare_op=ALU.not_equal, fill=1.0,
                                    base=0, pattern=[[-1, P]], channel_multiplier=1).then_inc(consts, 1)
            nc.gpsimd.affine_select(out=tri_f[:, 0:P], in_=tri_f[:, 0:P], compare_op=ALU.is_ge, fill=0.0,
                                    base=0, pattern=[[1, P]], channel_multiplier=-1).then_inc(pool_self, 1)
            nc.gpsimd.affine_select(out=causal[:, P:SEQ], in_=causal[:, P:SEQ], compare_op=ALU.is_ge, fill=MASKED,
                                    base=0, pattern=[[-1, P]], channel_multiplier=1).then_inc(consts, 1)
            nc.gpsimd.iota(iota8[:, :], pattern=[[1, EXPERTS]], base=0, channel_multiplier=0,
                           allow_small_or_imprecise_dtypes=True).then_inc(d["iota"], 1)
            pool.wait_ge(pool_self, 4)
            nc.gpsimd.tensor_copy(tri[:, :], tri_f[:, :]).then_inc(consts, 1)
            nc.gpsimd.tensor_copy(ones_row[:, :], tri_f[0:1, P:2 * P]).then_inc(consts, 1)

            split_count = [0]
            split_self = sem("split_self")

            def split(p, n, base):
                hold(pool, raw_loaded[p], 16 * n + 16, pool_held)
                if not isinstance(n, int) or n >= 1:
                    hold(pool, w_free[p], n, pool_held)
                nc.gpsimd.tensor_copy(wsplit[:, p, 0, :], wraw[:, p, :]).then_inc(split_self, 1)
                hold(pool, split_self, base + 1, pool_held)
                nc.gpsimd.tensor_tensor(out=wsplit[:, p, 1, :], in0=wraw[:, p, :], in1=wsplit[:, p, 0, :],
                                        op=ALU.subtract).then_inc(w_ready[p], 1)

            split(1, 0, 0)

            PER_A = 2 * 11

            def rstd_a(b, ch):
                hold(pool, a["stats"], b + 1, pool_held)
                for t in range(TPB):
                    m, v = mv[:, t, 0:1], mv[:, t, 1:2]
                    L = [ln[:, t, i:i + 1] for i in range(8)]
                    ch.link(nc.gpsimd.tensor_scalar(L[4], v, 1.0, LN_EPS, ALU.mult, ALU.add))
                    ch.link(nc.gpsimd.tensor_tensor(out=L[0], in0=L[4], in1=half_neg[:, 0:1], op=ALU.pow))
                    ch.link(nc.gpsimd.tensor_tensor(out=L[5], in0=v, in1=L[0], op=ALU.mult))
                    ch.link(nc.gpsimd.tensor_tensor(out=L[5], in0=L[5], in1=L[0], op=ALU.mult))
                    ch.link(nc.gpsimd.tensor_scalar(L[5], L[5], 1.0, RMS_EPS, ALU.mult, ALU.add))
                    ch.link(nc.gpsimd.tensor_tensor(out=L[6], in0=L[5], in1=half_neg[:, 0:1], op=ALU.pow))
                    ch.link(nc.gpsimd.tensor_tensor(out=L[1], in0=L[6], in1=L[0], op=ALU.mult))
                    ch.link(nc.gpsimd.tensor_scalar(L[2], L[0], 1.0, 1.0, ALU.mult, ALU.add))
                    ch.link(nc.gpsimd.tensor_tensor(out=L[7], in0=m, in1=L[0], op=ALU.mult))
                    ch.link(nc.gpsimd.tensor_scalar(L[3], L[7], -1.0, 0.0, ALU.mult, ALU.add))
                    ins = nc.gpsimd.tensor_scalar(L[4], L[3], 1.0, 0.0, ALU.mult, ALU.add)
                    ch.mark(ins)
                ch.wait(ch.n)
                pool.sem_inc(a["rstd"], 1)

            PER_T = 14

            def rms_and_split(b, tt, ch):
                t = 2 * b + tt
                for i in range(2):
                    hold(pool, a["ssq"], 2 * t + i + 1, pool_held)
                    ch.link(nc.gpsimd.tensor_scalar(rq[:, 2 + i:3 + i], sums[:, i:i + 1], 1.0 / D, RMS_EPS, ALU.mult, ALU.add))
                    ch.link(nc.gpsimd.tensor_tensor(out=rq[:, 4 + i:5 + i], in0=rq[:, 2 + i:3 + i], in1=half_neg[:, 0:1], op=ALU.pow))
                    ch.link(nc.gpsimd.tensor_scalar(rq[:, i:i + 1], rq[:, 4 + i:5 + i], [-1.0, 1.0][i], 0.0, ALU.mult, ALU.add))
                    pool.sem_inc(a["rms"], 1)
                if not isinstance(b, int) or b >= 1:
                    hold(pool, a["scan"], 2 * b, pool_held)
                hold(pool, a["w"], t + 1, pool_held)
                ch.link(nc.gpsimd.tensor_copy(wv_s[:, tt, 0, 0, :], w_k[:, :]))
                ch.link(nc.gpsimd.tensor_tensor(out=wv_s[:, tt, 0, 1, :], in0=w_k[:, :], in1=wv_s[:, tt, 0, 0, :], op=ALU.subtract))
                hold(pool, a["wv"], t + 1, pool_held)
                ch.link(nc.gpsimd.tensor_copy(wv_s[:, tt, 1, 0, :], wv_f[:, :]))
                ch.link(nc.gpsimd.tensor_tensor(out=wv_s[:, tt, 1, 1, :], in0=wv_f[:, :], in1=wv_s[:, tt, 1, 0, :], op=ALU.subtract))
                pool.sem_inc(a["split"], 1)

            def batch_a(b, last):
                per = PER_A + 2 * 10
                ch = Chain(pool, a["pool"], b * per + PER_A, None, pool_held)
                for tt in range(TPB):
                    rms_and_split(b, tt, ch)
                if not last:
                    rstd_a(b + 1, ch)
                    assert ch.n == per, ch.n

            rstd_a(0, Chain(pool, a["pool"], 0))
            with pool.Fori(0, BATCH - 1) as b:
                batch_a(b, False)
            batch_a(BATCH - 1, True)

            with pool.Fori(0, SLOT_X // 2 - 1) as n:
                split(0, n + 1, 2 * n + 1)
                split(1, n + 1, 2 * n + 2)
            base = 1 + 2 * (SLOT_X // 2 - 1)
            split(0, SLOT_X // 2, base)
            split(1, SLOT_X // 2, base + 1)
            base += 2

            PER_C = 4 + 2 + 2

            def ctx_split(b, ch):
                hold(pool, c["ctx"], 16 * b + 16, pool_held)
                if not isinstance(b, int) or b >= 1:
                    hold(pool, c["kv_ps"], b, pool_held)
                ch.link(nc.gpsimd.tensor_copy(ctx_s[:, 0, :, :], ctx_raw[:, :, :]))
                ch.link(nc.gpsimd.tensor_tensor(out=ctx_s[:, 1, :, :], in0=ctx_raw[:, :, :], in1=ctx_s[:, 0, :, :], op=ALU.subtract))
                pool.sem_inc(c["ctx_s"], 1)

            def batch_c(b, last):
                ch = Chain(pool, c["pool"], b * PER_C + 2, PER_C, pool_held)
                hold(pool, c["stats"], b + 1, pool_held)
                for t in range(TPB):
                    ch.link(nc.gpsimd.tensor_scalar(ln[:, t, 4:5], mv[:, t, 1:2], 1.0, LN_EPS, ALU.mult, ALU.add))
                    ch.link(nc.gpsimd.tensor_tensor(out=ln[:, t, 0:1], in0=ln[:, t, 4:5], in1=half_neg[:, 0:1], op=ALU.pow))
                pool.sem_inc(c["rstd"], 1)
                if not last:
                    ctx_split(b + 1, ch)
                for t in range(TPB):
                    k, n = piece_turn(f"q{t}", b - 1)
                    hold(pool, piece_read[k], n + 1, pool_held)
                    ch.link(nc.gpsimd.tensor_copy(q4[:, :, 2:4, :], q4[:, :, 0:2, :]))
                    pool.sem_inc(c["q4"], 1)
                if not last:
                    ch.done()

            ctx_split(0, Chain(pool, c["pool"], 0, 2, pool_held))
            with pool.Fori(0, BATCH - 1) as b:
                batch_c(b, False)
            batch_c(BATCH - 1, True)

            split(0, SLOT_MOE // 2, base)
            ch = Chain(pool, d["pool"])
            for cc in range(CHUNKS):
                pool.wait_ge(d["stats"], cc + 1)
                ch.link(nc.gpsimd.tensor_scalar(ln_d[:, :, 0:1], mv_d[:, :, 1:2], 1.0, LN_EPS, ALU.mult, ALU.add))
                ch.link(nc.gpsimd.tensor_tensor(out=ln_d[:, :, 1:2], in0=ln_d[:, :, 0:1],
                                                in1=half_neg[:, 0:TPC].rearrange("p (t o) -> p t o", o=1), op=ALU.pow))
                pool.sem_inc(d["rstd"], 1)
            split(1, SLOT_MOE // 2, base + 1)
            with pool.Fori(0, SLOTS // 2 - SLOT_MOE // 2 - 1) as n:
                split(0, n + (SLOT_MOE // 2 + 1), 2 * n + base + 2)
                split(1, n + (SLOT_MOE // 2 + 1), 2 * n + base + 3)
            split(0, SLOTS // 2, base + 2 + 2 * (SLOTS // 2 - SLOT_MOE // 2 - 1))

        def three(pe, out_, w_hi, w_lo, m_hi, m_lo, first, last):
            nc.tensor.matmul(out_, w_hi, m_hi, start=first, stop=False)
            nc.tensor.matmul(out_, w_lo, m_hi, start=False, stop=False)
            return nc.tensor.matmul(out_, w_hi, m_lo, start=False, stop=last)

        def mlp_pe(pe, s_, groups, slot0, input_ready):
            first_parity = slot0 % 2

            def weights_of(g_par, part):
                return lambda at_, n: slot_block(g_par, part, at_, n)

            def up(s, par, ch, first_of_group, wait_n, static0):
                if first_of_group:
                    pe.wait_ge(w_ready[par], wait_n)
                for j in range(JB):
                    if not static0:
                        pe.wait_ge(s_["m"], JB * s + j - 1)
                    if input_ready is not None and isinstance(s, int) and s < CHUNKS:
                        pe.wait_ge(*input_ready(s))
                    for kind in range(2):
                        for k in range(KB):
                            o = ((kind * JB + j) * KB + k) * P
                            mm = three(pe, ps[:, 2 * j + kind, :], slot_block(par, 0, o, P), slot_block(par, 1, o, P),
                                       feat[:, 0, k, ch * CHUNK:(ch + 1) * CHUNK], feat[:, 1, k, ch * CHUNK:(ch + 1) * CHUNK],
                                       k == 0, k == KB - 1)
                    mm.then_inc(s_["up"], 1)

            def down(s, par, ch, static0):
                sp_ = ch % 2
                pe.wait_ge(s_["lo"], JB * s + JB)
                for t in range(TPC):
                    if not static0:
                        pe.wait_ge(s_["acc"], TPC * s + t - 3)
                    for j in range(JB):
                        o = 2 * JB * KB * P + j * D
                        mm = three(pe, ps[:, 4 + t, :], m_s[:, sp_, 0, j, t * P:(t + 1) * P], m_s[:, sp_, 1, j, t * P:(t + 1) * P],
                                   slot_block(par, 0, o, D), slot_block(par, 1, o, D), j == 0, j == JB - 1)
                    mm.then_inc(s_["down"], 1)
                if ch == CHUNKS - 1:
                    pe.sem_inc(w_free[par], 1) if False else None

            return up, down

        @block.tensor
        def _(pe):
            pe.wait_ge(consts, 5)

            def qkv(b, tt):
                t = 2 * b + tt
                hb = 0 if tt == 0 else 7
                pe.wait_ge(a["h"], t + 1)
                for k in range(KB):
                    tr = nc.tensor.transpose(ps[:, hb, k * P:(k + 1) * P], ha[:, k * P:(k + 1) * P], ident[:, :])
                tr.then_inc(a["hT_ps"], 1)
                pe.wait_ge(a["hT"], t + 1)
                for i, (name, freed) in enumerate((("q", "e"), ("k", "w"), ("v", "wv"))):
                    if not isinstance(b, int) or b + tt >= 1:
                        pe.wait_ge(a[freed], t)
                    for k in range(KB):
                        col = (i * KB + k) * D
                        p, o = col // SLOT, col % SLOT
                        mm = three(pe, ps[:, 1 + i, :], hTa[:, 0, k, :], hTa[:, 1, k, :],
                                   slot_block(p, 0, o, D), slot_block(p, 1, o, D), k == 0, k == KB - 1)
                    mm.then_inc(a[name], 1)

            def scan(b, half):
                s = 2 * b + half
                if half == 0:
                    pe.wait_ge(a["split"], 2 * b + 2)
                if not (isinstance(b, int) and b == 0 and half == 0):
                    pe.wait_ge(a["y"], s)
                for bank, kind in ((4, 1), (5, 0)):
                    for i in range(2):
                        blk = slice((2 * half + i) * P, (2 * half + i + 1) * P)
                        o = ps[:, bank, i * SEQ:(i + 1) * SEQ]
                        nc.tensor.matmul(o, wv_s[:, 0, kind, 0, blk], tri[:, :], start=True, stop=False)
                        nc.tensor.matmul(o, wv_s[:, 0, kind, 1, blk], tri[:, :], start=False, stop=False)
                        o1 = ps[:, bank, i * SEQ + P:(i + 1) * SEQ]
                        nc.tensor.matmul(o1, wv_s[:, 1, kind, 0, blk], tri[:, 0:P], start=False, stop=False)
                        nc.tensor.matmul(o1, wv_s[:, 1, kind, 1, blk], tri[:, 0:P], start=False, stop=True)
                for i in range(2):
                    blk = slice((2 * half + i) * P, (2 * half + i + 1) * P)
                    for tt in range(TPB):
                        tr = nc.tensor.transpose(ps[:, 6, i * SEQ + tt * P:i * SEQ + (tt + 1) * P], e_q[:, tt, blk], ident[:, :])
                tr.then_inc(a["scan"], 1)

            pe.wait_ge(w_ready[0], 1)
            pe.wait_ge(w_ready[1], 1)
            qkv(0, 0)
            qkv(0, 1)
            with pe.Fori(0, BATCH - 1) as b:
                scan(b, 0)
                scan(b, 1)
                qkv(b + 1, 0)
                qkv(b + 1, 1)
            pe.sem_inc(w_free[0], 1)
            pe.sem_inc(w_free[1], 1)
            scan(BATCH - 1, 0)
            scan(BATCH - 1, 1)

            def run_mlp(s_, groups, slot0, before_up):
                up, down = mlp_pe(pe, s_, groups, slot0, None)
                last_group = groups - 1

                def pair(s, r, g_static, n_expr, parity, last):
                    pass

                par0 = slot0 % 2
                n0 = slot0 // 2

                def steps(s0, count, slot_half, par_first, last, ch0=0):
                    for g in range(count):
                        par = (par_first + g) % 2
                        for ch in range(ch0, CHUNKS):
                            s = s0 + (g * CHUNKS + ch - ch0)
                            final = last and g == count - 1 and ch == CHUNKS - 1
                            if not final:
                                nch = (ch + 1) % CHUNKS
                                npar = par if nch else 1 - par
                                turn = slot_half + ((par_first + g) // 2 if nch else (par_first + g + 1) // 2)
                                before_up(s, nch)
                                up(s + 1, npar, nch, nch == 0, turn + 1, False)
                            down(s, par, ch, isinstance(s, int) and s == 0)
                            if ch == CHUNKS - 1:
                                pe.wait_ge(s_["down"], TPC * s + TPC)
                                pe.sem_inc(w_free[par], 1)

                return up, down, steps

            def run_b():
                pe.wait_ge(a["yT"], 2 * BATCH)
                up, down, steps = run_mlp(mlp[0], MLP_GROUPS, SLOT_MLP, lambda s, ch: None)
                up(0, 0, 0, True, SLOT_MLP // 2 + 1, True)
                steps(0, 2, SLOT_MLP // 2, 0, False)
                with pe.Fori(1, MLP_GROUPS // 2 - 1) as i:
                    steps(i * (2 * CHUNKS), 2, i + SLOT_MLP // 2, 0, False)
                i = MLP_GROUPS // 2 - 1
                steps(i * 2 * CHUNKS, 2, i + SLOT_MLP // 2, 0, True)

            run_b()

            def piece(name, b, sides):
                k, n = piece_turn(name, b)
                after(pe, piece_read[k], n)
                if piece_side(name) not in sides:
                    pe.sem_inc(piece_read[k], 1)
                    return
                bank = ps[:, 6 + k, :]

                def ready(other):
                    ko, no = piece_turn(other, b)
                    pe.wait_ge(piece_read[ko], no + 1)

                tt = int(name[3] if name[:2] == "q4" or name[:2] == "k4" else name[-1]) if name != "kv" else 0
                if name == "kv":
                    pe.wait_ge(c["ctx_s"], b + 2)
                    for t in range(TPB):
                        for kb in range(KB):
                            o = KB * D + kb * 2 * P
                            mm = three(pe, bank[:, t * SEQ:(t + 1) * SEQ], ctx_s[:, 0, kb, t * P:(t + 1) * P],
                                       ctx_s[:, 1, kb, t * P:(t + 1) * P], slot_block(0, 0, o, 2 * P), slot_block(0, 1, o, 2 * P),
                                       kb == 0, kb == KB - 1)
                    mm.then_inc(c["kv_ps"], 1)
                elif name[:3] == "k4T":
                    tt = int(name[3])
                    ready("kv")
                    for p in range(PAIRS):
                        tr = nc.tensor.transpose(bank[:, p * P:(p + 1) * P], k4[:, tt, 2 * p:2 * p + 2, :, :].rearrange("t g r d -> t (g r d)"),
                                                 ident[:, :])
                    tr.then_inc(c["k4T_ps"], 1)
                elif name[:2] == "hT":
                    pe.wait_ge(c["h"], 2 * (b + 1) + tt + 1)
                    for kb in range(KB):
                        tr = nc.tensor.transpose(bank[:, kb * P:(kb + 1) * P], hc[:, kb * P:(kb + 1) * P], ident[:, :])
                    tr.then_inc(c["hT_ps"], 1)
                elif name[:3] == "q4T":
                    tt, r = int(name[3]), int(name[4])
                    pe.wait_ge(c["q4"], 2 * (b + 1) + tt + 1)
                    for i in range(4):
                        n = 4 * r + i
                        tr = nc.tensor.transpose(bank[:, i * P:(i + 1) * P], q4[:, 2 * n:2 * n + 2, :, :].rearrange("t h r d -> t (h r d)"),
                                                 ident[:, :])
                    tr.then_inc(c["q4T_ps"], 1)
                elif name[:1] == "q":
                    ready(f"hT{tt}")
                    for kb in range(KB):
                        mm = three(pe, bank, hTc[:, tt, 0, kb, :], hTc[:, tt, 1, kb, :],
                                   slot_block(0, 0, kb * D, D), slot_block(0, 1, kb * D, D), kb == 0, kb == KB - 1)
                    mm.then_inc(c["q_ps"], 1)
                elif name[0] == "n":
                    n = 4 * (b - int(name[1])) + 2 * int(name[1]) + tt
                    pe.wait_ge(c["o_raw"], n + 1)
                    for i in range(4):
                        tr = nc.tensor.transpose(bank[:, i * P:(i + 1) * P], o_raw[:, tt, i * P:(i + 1) * P], ident[:, :])
                    tr.then_inc(c["n_ps"], 1)
                elif name[:2] == "oT":
                    ready("n11")
                    for kb in range(KB):
                        tr = nc.tensor.transpose(bank[:, kb * P:(kb + 1) * P], o_tok[par(b, 1)][:, tt, kb * P:(kb + 1) * P], ident[:, :])
                    tr.then_inc(c["oT_ps"], 1)
                else:
                    ready(f"oT{tt}")
                    bo = KB * (D + EXPERTS)
                    nc.tensor.matmul(bank, ones_row[:, :], wsplit[0:1, 1, 0, bo:bo + D], start=True, stop=False)
                    nc.tensor.matmul(bank, ones_row[:, :], wsplit[0:1, 1, 1, bo:bo + D], start=False, stop=False)
                    for kb in range(KB):
                        mm = three(pe, bank, oT[:, tt, 0, kb, :], oT[:, tt, 1, kb, :],
                                   slot_block(1, 0, kb * D, D), slot_block(1, 1, kb * D, D), False, kb == KB - 1)
                    mm.then_inc(c["wo_ps"], 1)

            parity_now = [0]

            def par(b, back):
                return (parity_now[0] + back) % 2

            def scores(b, u):
                v, heads, tile = unit_of(u)
                after(pe, c["mx"], UNITS * b + u - 1)
                rows = slice(64 * (v % 2), 64 * (v % 2) + 64)
                w = P * (tile + 1)
                for n, i in enumerate(heads):
                    mm = nc.tensor.matmul(ps[:, u % 2, n * w:(n + 1) * w], q4T[rows, par(b, 0), 4 * (v // 2) + i, tile * P:(tile + 1) * P],
                                          k4T[rows, par(b, 0), v // 2, 0:w], start=True, stop=True)
                mm.then_inc(c["S"], 1)

            def probs_t(b, u):
                pe.wait_ge(c["P"], UNITS * b + u + 1)
                after(pe, PT_read[u % 2], UNITS // 2 * b + u // 2)
                for i in range(4):
                    tr = nc.tensor.transpose(ps[:, 2 + u % 2, i * P:(i + 1) * P], sc[:, u % 4, i * P:(i + 1) * P], ident[:, :])
                tr.then_inc(c["PT_ps"], 1)

            def attend(b, u, back):
                v, heads, tile = unit_of(u % UNITS)
                pe.wait_ge(PT_read[u % 2], UNITS // 2 * b + u // 2 + 1)
                if u % UNITS % 12 in (0, 4):
                    ends = sum(u % UNITS > e for e in QUAD_ENDS)
                    after(pe, c["o_raw"], 4 * (b + u // UNITS) + ends - 1)
                rows = slice(32 * (v % 4), 32 * (v % 4) + 32)
                p_in = pt[:, u % 3, :].rearrange("p (n m t) -> p m n t", m=tile + 1, t=P)
                for m in range(tile + 1):
                    mm = nc.tensor.matmul(ps[rows, 4 + tile, heads[0] * P:(heads[-1] + 1) * P], v32[:, par(b, back), m, v, :],
                                          p_in[:, m, :, :], start=(m == 0), stop=(m == tile))
                mm.then_inc(c["O"], 1)

            def pass_c(b, sides, units=UNITS):
                first = isinstance(b, int) and b == 0
                for u in range(UNITS):
                    if units:
                        for name in {0: ["q4T02", "q4T03"], 4: ["q4T12", "q4T13"]}.get(u, []):
                            k, n = piece_turn(name, b - 1)
                            pe.wait_ge(piece_read[k], n + 1)
                        scores(b, u)
                    if units or u < 3:
                        if u >= 2 or not first:
                            if units or u < 2:
                                probs_t(b, u - 2)
                        if u >= 3 or not first:
                            attend(b, u - 3, int(u < 3))
                    if u in PIECES:
                        piece(PIECES[u], b, sides)

            pe.wait_ge(w_ready[0], SLOT_X // 2 + 1)
            pe.wait_ge(w_ready[1], SLOT_X // 2 + 1)
            pe.wait_ge(mlp[0]["acc"], TPC * CHUNKS * MLP_GROUPS)
            for name in ORDER:
                parity_now[0] = 1
                piece(name, -1, ("in",))
            parity_now[0] = 0
            pass_c(0, ("in", "own"))
            with pe.Fori(0, BATCH // 2 - 1) as i:
                for half in range(2):
                    parity_now[0] = (1 + half) % 2
                    pass_c(2 * i + (1 + half), ("in", "own", "out"))
            pe.sem_inc(w_free[0], 1)
            parity_now[0] = (BATCH - 1) % 2
            pass_c(BATCH - 1, ("own", "out"))
            parity_now[0] = BATCH % 2
            pass_c(BATCH, ("out",), 0)

            def prep(cc):
                for t in range(TPC):
                    g = TPC * cc + t
                    pe.wait_ge(d["h"], g + 1)
                    if t < 2 and cc >= 2:
                        pe.wait_ge(mlp[1]["acc"], TPC * (cc - 1))
                    if t >= 2:
                        pe.wait_ge(d["hT"], g - 1)
                    for k in range(KB):
                        tr = nc.tensor.transpose(ps[:, 4 + t % 2, k * P:(k + 1) * P], hd[:, t, k * P:(k + 1) * P], ident[:, :])
                    tr.then_inc(d["hT_ps"], 1)
                for t in range(TPC):
                    g = TPC * cc + t
                    pe.wait_ge(d["hT"], g + 1)
                    n = 0
                    for k in range(KB):
                        for hp in range(2):
                            for wp in range(2):
                                mm = nc.tensor.matmul(ps[:, 6, t * EXPERTS:(t + 1) * EXPERTS], feat[:, hp, k, g * P:(g + 1) * P],
                                                      slot_block(1, wp, KB * D + k * EXPERTS, EXPERTS), start=(n == 0), stop=(n == 15))
                                n += 1
                mm.then_inc(d["logit"], 1)

            k, n = piece_turn("wo1", BATCH)
            pe.wait_ge(piece_read[k], n + 1)
            s_ = mlp[1]
            up, down, steps = run_mlp(s_, 1 + EXPERTS, SLOT_MOE, lambda s, ch: None)
            prep(0)
            up(0, 0, 0, True, SLOT_MOE // 2 + 1, True)
            prep(1)
            for cc in range(1, CHUNKS):
                up(cc, 0, cc, False, 0, False)
                pe.wait_ge(d["copied"], min(cc + 1, CHUNKS))
                down(cc - 1, 0, cc - 1, cc == 1)
                if cc + 1 < CHUNKS:
                    prep(cc + 1)
            pe.wait_ge(d["logit"], CHUNKS)
            pe.sem_inc(w_free[1], 1)
            steps(CHUNKS - 1, 1, SLOT_MOE // 2, 0, False, CHUNKS - 1)
            with pe.Fori(0, EXPERTS // 2 - 1) as i:
                steps(i * (2 * CHUNKS) + CHUNKS, 2, i + SLOT_MOE // 2, 1, False)
            i = EXPERTS // 2 - 1
            steps(i * 2 * CHUNKS + CHUNKS, 2, i + SLOT_MOE // 2, 1, True)

        def mlp_act(act, s_):
            def act_step(s, ch, static0):
                for j in range(JB):
                    act.wait_ge(s_["up"], JB * s + j + 1)
                    nc.scalar.activation(sg[:, j, :], ps[:, 2 * j + 1, :], ACT.Silu).then_inc(s_["silu"], 1)
                    act.wait_ge(s_["m"], JB * s + j + 1)
                    if not (isinstance(s, int) and s < 2):
                        act.wait_ge(s_["down"], TPC * s - TPC)
                    nc.scalar.copy(m_s[:, ch % 2, 0, j, :], m_f[:, j, :]).then_inc(s_["hi"], 1)
            return act_step

        @block.scalar
        def _(act):
            def tile_a(b, tt):
                t = 2 * b + tt
                hb = 0 if tt == 0 else 7
                act.wait_ge(a["hT_ps"], t + 1)
                if not isinstance(b, int) or b + tt >= 1:
                    act.wait_ge(a["v"], t)
                nc.scalar.copy(hTa[:, 0, :, :], ps[:, hb, :]).then_inc(a["hT_hi"], 1)
                act.wait_ge(a["q"], t + 1)
                if (not isinstance(b, int)) or b >= 1:
                    act.wait_ge(a["scan"], 2 * b)
                nc.scalar.activation(e_q[:, tt, :], ps[:, 1, :], ACT.Square, accum_out=sums[:, 0:1]).then_inc(a["ssq"], 1)
                act.wait_ge(a["rms"], 2 * t + 1)
                nc.scalar.activation(e_q[:, tt, :], ps[:, 1, :], ACT.Exp, scale=rq[:, 0:1]).then_inc(a["e"], 1)
                act.wait_ge(a["k"], t + 1)
                if not isinstance(b, int) or b + tt >= 1:
                    act.wait_ge(a["split"], t)
                nc.scalar.activation(w_k[:, :], ps[:, 2, :], ACT.Square, accum_out=sums[:, 1:2]).then_inc(a["ssq"], 1)
                act.wait_ge(a["rms"], 2 * t + 2)
                nc.scalar.activation(w_k[:, :], ps[:, 2, :], ACT.Exp, scale=rq[:, 1:2]).then_inc(a["w"], 1)

            def scan_a(b, half):
                s = 2 * b + half
                act.wait_ge(a["scan"], s + 1)
                if not (isinstance(b, int) and b == 0 and half == 0):
                    act.wait_ge(a["den"], s)
                nc.scalar.activation(wce[:, :], ps[:, 5, :], ACT.Copy, bias=1e-6).then_inc(a["wce"], 1)
                act.wait_ge(a["y"], s + 1)
                dst = feat[:, 0, 2 * half:2 * half + 2, bass.ds(b * SEQ, SEQ)] if not isinstance(b, int) else \
                    feat[:, 0, 2 * half:2 * half + 2, b * SEQ:(b + 1) * SEQ]
                nc.scalar.copy(dst, den[:, :].rearrange("p (k n) -> p k n", k=2)).then_inc(a["yhi"], 1)

            tile_a(0, 0)
            tile_a(0, 1)
            with act.Fori(0, BATCH - 1) as b:
                scan_a(b, 0)
                scan_a(b, 1)
                tile_a(b + 1, 0)
                tile_a(b + 1, 1)
            scan_a(BATCH - 1, 0)
            scan_a(BATCH - 1, 1)
            act.wait_ge(a["yT"], 2 * BATCH)

            step = mlp_act(act, mlp[0])
            for s in range(2 * CHUNKS):
                step(s, s % CHUNKS, s == 0)
            with act.Fori(1, MLP_GROUPS // 2) as i:
                for r in range(2 * CHUNKS):
                    step(i * (2 * CHUNKS) + r, r % CHUNKS, False)

            def piece(name, b, pb):
                k, n = piece_turn(name, b)
                bank = ps[:, 6 + k, :]
                if name[:3] == "k4T":
                    t = int(name[3])
                    act.wait_ge(c["k4T_ps"], 2 * (b + 1) + t + 1)
                    nc.scalar.copy(k4T[:, pb, :, t * P:(t + 1) * P], bank.rearrange("p (k n) -> p k n", k=PAIRS)).then_inc(piece_read[k], 1)
                elif name[:3] == "q4T":
                    t, r = int(name[3]), int(name[4])
                    act.wait_ge(c["q4T_ps"], 8 * (b + 1) + 4 * t + r + 1)
                    nc.scalar.copy(q4T[:, pb, 4 * r:4 * r + 4, t * P:(t + 1) * P], bank.rearrange("p (k n) -> p k n", k=4)).then_inc(piece_read[k], 1)

            def exps(b, u):
                _, heads, tile = unit_of(u)
                act.wait_ge(c["mx"], UNITS * b + u + 1)
                w = P * (tile + 1)
                for n in range(len(heads)):
                    cols = sc[:, u % 4, n * w:(n + 1) * w]
                    ins = nc.scalar.activation(cols, cols, ACT.Exp, bias=mxs[:, u % 4, n:n + 1], scale=-1.0)
                ins.then_inc(c["P"], 1)

            def pt_read(b, u):
                act.wait_ge(c["PT_ps"], UNITS * b + u + 1)
                after(act, c["O"], UNITS * b + u - 2)
                nc.scalar.copy(pt[:, u % 3, :], ps[:, 2 + u % 2, :]).then_inc(PT_read[u % 2], 1)

            def copy_out(b, end):
                n = QUAD_ENDS.index(end)
                act.wait_ge(c["O"], UNITS * b + end + 1)
                after(act, c["n_ps"], 4 * b + n - 1)
                nc.scalar.copy(o_raw[:, n % 2, :], ps[:, 4 + n % 2, :]).then_inc(c["o_raw"], 1)

            def pass_c(b, pb, sides, units=UNITS):
                first = isinstance(b, int) and b == 0
                for u in range(UNITS):
                    if (units or u < 2) and (u >= 2 or not first) and u % 4 != 3:
                        pt_read(b, u - 2)
                    if units:
                        exps(b, u)
                    if units and u - 4 in QUAD_ENDS:
                        copy_out(b, u - 4)
                    if u == 3 and not first:
                        copy_out(b - 1, UNITS - 1)
                    if u - 1 in PIECES and piece_side(PIECES[u - 1]) in sides:
                        piece(PIECES[u - 1], b, pb)
                if piece_side(PIECES[UNITS - 1]) in sides:
                    piece(PIECES[UNITS - 1], b, pb)

            act.wait_ge(mlp[0]["acc"], TPC * CHUNKS * MLP_GROUPS)
            for name in ORDER:
                if piece_side(name) == "in":
                    piece(name, -1, 0)
            pass_c(0, 1, ("in", "own"))
            with act.Fori(0, BATCH // 2 - 1) as i:
                for half in range(2):
                    pass_c(2 * i + (1 + half), half, ("in", "own", "out"))
            pass_c(BATCH - 1, 0, ("own", "out"))
            pass_c(BATCH, 1, ("out",), 0)

            def prep(cc):
                for t in range(TPC):
                    g = TPC * cc + t
                    act.wait_ge(d["hT_ps"], g + 1)
                    nc.scalar.copy(feat[:, 0, :, g * P:(g + 1) * P], ps[:, 4 + t % 2, :].rearrange("p (k n) -> p k n", k=KB)).then_inc(d["hT_hi"], 1)
                act.wait_ge(d["shifted"], cc + 1)
                nc.scalar.activation(gl[:, 2, :, :], gl[:, 1, :, :], ACT.Exp).then_inc(d["ex"], 1)

            k, n = piece_turn("wo1", BATCH)
            act.wait_ge(piece_read[k], n + 1)
            step = mlp_act(act, mlp[1])
            prep(0)
            step(0, 0, True)
            for cc in range(1, CHUNKS):
                prep(cc)
                step(cc, cc, False)
            with act.Fori(0, EXPERTS // 2) as i:
                for r in range(2 * CHUNKS):
                    step(i * (2 * CHUNKS) + (CHUNKS + r), r % CHUNKS, False)

        def mlp_dve(dve, s_, scale_of):
            def hidden(s, j, ch):
                dve.wait_ge(s_["silu"], JB * s + j + 1)
                nc.vector.tensor_tensor(m_f[:, j, :], ps[:, 2 * j, :], sg[:, j, :], ALU.mult).then_inc(s_["m"], 1)

            def low(s, j, ch):
                dve.wait_ge(s_["hi"], JB * s + j + 1)
                nc.vector.tensor_tensor(m_s[:, ch % 2, 1, j, :], m_f[:, j, :], m_s[:, ch % 2, 0, j, :], ALU.subtract).then_inc(s_["lo"], 1)

            def sums_(s, t, tile, scale):
                dve.wait_ge(s_["down"], TPC * s + t + 1)
                if scale is None:
                    nc.vector.tensor_tensor(acc[:, tile, :], ps[:, 4 + t, :], acc[:, tile, :], ALU.add).then_inc(s_["acc"], 1)
                else:
                    nc.vector.scalar_tensor_tensor(out=acc[:, tile, :], in0=ps[:, 4 + t, :], scalar=scale, in1=acc[:, tile, :],
                                                   op0=ALU.mult, op1=ALU.add).then_inc(s_["acc"], 1)

            def head(s, ch):
                for j in range(JB):
                    hidden(s, j, ch)
                    low(s, j, ch)

            def steps(s0, groups, last, expert, ch0=0):
                for g in range(groups):
                    for ch in range(ch0, CHUNKS):
                        s = s0 + (g * CHUNKS + ch - ch0)
                        if not (last and g == groups - 1 and ch == CHUNKS - 1):
                            head(s + 1, (ch + 1) % CHUNKS)
                        if not (isinstance(s, int) and s < CHUNKS):
                            dve.wait_ge(s_["acc"], TPC * s + TPC - TPC * CHUNKS)
                        for t in range(TPC):
                            tile = ch * TPC + t
                            scale = None
                            if expert is not None:
                                e = expert + g
                                scale = comb[:, tile, e:e + 1] if isinstance(e, int) else comb[:, tile, bass.ds(e, 1)]
                            sums_(s, t, tile, scale)
            return head, steps

        @block.vector
        def _(dve):
            dve.wait_ge(raw_loaded[0], 16)
            ch0 = Chain(dve, a["dve"], 0)
            ch0.link(nc.vector.tensor_copy(wsplit[:, 0, 0, :], wraw[:, 0, :]))
            nc.vector.tensor_tensor(wsplit[:, 0, 1, :], wraw[:, 0, :], wsplit[:, 0, 0, :], ALU.subtract).then_inc(w_ready[0], 1)
            DVE0 = 1

            def accs(b, tt):
                return acc[:, 2 * b + tt, :] if isinstance(b, int) else acc[:, bass.ds(2 * b + tt, 1), :].rearrange("p o d -> p (o d)")

            def norm_stats(b, s_, ch):
                for t in range(TPB):
                    ch.mark(nc.vector.bn_stats(stats[:, t, :], accs(b, t)))
                hold(dve, ch.sem, ch.base + ch.n, dve_held)
                for t in range(TPB):
                    ins = nc.vector.bn_aggr(mv[:, t, :], stats[:, t, :])
                    ch.mark(ins)
                ch.wait(ch.n)
                dve.sem_inc(s_, 1)

            def norm_a(b, ch):
                norm_stats(b, a["stats"], ch)
                dve.wait_ge(a["rstd"], b + 1)

            def tile_a(b, tt, ch):
                t = 2 * b + tt
                first = isinstance(b, int) and b + tt == 0
                if not first:
                    dve.wait_ge(a["hT_ps"], t)
                nc.vector.tensor_scalar(ha[:, :], accs(b, tt), mv[:, tt, 0:1], ln[:, tt, 1:2], ALU.subtract, ALU.mult).then_inc(a["h"], 1)
                dve.wait_ge(a["h"], t + 1)
                nc.vector.tensor_scalar(accs(b, tt), accs(b, tt), ln[:, tt, 2:3], ln[:, tt, 3:4], ALU.mult, ALU.add).then_inc(a["acc"], 1)
                hb = 0 if tt == 0 else 7
                dve.wait_ge(a["hT_hi"], t + 1)
                nc.vector.tensor_tensor(hTa[:, 1, :, :].rearrange("p k n -> p (k n)"), ps[:, hb, :],
                                        hTa[:, 0, :, :].rearrange("p k n -> p (k n)"), ALU.subtract).then_inc(a["hT"], 1)
                dve.wait_ge(a["v"], t + 1)
                dve.wait_ge(a["w"], t + 1)
                if not first:
                    dve.wait_ge(a["split"], t)
                nc.vector.tensor_tensor(wv_f[:, :], ps[:, 3, :], w_k[:, :], ALU.mult).then_inc(a["wv"], 1)

            def scan_a(b, half):
                s = 2 * b + half
                dve.wait_ge(a["wce"], s + 1)
                if not (isinstance(b, int) and b == 0 and half == 0):
                    dve.wait_ge(a["yT"], s)
                nc.vector.scalar_tensor_tensor(out=den[:, :], in0=ps[:, 6, :], scalar=1.0, in1=wce[:, :], op0=ALU.add,
                                               op1=ALU.mult).then_inc(a["den"], 1)
                dve.wait_ge(a["den"], s + 1)
                nc.vector.reciprocal(den[:, :], den[:, :]).then_inc(rec_done, 1)
                dve.wait_ge(rec_done, s + 1)
                nc.vector.tensor_tensor(den[:, :], ps[:, 4, :], den[:, :], ALU.mult).then_inc(a["y"], 1)
                dve.wait_ge(a["yhi"], s + 1)
                cols = slice(b * SEQ, (b + 1) * SEQ) if isinstance(b, int) else bass.ds(b * SEQ, SEQ)
                nc.vector.tensor_tensor(feat[:, 1, 2 * half:2 * half + 2, cols], den[:, :].rearrange("p (k n) -> p k n", k=2),
                                        feat[:, 0, 2 * half:2 * half + 2, cols], ALU.subtract).then_inc(a["yT"], 1)

            rec_done = sem("a_rec")
            dve.wait_ge(x_first, 16)
            norm_a(0, Chain(dve, a["dve"], DVE0))
            tile_a(0, 0, None)
            tile_a(0, 1, None)
            dve.wait_ge(x_rest, 16)
            with dve.Fori(0, BATCH - 1) as b:
                norm_a(b + 1, Chain(dve, a["dve"], b * 4 + (DVE0 + 4)))
                scan_a(b, 0)
                scan_a(b, 1)
                tile_a(b + 1, 0, None)
                tile_a(b + 1, 1, None)
            scan_a(BATCH - 1, 0)
            scan_a(BATCH - 1, 1)
            dve.wait_ge(a["yT"], 2 * BATCH)
            dve.wait_ge(a["acc"], TILES)

            head, steps = mlp_dve(dve, mlp[0], None)
            head(0, 0)
            steps(0, 2, False, None)
            with dve.Fori(1, MLP_GROUPS // 2 - 1) as i:
                steps(i * (2 * CHUNKS), 2, False, None)
            steps((MLP_GROUPS // 2 - 1) * 2 * CHUNKS, 2, True, None)
            dve.wait_ge(mlp[0]["acc"], TPC * CHUNKS * MLP_GROUPS)

            nc.vector.memset(v32[:, :, :, :, HD:2 * HD], 0.0).then_inc(c["ones"], 1)
            dve.wait_ge(c["ones"], 1)
            nc.vector.memset(v32[:, :, :, :, HD:HD + 1], 1.0).then_inc(c["ones"], 1)
            dve.wait_ge(consts, 5)
            dve.wait_ge(w_ready[0], SLOT_X // 2 + 1)
            dve.wait_ge(w_ready[1], SLOT_X // 2 + 1)
            dve.wait_ge(c["ones"], 2)

            def masks(b, pb):
                dve.wait_ge(c["mask_i"], 16 * b + 16)
                nc.vector.tensor_scalar(pad[:, :], msk_i[:, :], 0.0, MASKED, ALU.is_equal, ALU.mult).then_inc(c["pad"], 1)
                dve.wait_ge(c["pad"], b + 1)
                nc.vector.tensor_tensor(msk[:, pb, 0, :], pad[:, 0:P], causal[:, P:SEQ], ALU.add)
                nc.vector.tensor_tensor(msk[:, pb, 1:3, :].rearrange("p a n -> p (a n)"), pad[:, :],
                                        causal[:, :], ALU.add).then_inc(c["mask"], 1)

            def norm_c(b, t):
                nc.vector.bn_stats(stats[:, t, :], accs(b, t)).then_inc(c["dve"], 1)
                hold(dve, c["dve"], 4 * b + 2 * t + 1, dve_held)
                nc.vector.bn_aggr(mv[:, t, :], stats[:, t, :]).then_inc(c["dve"], 1)
                dve.wait_ge(c["dve"], 4 * b + 2 * t + 2)
                if t == TPB - 1:
                    dve.sem_inc(c["stats"], 1)

            def h_c(b, t):
                dve.wait_ge(c["rstd"], b + 1)
                after(dve, c["hT_ps"], 2 * b + t)
                nc.vector.tensor_scalar(hc[:, :], accs(b, t), mv[:, t, 0:1], ln[:, t, 0:1], ALU.subtract, ALU.mult).then_inc(c["h"], 1)

            def piece(name, b, pb):
                k, n = piece_turn(name, b)
                bank = ps[:, 6 + k, :]
                if name == "kv":
                    dve.wait_ge(c["kv_ps"], b + 2)
                    kv_in = bank.rearrange("p (t n) -> p t n", t=TPB)
                    for t in range(TPB):
                        k_in = kv_in[:, t, 0:P].rearrange("p (g o d) -> p g o d", g=KVG, o=1).broadcast_to([P, KVG, 2, HD])
                        ins = nc.vector.tensor_copy(k4[:, t, :, 0:2, :].bitcast(F32R), k_in)
                    ins.then_inc(c["kv_hi"], 1)
                    after(dve, c["O"], UNITS * b)
                    for t in range(TPB):
                        nc.vector.tensor_copy(v32[:, 1 - pb, t, :, 0:HD], kv_in[:, t, P:SEQ].rearrange("p (g d) -> p g d", g=KVG))
                    dve.wait_ge(c["kv_hi"], b + 2)
                    for t in range(TPB):
                        k_in = kv_in[:, t, 0:P].rearrange("p (g o d) -> p g o d", g=KVG, o=1).broadcast_to([P, KVG, 2, HD])
                        ins = nc.vector.tensor_tensor(k4[:, t, :, 2:4, :].bitcast(F32R), k_in, k4[:, t, :, 0:2, :], ALU.subtract)
                    ins.then_inc(piece_read[k], 1)
                elif name[:2] in ("hT", "oT"):
                    t = int(name[2])
                    tile, which, i = (hTc, "hT", b + 1) if name[0] == "h" else (oT, "oT", b - 1)
                    hi, lo = (tile[:, t, part, :, :].rearrange("p k n -> p (k n)") for part in range(2))
                    dve.wait_ge(c[which + "_ps"], 2 * i + t + 1)
                    nc.vector.tensor_copy(hi, bank).then_inc(c[which + "_hi"], 1)
                    dve.wait_ge(c[which + "_hi"], 2 * i + t + 1)
                    nc.vector.tensor_tensor(lo, bank, hi, ALU.subtract).then_inc(piece_read[k], 1)
                elif name in ("q0", "q1"):
                    t = int(name[1])
                    dve.wait_ge(c["q_ps"], 2 * (b + 1) + t + 1)
                    after(dve, c["q4T_ps"], 8 * (b + 1) + 4 * t)
                    q_in = bank.rearrange("p (h d) -> p h d", h=HEADS)
                    nc.vector.tensor_copy(q4[:, :, 0, :].bitcast(F32R), q_in).then_inc(c["q_hi"], 1)
                    dve.wait_ge(c["q_hi"], 2 * (b + 1) + t + 1)
                    nc.vector.tensor_tensor(q4[:, :, 1, :].bitcast(F32R), q_in, q4[:, :, 0, :], ALU.subtract).then_inc(piece_read[k], 1)
                elif name[0] == "n":
                    quad, t = int(name[1]), int(name[2])
                    n = 4 * (b - quad) + 2 * quad + t
                    dve.wait_ge(c["n_ps"], n + 1)
                    o32 = bank.rearrange("p (i j d) -> p i j d", i=4, j=4)
                    r = rden[:, :].rearrange("p (i j o) -> p i j o", i=4, j=4)
                    nc.vector.reciprocal(r, o32[:, :, :, HD:HD + 1]).then_inc(c["rden"], 1)
                    dve.wait_ge(c["rden"], n + 1)
                    dst = o_tok[(pb + quad) % 2][:, t, quad * SEQ:(quad + 1) * SEQ].rearrange("p (j i d) -> p i j d", i=4, j=4)
                    nc.vector.tensor_tensor(dst, o32[:, :, :, 0:HD], r.broadcast_to([P, 4, 4, HD]), ALU.mult).then_inc(piece_read[k], 1)
                elif name[:2] == "wo":
                    t = int(name[2])
                    dve.wait_ge(c["wo_ps"], 2 * (b - 1) + t + 1)
                    nc.vector.tensor_tensor(accs(b - 1, t), bank, accs(b - 1, t), ALU.add).then_inc(piece_read[k], 1)

            def maxes(b, u, pb):
                _, heads, tile = unit_of(u)
                hold(dve, c["S"], UNITS * b + u + 1, dve_held)
                if not (isinstance(b, int) and b == 0 and u < 4):
                    hold(dve, c["PT_ps"], UNITS * b + u - 3, dve_held)
                w = P * (tile + 1)
                m_in = msk[:, pb, 0, :] if tile == 0 else msk[:, pb, 1:3, :].rearrange("p a n -> p (a n)")
                for n in range(len(heads)):
                    ins = nc.vector.tensor_tensor_reduce(sc[:, u % 4, n * w:(n + 1) * w], ps[:, u % 2, n * w:(n + 1) * w], m_in, -0.25, 3e38,
                                                         ALU.add, ALU.min, mxs[:, u % 4, n:n + 1])
                ins.then_inc(c["mx"], 1)

            def pt_read(b, u):
                dve.wait_ge(c["PT_ps"], UNITS * b + u + 1)
                after(dve, c["O"], UNITS * b + u - 2)
                nc.vector.tensor_copy(pt[:, u % 3, :], ps[:, 2 + u % 2, :]).then_inc(PT_read[u % 2], 1)

            def pass_c(b, pb, sides, units=UNITS):
                first = isinstance(b, int) and b == 0
                for u in range(UNITS):
                    if "in" in sides:
                        if u < TPB:
                            norm_c(b + 1, u)
                        if u == 9:
                            masks(b + 1, 1 - pb)
                        if u == 2:
                            h_c(b + 1, 0)
                        if u == 4:
                            h_c(b + 1, 1)
                    if units:
                        maxes(b, u, pb)
                    if (units or u < 2) and (u >= 2 or not first) and u % 4 == 3:
                        pt_read(b, u - 2)
                    if u - 1 in PIECES and piece_side(PIECES[u - 1]) in sides:
                        piece(PIECES[u - 1], b, pb)

            norm_c(0, 0)
            norm_c(0, 1)
            masks(0, 0)
            for name in ORDER:
                if piece_side(name) == "in":
                    if name[:2] == "hT":
                        h_c(0, int(name[2]))
                    piece(name, -1, 1)
            pass_c(0, 0, ("in", "own"))
            with dve.Fori(0, BATCH // 2 - 1) as i:
                for half in range(2):
                    pass_c(2 * i + (1 + half), (1 + half) % 2, ("in", "own", "out"))
            pass_c(BATCH - 1, 1, ("own", "out"))
            pass_c(BATCH, 0, ("out",), 0)
            k, n = piece_turn("wo1", BATCH)
            dve.wait_ge(piece_read[k], n + 1)

            dve.wait_ge(d["iota"], 1)
            chd = Chain(dve, d["dve"])

            def prep(cc):
                tiles = [TPC * cc + t for t in range(TPC)]
                for t, g in enumerate(tiles):
                    chd.mark(nc.vector.bn_stats(stats_d[:, t, :], acc[:, g, :]))
                chd.wait(chd.n)
                for t in range(TPC):
                    chd.mark(nc.vector.bn_aggr(mv_d[:, t, :], stats_d[:, t, :]))
                chd.wait(chd.n)
                dve.sem_inc(d["stats"], 1)
                dve.wait_ge(d["rstd"], cc + 1)
                after(dve, d["hT_ps"], TPC * cc)
                for t, g in enumerate(tiles):
                    nc.vector.tensor_scalar(hd[:, t, :], acc[:, g, :], mv_d[:, t, 0:1], ln_d[:, t, 1:2], ALU.subtract, ALU.mult).then_inc(d["h"], 1)
                for t, g in enumerate(tiles):
                    dve.wait_ge(d["hT_hi"], g + 1)
                    cols = slice(g * P, (g + 1) * P)
                    nc.vector.tensor_tensor(feat[:, 1, :, cols], ps[:, 4 + t % 2, :].rearrange("p (k n) -> p k n", k=KB), feat[:, 0, :, cols],
                                            ALU.subtract).then_inc(d["hT"], 1)
                dve.wait_ge(d["logit"], cc + 1)
                chd.link(nc.vector.tensor_copy(gl[:, 0, :, :].rearrange("p t e -> p (t e)"), ps[:, 6, 0:TPC * EXPERTS]))
                dve.sem_inc(d["copied"], 1)
                chd.link(nc.vector.tensor_reduce(gs[:, 0, :], gl[:, 0, :, :], AX.X, ALU.max))

                def per_tile(x):
                    return x.rearrange("p (t o) -> p t o", o=1).broadcast_to([P, TPC, EXPERTS])

                nc.vector.tensor_tensor(gl[:, 1, :, :], gl[:, 0, :, :], per_tile(gs[:, 0, :]), ALU.subtract).then_inc(d["shifted"], 1)
                dve.wait_ge(d["ex"], cc + 1)
                chd.link(nc.vector.tensor_reduce(gs[:, 1, :], gl[:, 2, :, :], AX.X, ALU.add))
                chd.link(nc.vector.reciprocal(gs[:, 2, :], gs[:, 1, :]))
                chd.link(nc.vector.tensor_tensor(gl[:, 3, :, :], gl[:, 2, :, :], per_tile(gs[:, 2, :]), ALU.mult))
                for t in range(TPC):
                    chd.mark(nc.vector.max(gl[:, 4, t, :], gl[:, 3, t, :]))
                chd.wait(chd.n)
                for t in range(TPC):
                    chd.mark(nc.vector.max_index(gi[:, t, :], gl[:, 4, t, :], gl[:, 3, t, :]))
                chd.wait(chd.n)
                chd.link(nc.vector.tensor_copy(gl[:, 5, :, :], gi[:, :, :]))
                iota = iota8[:, :].rearrange("p (o e) -> p o e", o=1).broadcast_to([P, TPC, EXPERTS])
                for j in range(2):
                    chd.mark(nc.vector.tensor_tensor(gl[:, 6 + j, :, :], iota, gl[:, 5, :, j:j + 1].broadcast_to([P, TPC, EXPERTS]), ALU.is_equal))
                chd.wait(chd.n)
                for j in range(2):
                    chd.mark(nc.vector.tensor_tensor(gl[:, 6 + j, :, :], gl[:, 6 + j, :, :],
                                                     gl[:, 4, :, j:j + 1].broadcast_to([P, TPC, EXPERTS]), ALU.mult))
                chd.wait(chd.n)
                chd.link(nc.vector.tensor_tensor(comb[:, TPC * cc:TPC * cc + TPC, :], gl[:, 6, :, :], gl[:, 7, :, :], ALU.add))

            head, steps = mlp_dve(dve, mlp[1], comb)
            prep(0)
            head(0, 0)
            prep(1)
            for cc in range(1, CHUNKS):
                head(cc, cc)
                for t in range(TPC):
                    tile = (cc - 1) * TPC + t
                    dve.wait_ge(mlp[1]["down"], TPC * (cc - 1) + t + 1)
                    nc.vector.tensor_tensor(acc[:, tile, :], ps[:, 4 + t, :], acc[:, tile, :], ALU.add).then_inc(mlp[1]["acc"], 1)
                if cc + 1 < CHUNKS:
                    prep(cc + 1)
            steps(CHUNKS - 1, 1, False, None, CHUNKS - 1)
            with dve.Fori(0, EXPERTS // 2 - 1) as i:
                steps(i * (2 * CHUNKS) + CHUNKS, 2, False, 2 * i)
            i = EXPERTS // 2 - 1
            steps(i * 2 * CHUNKS + CHUNKS, 2, True, 2 * i)


def blocks(w_t):
    k, n = w_t.shape
    return w_t.reshape(k // P, P, n).transpose(1, 0, 2).reshape(P, k // P * n)


def group_slot(up, gate, down):
    import numpy as np

    cols = []
    for w in (up, gate):
        t = w.T.reshape(KB, P, JB, P)
        cols.append(t.transpose(1, 2, 0, 3).reshape(P, JB * KB * P))
    cols.append(blocks(down.T))
    return np.concatenate(cols, axis=1)


def kernel(**inputs):
    import numpy as np
    import concourse.bacc as bacc
    from concourse.bass_utils import run_bass_kernel_spmd

    f = {k: np.asarray(v) for k, v in inputs.items()}
    qkv = f["L0_attn_w_qkv"]
    a_w = np.concatenate([blocks(qkv[i * D:(i + 1) * D].T) for i in range(3)], axis=1)
    slots = [a_w[:, :SLOT], a_w[:, SLOT:]]
    sw, wo = f["L0_attn_w_swiglu"], f["L0_attn_w_out"]
    for g in range(MLP_GROUPS):
        u = slice(g * GROUP, (g + 1) * GROUP)
        slots.append(group_slot(sw[:DFF][u], sw[DFF:][u], wo[:, u]))
    order = [(2 * p + half) * (HEADS // KVG) + i for p in range(PAIRS) for i in range(HEADS // KVG) for half in range(2)]
    rows = np.concatenate([np.arange(h * HD, (h + 1) * HD) for h in order])
    kv = np.concatenate([f["L0_xattn_w_k"], f["L0_xattn_w_v"]])
    slots.append(np.concatenate([blocks(f["L0_xattn_w_q"][rows].T), blocks(kv.T)], axis=1))
    o_slot = np.zeros((P, SLOT), np.float32)
    o_slot[:, :KB * D] = blocks(f["L0_xattn_w_o"].T)
    o_slot[:, KB * D:KB * (D + EXPERTS)] = blocks(f["L0_ffn_gate_w"].T)
    o_slot[0, KB * (D + EXPERTS):KB * (D + EXPERTS) + D] = f["L0_xattn_b_o"]
    slots.append(o_slot)
    slots.append(group_slot(f["L0_ffn_ws3"], f["L0_ffn_ws1"], f["L0_ffn_ws2"]))
    for e in range(EXPERTS):
        slots.append(group_slot(f["L0_ffn_w3"][e], f["L0_ffn_w1"][e], f["L0_ffn_w2"][e]))
    arrays = {
        "x": np.ascontiguousarray(f["x"].reshape(BATCH * SEQ, D)),
        "weights": np.ascontiguousarray(np.stack(slots)),
        "ctx_t": np.ascontiguousarray(f["ctx_2048"].reshape(BATCH, SEQ, KB, P).transpose(0, 3, 2, 1)),
        "mask": np.ascontiguousarray(f["mask_BxS2_if1"]),
    }
    nc = bacc.Bacc("TRN2", target_bir_lowering=False, num_devices=1)
    args = [nc.dram_tensor(n, v.shape, mybir.dt.from_np(v.dtype), kind="ExternalInput").ap() for n, v in arrays.items()]
    out = nc.dram_tensor("out", (BATCH * SEQ, D), F32, kind="ExternalOutput").ap()
    decoder_layer(nc, *args, out)
    r = run_bass_kernel_spmd(nc, [arrays], core_ids=[0])
    return r.results[0]["out"].reshape(BATCH, SEQ, D)
```

```python
from contextlib import ExitStack

import concourse.bass as bass
from concourse import mybir
from concourse.alu_op_type import AluOpType as ALU

ACT = mybir.ActivationFunctionType
AX = mybir.AxisListType
F32 = mybir.dt.float32
F32R = mybir.dt.float32r
U32 = mybir.dt.uint32
I32 = mybir.dt.int32

P = 128
D = 512
KB = D // P
BATCH, SEQ = 8, 256
TPB = SEQ // P
TILES = BATCH * TPB
DFF = 2048
GROUP = 256
JB = GROUP // P
MLP_GROUPS = DFF // GROUP
EXPERTS = 8
CHUNK = 512
CHUNKS = BATCH * SEQ // CHUNK
TPC = CHUNK // P
PIECE_A = 1024
SLOT = (2 * JB * KB + JB * KB) * P
HEADS, KVG, HD = 32, 8, 16
PAIRS = KVG // 2
PT_PLACES = 6
UNITS = 3 * KVG
LN_EPS = 1e-5
RMS_EPS = 1.1920929e-07
MASKED = -1e37

SLOT_QKV, SLOT_MLP, SLOT_X = 0, 2, 2 + MLP_GROUPS
SLOT_O = SLOT_X + 1
SLOT_MOE = SLOT_X + 2
SLOTS = SLOT_MOE + 1 + EXPERTS


def after(eng, sem, value):
    if not (isinstance(value, int) and value <= 0):
        eng.wait_ge(sem, value)


PIECES = {0: "n10", 2: "kv", 3: "hT0", 4: "k4T0", 5: "hT1", 6: "k4T1", 7: "n11", 8: "q0",
          9: "n00", 10: "oT0", 11: "oT1", 12: "q4T00", 13: "q4T01", 14: "q4T02", 15: "q4T03", 16: "q1",
          17: "wo0", 18: "n01", 19: "q4T10", 20: "q4T11", 21: "wo1", 22: "q4T12", 23: "q4T13"}


def piece_side(name):
    if name[0] == "n":
        return "own" if name[1] == "0" else "out"
    return "out" if name[:2] in ("oT", "wo") else "in"


ORDER = list(PIECES.values())
PIECE_BANKS = 2
IN_BANK = [len(ORDER[k::PIECE_BANKS]) for k in range(PIECE_BANKS)]


def piece_turn(name, b):
    at = ORDER.index(name)
    return at % PIECE_BANKS, IN_BANK[at % PIECE_BANKS] * (b + 1) + at // PIECE_BANKS


def place_a(b_parity, tt):
    return b_parity if tt == 0 else 2


def unit_of(u):
    quad, r = divmod(u, UNITS // 2)
    part, j = divmod(r, 4)
    return 4 * quad + j, range(4) if part == 0 else range(2 * part - 2, 2 * part), int(part > 0)


QUAD_ENDS = (3, 11, 15, 23)


def hold(eng, sem, value, settled):
    eng.wait_ge(sem, value)
    eng.sem_inc(settled, 1)


class Chain:

    def __init__(self, eng, sem, base=0, per=None, settled=None):
        self.eng, self.sem, self.base, self.n, self.per, self.settled = eng, sem, base, 0, per, settled

    def mark(self, ins):
        self.n += 1
        ins.then_inc(self.sem, 1)
        return self.n

    def wait(self, n):
        self.eng.wait_ge(self.sem, self.base + n)
        if self.settled is not None:
            self.eng.sem_inc(self.settled, 1)

    def link(self, ins):
        self.wait(self.mark(ins))

    def done(self):
        assert self.per is None or self.n == self.per, (self.n, self.per)


def decoder_layer(nc: bass.Bass, x, weights, ctx_t, mask, out):
    with ExitStack() as es:
        start = (nc.sbuf_base + 63) // 64 * 64
        place = [start]

        def at(name, shape, dt, off=None):
            size = 4
            for n in shape[1:]:
                size *= n
            if off is None:
                off = place[0]
                place[0] += (size + 31) // 32 * 32
            assert off + size <= nc.sbuf_usable_end, (name, off + size)
            return nc.alloc_sbuf_tensor_at(name, shape, dt, offset=off)

        acc = at("acc", [P, TILES, D], F32)
        feat_at = place[0]
        feat = at("feat", [P, 2, KB, BATCH * SEQ], F32R)
        wsplit = at("wsplit", [P, 2, 2, SLOT], F32R)
        raw0_at = place[0]
        wraw = at("wraw", [P, 2, SLOT], F32)
        raw1_at = raw0_at + 4 * SLOT
        ident = at("ident", [P, P], F32)
        tri = at("tri", [P, 2 * P], F32R)
        causal = at("causal", [P, SEQ], F32)
        half_neg = at("half_neg", [P, 4], F32)
        stats_d = at("stats_d", [P, TPC, 6], F32)
        mv_d = at("mv_d", [P, TPC, 2], F32)
        ln_d = at("ln_d", [P, TPC, 2], F32)
        iota8 = at("iota8", [P, EXPERTS], F32)
        comb = at("comb", [P, TILES, EXPERTS], F32)
        stats = at("stats", [P, TPB, 6], F32)
        mv = at("mv", [P, TPB, 2], F32)
        ln = at("ln", [P, TPB, 8], F32)
        rq = at("rq", [P, 8], F32)
        sums = at("sums", [P, 4], F32)
        temp_at = place[0]

        def region(first):
            place[0] = first

        hTa = at("hTa", [P, 2, 2, KB, P], F32R)
        wv_s = at("wv_s", [P, 3, 2, 2, D], F32R)
        wce = at("wce", [P, 2 * SEQ], F32)
        tri_f = at("tri_f", [P, 2 * P], F32, off=place[0])
        den = at("den", [P, 2 * SEQ], F32)
        region(feat_at)
        qkv_raw = at("qkv_raw", [P, 2 * SLOT], F32)
        region(raw1_at)
        ha = at("ha", [P, D], F32)
        e_q = at("e_q", [P, 3, D], F32)
        w_k = at("w_k", [P, D], F32)
        wv_f = at("wv_f", [P, D], F32)
        region(temp_at)
        m_s = at("m_s", [P, 2, 2, JB, CHUNK], F32R)
        m_f = at("m_f", [P, JB, CHUNK], F32)
        sg = at("sg", [P, JB, CHUNK], F32)
        hd = at("hd", [P, TPC, D], F32)
        gl = at("gl", [P, 8, TPC, EXPERTS], F32)
        gs = at("gs", [P, 4, TPC], F32)
        gi = at("gi", [P, TPC, EXPERTS], U32)
        router_w = at("router_w", [P, KB, 2, EXPERTS], F32R)
        logits_f = at("logits_f", [2 * EXPERTS, CHUNK], F32)
        region(temp_at)
        q4 = at("q4", [P, HEADS, 4, HD], F32)
        v32 = at("v32", [P, 2, TPB, KVG, 2 * HD], F32)
        msk = at("msk", [P, 2, 3, P], F32)
        sc = at("sc", [P, 4, 512], F32)
        pt = at("pt", [P, PT_PLACES, 512], F32)
        mxs = at("mxs", [P, 4, 4], F32)
        rden = at("rden", [P, 16], F32)
        region(raw0_at)
        ctx_raw = at("ctx_raw", [P, KB, SEQ], F32)
        hc = at("hc", [P, D], F32)
        msk_i = at("msk_i", [P, SEQ], I32)
        pad = at("pad", [P, SEQ], F32)
        k4 = at("k4", [P, TPB, KVG, 4, HD], F32)
        assert place[0] <= raw1_at
        region(raw1_at)
        o_tok0 = at("o_tok0", [P, TPB, D], F32)
        o_tok1 = at("o_tok1", [P, TPB, D], F32)
        o_raw = at("o_raw", [P, 2, 512], F32)
        assert place[0] <= raw1_at + 4 * SLOT
        o_tok = [o_tok0, o_tok1]
        region(feat_at)
        q4T = at("q4T", [P, 2, HEADS // 2, SEQ], F32R)
        k4T = at("k4T", [P, 2, PAIRS, SEQ], F32R)
        ctx_s = at("ctx_s", [P, 2, KB, SEQ], F32R)
        hTc = at("hTc", [P, TPB, 2, KB, P], F32R)
        oT = at("oT", [P, TPB, 2, KB, P], F32R)
        assert place[0] <= feat_at + 65536

        ps = es.enter_context(nc.psum_tensor("ps", [P, 8, 512], F32))

        names = set()

        def sem(name):
            assert name not in names
            names.add(name)
            return es.enter_context(nc.semaphore(name))

        raw_loaded = [sem(f"raw_loaded{p}") for p in range(2)]
        w_ready = [sem(f"w_ready{p}") for p in range(2)]
        w_free = [sem(f"w_free{p}") for p in range(2)]
        pool_self = sem("pool_self")
        pool_held = sem("pool_held")
        dve_held = sem("dve_held")
        consts = sem("consts")
        piece_loaded = [sem(f"a_piece_loaded{n}") for n in range(2 * SLOT // PIECE_A)]
        x_first = sem("x_first")
        x_rest = sem("x_rest")

        def signals(prefix, **meanings):
            return {name: sem(prefix + name) for name in meanings}

        a = signals(
            "a_", stats="batches whose mean and variance are made", rstd="batches whose scales are made",
            h="tiles normalised", acc="tiles with x + LN(x) in the residual", hT_ps="tiles of h transposed in PSUM",
            hT_hi="their hi in SBUF", hT="their lo too", q="tiles with q in PSUM", k="k in PSUM", v="v in PSUM",
            ssq="sums of squares, q's and k's in turn", rms="their scales", e="tiles of exp(-q)", w="tiles of exp(k)",
            w_hi="tiles of its hi", wv="tiles of w * v", wv_hi="tiles of its hi", split="tiles with w and w * v split",
            w_hi_piece="pieces of w_qkv with hi", w_piece="pieces split", w2_hi="the first MLP slot's hi",
            w_sum="running sums of w, half batches", scan="those of w * v and exp(-q)^T too", wce="w's sums plus 1e-6",
            den="denominators", rec="their reciprocals", y="outputs, half batches", yhi="their hi in feat", yT="their lo too",
            pool="GpSimd's own small steps", dve="the vector engine's")
        c = signals(
            "c_", wo_hi="the output weights' hi", ctx_hi="the first context's hi", ones="v's columns of ones and zeros",
            ctx="contexts loaded, by 16", ctx_s="contexts split", mask_i="masks loaded, by 16", pad="masks of padding",
            mask="masks made", stats="batches whose mean and variance are made", rstd="batches whose scales are made",
            h="tiles normalised", hT_ps="tiles of h transposed in PSUM", hT_hi="their hi", kv_ps="batches with k | v in PSUM",
            kv_hi="their k's hi", k4T_ps="tiles of split k transposed in PSUM", q_ps="tiles of q in PSUM", q_hi="their hi",
            q4="tiles of q split and doubled", q4T_ps="quarter tiles of q4 transposed in PSUM",
            oT_ps="tiles of o transposed in PSUM", oT_hi="their hi", wo_ps="tiles of the output projection in PSUM",
            S="units with scores in PSUM", mx="units with masked scores and their maximum", P="units of probabilities",
            PT_ps="units transposed in PSUM", PT="units transposed in SBUF", O="fours of units summed over v",
            o_raw="quads' tiles copied out", n_ps="quads' tiles transposed back", rden="their reciprocal row sums",
            pool="GpSimd's own small steps", dve="the vector engine's")
        piece_read = [sem(f"c_piece_read{k}") for k in range(PIECE_BANKS)]
        d = signals(
            "d_", iota="0..7 on every partition", stats="chunks whose mean and variance are made",
            rstd="chunks whose scales are made", h="tiles normalised", hT_ps="tiles of h transposed in PSUM",
            hT_hi="their hi in feat", hT="their lo too", router="the router's weights copied",
            logit="chunks of logits in PSUM, by expert", logits_f="the same in SBUF", logit_ps="transposed in PSUM",
            copied="read", shifted="chunks of logits minus their maximum", ex="their exponentials",
            pool="GpSimd's own small steps", dve="the vector engine's")
        mlp = [signals(
            f"mlp{i}_", up="up and gate in PSUM", silu="silu(gate)", m="silu(gate) * up", hi="its hi", lo="its lo",
            down="sums in PSUM", acc="sums added to the residual") for i in range(2)]
        stored = sem("stored")

        block = es.enter_context(nc.Block())

        def slot_block(p, part, at_, n):
            return wsplit[:, p, part, at_:at_ + n]

        @block.sync
        def _(sp):
            x_v = x.rearrange("(t p) d -> p t d", p=P)
            out_v = out.rearrange("(t p) d -> p t d", p=P)
            sp.dma_start(acc[:, 0:TPB, :], x_v[:, 0:TPB, :]).then_inc(x_first, 16)
            for n in range(2 * SLOT // PIECE_A):
                s, at_ = divmod(n * PIECE_A, SLOT)
                sp.dma_start(qkv_raw[:, n * PIECE_A:(n + 1) * PIECE_A], weights[s, :, at_:at_ + PIECE_A]).then_inc(piece_loaded[n], 16)
            sp.dma_start(acc[:, TPB:TILES, :], x_v[:, TPB:TILES, :]).then_inc(x_rest, 16)
            sp.dma_start(wraw[:, 0, :], weights[2]).then_inc(raw_loaded[0], 16)
            sp.wait_ge(a["split"], TILES)
            sp.wait_ge(a["scan"], 2 * BATCH)
            sp.dma_start(wraw[:, 1, :], weights[3]).then_inc(raw_loaded[1], 16)
            with sp.Fori(2, SLOT_X // 2) as n:
                for p in range(2):
                    sp.wait_ge(w_ready[p], n)
                    sp.dma_start(wraw[:, p, :], weights[bass.ds(2 * n + p, 1)].rearrange("s p n -> (s p) n")).then_inc(raw_loaded[p], 16)
            n = SLOT_X // 2
            for p in range(2):
                sp.wait_ge(w_ready[p], n)
                sp.dma_start(wraw[:, p, :], weights[2 * n + p]).then_inc(raw_loaded[p], 16)

            sp.wait_ge(w_ready[0], SLOT_X // 2 + 1)
            for b in range(BATCH):
                after(sp, c["ctx_s"], b)
                sp.dma_start(ctx_raw[:, :, :], ctx_t[b]).then_inc(c["ctx"], 16)
                after(sp, c["mask"], b)
                sp.dma_start(msk_i[:, :], mask[b:b + 1].broadcast_to([P, SEQ])).then_inc(c["mask_i"], 16)
            sp.wait_ge(c["ctx_s"], BATCH)
            sp.wait_ge(c["mask"], BATCH)
            k, n = piece_turn("k4T1", BATCH - 2)
            sp.wait_ge(piece_read[k], n + 1)
            sp.dma_start(wraw[:, 0, :], weights[SLOT_MOE]).then_inc(raw_loaded[0], 16)
            k, n = piece_turn("oT1", BATCH)
            sp.wait_ge(piece_read[k], n + 1)
            sp.dma_start(wraw[:, 1, :], weights[SLOT_MOE + 1]).then_inc(raw_loaded[1], 16)
            with sp.Fori(SLOT_MOE // 2 + 1, SLOTS // 2) as n:
                for p in range(2):
                    sp.wait_ge(w_ready[p], n)
                    sp.dma_start(wraw[:, p, :], weights[bass.ds(2 * n + p, 1)].rearrange("s p n -> (s p) n")).then_inc(raw_loaded[p], 16)
            sp.wait_ge(w_ready[0], SLOTS // 2)
            sp.dma_start(wraw[:, 0, :], weights[SLOTS - 1]).then_inc(raw_loaded[0], 16)
            total = 4 * CHUNKS * (1 + EXPERTS)
            for ch in range(CHUNKS):
                sp.wait_ge(mlp[1]["acc"], total - 4 * (CHUNKS - 1 - ch))
                t = slice(ch * TPC, (ch + 1) * TPC)
                sp.dma_start(out_v[:, t, :], acc[:, t, :]).then_inc(stored, 16)
            sp.wait_ge(stored, 16 * CHUNKS)

        @block.gpsimd
        def _(pool):
            nc.gpsimd.memset(half_neg[:, :], -0.5).then_inc(consts, 1)
            nc.gpsimd.memset(tri_f[:, :], 1.0).then_inc(pool_self, 1)
            nc.gpsimd.memset(ident[:, :], 0.0).then_inc(pool_self, 1)
            nc.gpsimd.memset(causal[:, :], 0.0).then_inc(pool_self, 1)
            pool.wait_ge(pool_self, 3)
            nc.gpsimd.affine_select(out=ident[:, :], in_=ident[:, :], compare_op=ALU.not_equal, fill=1.0,
                                    base=0, pattern=[[-1, P]], channel_multiplier=1).then_inc(consts, 1)
            nc.gpsimd.affine_select(out=tri_f[:, 0:P], in_=tri_f[:, 0:P], compare_op=ALU.is_ge, fill=0.0,
                                    base=0, pattern=[[1, P]], channel_multiplier=-1).then_inc(pool_self, 1)
            nc.gpsimd.affine_select(out=causal[:, P:SEQ], in_=causal[:, P:SEQ], compare_op=ALU.is_ge, fill=MASKED,
                                    base=0, pattern=[[-1, P]], channel_multiplier=1).then_inc(consts, 1)
            nc.gpsimd.iota(iota8[:, :], pattern=[[1, EXPERTS]], base=0, channel_multiplier=0,
                           allow_small_or_imprecise_dtypes=True).then_inc(d["iota"], 1)
            pool.wait_ge(pool_self, 4)
            nc.gpsimd.tensor_copy(tri[:, :], tri_f[:, :]).then_inc(consts, 1)

            split_self = sem("split_self")

            def split(p, n, base):
                hold(pool, raw_loaded[p], 16 * n, pool_held)
                if not isinstance(n, int) or n >= 1:
                    hold(pool, w_free[p], n, pool_held)
                nc.gpsimd.tensor_copy(wsplit[:, p, 0, :], wraw[:, p, :]).then_inc(split_self, 1)
                hold(pool, split_self, base + 1, pool_held)
                nc.gpsimd.tensor_tensor(out=wsplit[:, p, 1, :], in0=wraw[:, p, :], in1=wsplit[:, p, 0, :],
                                        op=ALU.subtract).then_inc(w_ready[p], 1)

            NORM_OPS, RMS_OPS = 10, 5
            PER_A = NORM_OPS + TPB * RMS_OPS

            def rstd_a(b, ch):
                hold(pool, a["stats"], b + 1, pool_held)
                m, v = mv[:, :, 0:1], mv[:, :, 1:2]
                L = [ln[:, :, i:i + 1] for i in range(8)]
                minus_half = half_neg[:, 0:TPB].rearrange("p (t o) -> p t o", o=1)

                def scaled(out_, in_, mul, add):
                    ch.mark(nc.gpsimd.tensor_scalar(out_, in_, mul, add, ALU.mult, ALU.add))

                def both(out_, in0, in1, op):
                    ch.mark(nc.gpsimd.tensor_tensor(out=out_, in0=in0, in1=in1, op=op))

                scaled(L[4], v, 1.0, LN_EPS)
                ch.wait(ch.n)
                both(L[0], L[4], minus_half, ALU.pow)
                ch.wait(ch.n)
                both(L[5], v, L[0], ALU.mult)
                both(L[7], m, L[0], ALU.mult)
                scaled(L[2], L[0], 1.0, 1.0)
                ch.wait(ch.n)
                both(L[5], L[5], L[0], ALU.mult)
                scaled(L[3], L[7], -1.0, 0.0)
                ch.wait(ch.n)
                scaled(L[5], L[5], 1.0, RMS_EPS)
                ch.wait(ch.n)
                both(L[6], L[5], minus_half, ALU.pow)
                ch.wait(ch.n)
                both(L[1], L[6], L[0], ALU.mult)
                ch.wait(ch.n)
                pool.sem_inc(a["rstd"], 1)

            def rms(t, i, ch):
                hold(pool, a["ssq"], 2 * t + i + 1, pool_held)
                ch.link(nc.gpsimd.tensor_scalar(rq[:, 2 + i:3 + i], sums[:, i:i + 1], 1.0 / D, RMS_EPS, ALU.mult, ALU.add))
                ch.link(nc.gpsimd.tensor_tensor(out=rq[:, i + 4 * (1 - i):i + 4 * (1 - i) + 1], in0=rq[:, 2 + i:3 + i], in1=half_neg[:, 0:1], op=ALU.pow))
                if i == 0:
                    ch.link(nc.gpsimd.tensor_scalar(rq[:, 0:1], rq[:, 4:5], -1.0, 0.0, ALU.mult, ALU.add))
                pool.sem_inc(a["rms"], 1)

            def batch_a(b, pb, last):
                ch = Chain(pool, a["pool"], b * PER_A + NORM_OPS, None, pool_held)
                for tt in range(TPB):
                    t = 2 * b + tt
                    rms(t, 0, ch)
                    if tt == 0 and not last:
                        rstd_a(b + 1, ch)
                    rms(t, 1, ch)
                    at_ = place_a(pb, tt)
                    hold(pool, a["w_hi"], t + 1, pool_held)
                    nc.gpsimd.tensor_tensor(out=wv_s[:, at_, 0, 1, :], in0=w_k[:, :], in1=wv_s[:, at_, 0, 0, :], op=ALU.subtract)
                    hold(pool, a["wv_hi"], t + 1, pool_held)
                    nc.gpsimd.tensor_tensor(out=wv_s[:, at_, 1, 1, :], in0=wv_f[:, :], in1=wv_s[:, at_, 1, 0, :],
                                            op=ALU.subtract).then_inc(a["split"], 1)
                if not last:
                    assert ch.n == PER_A, ch.n

            rstd_a(0, Chain(pool, a["pool"], 0, None, pool_held))
            batch_a(0, 0, False)
            with pool.Fori(0, BATCH // 2 - 1) as i:
                for r in range(2):
                    batch_a(2 * i + (1 + r), (1 + r) % 2, False)
            batch_a(BATCH - 1, (BATCH - 1) % 2, True)

            pool.wait_ge(a["w2_hi"], 1)
            nc.gpsimd.tensor_tensor(out=wsplit[:, 0, 1, :], in0=wraw[:, 0, :], in1=wsplit[:, 0, 0, :],
                                    op=ALU.subtract).then_inc(w_ready[0], 1)
            with pool.Fori(0, SLOT_X // 2 - 1) as n:
                split(1, n + 1, 2 * n)
                split(0, n + 2, 2 * n + 1)
            base = 2 * (SLOT_X // 2 - 1)

            PER_C = 4 + 2 + 2

            def ctx_split(b, ch):
                hold(pool, c["ctx"], 16 * b + 16, pool_held)
                if not isinstance(b, int) or b >= 1:
                    hold(pool, c["kv_ps"], b, pool_held)
                ch.link(nc.gpsimd.tensor_copy(ctx_s[:, 0, :, :], ctx_raw[:, :, :]))
                ch.link(nc.gpsimd.tensor_tensor(out=ctx_s[:, 1, :, :], in0=ctx_raw[:, :, :], in1=ctx_s[:, 0, :, :], op=ALU.subtract))
                pool.sem_inc(c["ctx_s"], 1)

            def batch_c(b, last):
                first = isinstance(b, int) and b == 0
                ch = Chain(pool, c["pool"], 0 if first else (b - 1) * PER_C + (PER_C - 2), PER_C, pool_held)
                hold(pool, c["stats"], b + 1, pool_held)
                for t in range(TPB):
                    ch.link(nc.gpsimd.tensor_scalar(ln[:, t, 4:5], mv[:, t, 1:2], 1.0, LN_EPS, ALU.mult, ALU.add))
                    ch.link(nc.gpsimd.tensor_tensor(out=ln[:, t, 0:1], in0=ln[:, t, 4:5], in1=half_neg[:, 0:1], op=ALU.pow))
                pool.sem_inc(c["rstd"], 1)
                if not last:
                    ctx_split(b + 1, ch)
                for t in range(0 if first else TPB):
                    k, n = piece_turn(f"q{t}", b - 1)
                    hold(pool, piece_read[k], n + 1, pool_held)
                    ch.link(nc.gpsimd.tensor_copy(q4[:, :, 2:4, :], q4[:, :, 0:2, :]))
                    pool.sem_inc(c["q4"], 1)
                if not last and not first:
                    ch.done()

            batch_c(0, False)
            with pool.Fori(1, BATCH - 1) as b:
                batch_c(b, False)
            batch_c(BATCH - 1, True)

            split(0, SLOT_MOE // 2, base)
            ch = Chain(pool, d["pool"])
            for cc in range(CHUNKS):
                pool.wait_ge(d["stats"], cc + 1)
                ch.link(nc.gpsimd.tensor_scalar(ln_d[:, :, 0:1], mv_d[:, :, 1:2], 1.0, LN_EPS, ALU.mult, ALU.add))
                ch.link(nc.gpsimd.tensor_tensor(out=ln_d[:, :, 1:2], in0=ln_d[:, :, 0:1],
                                                in1=half_neg[:, 0:TPC].rearrange("p (t o) -> p t o", o=1), op=ALU.pow))
                pool.sem_inc(d["rstd"], 1)
            split(1, SLOT_MOE // 2, base + 1)
            with pool.Fori(0, SLOTS // 2 - SLOT_MOE // 2 - 1) as n:
                split(0, n + (SLOT_MOE // 2 + 1), 2 * n + base + 2)
                split(1, n + (SLOT_MOE // 2 + 1), 2 * n + base + 3)
            split(0, SLOTS // 2, base + 2 + 2 * (SLOTS // 2 - SLOT_MOE // 2 - 1))

        def three(pe, out_, w_hi, w_lo, m_hi, m_lo, first, last):
            nc.tensor.matmul(out_, w_hi, m_hi, start=first, stop=False)
            nc.tensor.matmul(out_, w_lo, m_hi, start=False, stop=False)
            return nc.tensor.matmul(out_, w_hi, m_lo, start=False, stop=last)

        def mlp_pe(pe, s_):
            def up(s, par, ch, first_of_group, wait_n, static0, between=None):
                if first_of_group:
                    pe.wait_ge(w_ready[par], wait_n)
                for j in range(JB):
                    if not static0:
                        pe.wait_ge(s_["m"], JB * s + j - 1)
                    for kind in range(2):
                        for k in range(KB):
                            o = ((kind * JB + j) * KB + k) * P
                            mm = three(pe, ps[:, 2 * j + kind, :], slot_block(par, 0, o, P), slot_block(par, 1, o, P),
                                       feat[:, 0, k, ch * CHUNK:(ch + 1) * CHUNK], feat[:, 1, k, ch * CHUNK:(ch + 1) * CHUNK],
                                       k == 0, k == KB - 1)
                    mm.then_inc(s_["up"], 1)
                    if j == 0 and between:
                        between()

            def down(s, par, ch, static0):
                sp_ = ch % 2
                pe.wait_ge(s_["lo"], JB * s + JB)
                for t in range(TPC):
                    if not static0:
                        pe.wait_ge(s_["acc"], TPC * s + t - 3)
                    for j in range(JB):
                        o = 2 * JB * KB * P + j * D
                        mm = three(pe, ps[:, 4 + t, :], m_s[:, sp_, 0, j, t * P:(t + 1) * P], m_s[:, sp_, 1, j, t * P:(t + 1) * P],
                                   slot_block(par, 0, o, D), slot_block(par, 1, o, D), j == 0, j == JB - 1)
                    mm.then_inc(s_["down"], 1)

            return up, down

        @block.tensor
        def _(pe):
            pe.wait_ge(consts, 4)

            def transposes(b, tt):
                pe.wait_ge(a["h"], 2 * b + tt + 1)
                for k in range(KB):
                    tr = nc.tensor.transpose(ps[:, 7 * tt, k * P:(k + 1) * P], ha[:, k * P:(k + 1) * P], ident[:, :])
                tr.then_inc(a["hT_ps"], 1)

            def project(b, tt, i):
                t = 2 * b + tt
                name, freed = (("q", "e"), ("k", "w_hi"), ("v", "wv"))[i]
                if i == 0:
                    pe.wait_ge(a["hT"], t + 1)
                after(pe, a[freed], t)
                for k in range(KB):
                    col = (i * KB + k) * D
                    p, o = col // SLOT, col % SLOT
                    if isinstance(b, int) and t == 0:
                        pe.wait_ge(a["w_piece"], col // PIECE_A + 1)
                    mm = three(pe, ps[:, 1 + i, :], hTa[:, tt, 0, k, :], hTa[:, tt, 1, k, :],
                               slot_block(p, 0, o, D), slot_block(p, 1, o, D), k == 0, k == KB - 1)
                mm.then_inc(a[name], 1)

            def scan(b, pb, half):
                s = 2 * b + half
                if half == 0:
                    pe.wait_ge(a["split"], 2 * b + 2)
                    pe.wait_ge(a["e"], 2 * b + 2)
                else:
                    pe.wait_ge(a["y"], s)
                at0, at1 = place_a(pb, 0), place_a(pb, 1)
                for bank, kind in ((5, 0), (4, 1)):
                    for i in range(2):
                        blk = slice((2 * half + i) * P, (2 * half + i + 1) * P)
                        o = ps[:, bank, i * SEQ:(i + 1) * SEQ]
                        nc.tensor.matmul(o, wv_s[:, at0, kind, 0, blk], tri[:, :], start=True, stop=False)
                        nc.tensor.matmul(o, wv_s[:, at0, kind, 1, blk], tri[:, :], start=False, stop=False)
                        o1 = ps[:, bank, i * SEQ + P:(i + 1) * SEQ]
                        nc.tensor.matmul(o1, wv_s[:, at1, kind, 0, blk], tri[:, 0:P], start=False, stop=False)
                        mm = nc.tensor.matmul(o1, wv_s[:, at1, kind, 1, blk], tri[:, 0:P], start=False, stop=True)
                    if kind == 0:
                        mm.then_inc(a["w_sum"], 1)
                for i in range(2):
                    blk = slice((2 * half + i) * P, (2 * half + i + 1) * P)
                    for tt in range(TPB):
                        tr = nc.tensor.transpose(ps[:, 6, i * SEQ + tt * P:i * SEQ + (tt + 1) * P], e_q[:, place_a(pb, tt), blk], ident[:, :])
                tr.then_inc(a["scan"], 1)

            def batch_a(b, pb, first, last):
                project(b, 0, 0)
                project(b, 0, 1)
                transposes(b, 1)
                if not first:
                    scan(b - 1, 1 - pb, 0)
                project(b, 0, 2)
                project(b, 1, 0)
                if not last:
                    transposes(b + 1, 0)
                if not first:
                    scan(b - 1, 1 - pb, 1)
                project(b, 1, 1)
                if last:
                    pe.wait_ge(a["k"], TILES)
                    pe.sem_inc(w_free[0], 1)
                project(b, 1, 2)
                if last:
                    pe.wait_ge(a["v"], TILES)
                    pe.sem_inc(w_free[1], 1)

            transposes(0, 0)
            batch_a(0, 0, True, False)
            with pe.Fori(0, BATCH // 2 - 1) as i:
                for r in range(2):
                    batch_a(2 * i + (1 + r), (1 + r) % 2, False, False)
            batch_a(BATCH - 1, (BATCH - 1) % 2, False, True)
            scan(BATCH - 1, (BATCH - 1) % 2, 0)

            def run_mlp(s_):
                up, down = mlp_pe(pe, s_)

                def steps(s0, count, slot_half, par_first, last, ch0=0):
                    for g in range(count):
                        par = (par_first + g) % 2
                        for ch in range(ch0, CHUNKS):
                            s = s0 + (g * CHUNKS + ch - ch0)
                            final = last and g == count - 1 and ch == CHUNKS - 1
                            if not final:
                                nch = (ch + 1) % CHUNKS
                                npar = par if nch else 1 - par
                                turn = slot_half + ((par_first + g) // 2 if nch else (par_first + g + 1) // 2)
                                up(s + 1, npar, nch, nch == 0, turn + 1, False)
                            down(s, par, ch, isinstance(s, int) and s == 0)
                            if ch == CHUNKS - 1:
                                pe.wait_ge(s_["down"], TPC * s + TPC)
                                pe.sem_inc(w_free[par], 1)

                return up, down, steps

            def run_b():
                up, down, steps = run_mlp(mlp[0])
                pe.wait_ge(a["e"], TILES)
                pe.wait_ge(a["w_hi"], TILES)
                pe.wait_ge(a["wv"], TILES)
                pe.wait_ge(a["yT"], 4)
                up(0, 0, 0, True, SLOT_MLP // 2 + 1, True, lambda: scan(BATCH - 1, (BATCH - 1) % 2, 1))
                pe.wait_ge(a["yT"], 2 * BATCH)
                steps(0, 2, SLOT_MLP // 2, 0, False)
                with pe.Fori(1, MLP_GROUPS // 2 - 1) as i:
                    steps(i * (2 * CHUNKS), 2, i + SLOT_MLP // 2, 0, False)
                i = MLP_GROUPS // 2 - 1
                steps(i * 2 * CHUNKS, 2, i + SLOT_MLP // 2, 0, True)

            run_b()

            def piece(name, b, sides):
                k, n = piece_turn(name, b)
                after(pe, piece_read[k], n)
                if piece_side(name) not in sides:
                    pe.sem_inc(piece_read[k], 1)
                    return
                bank = ps[:, 6 + k, :]

                def ready(other):
                    ko, no = piece_turn(other, b)
                    pe.wait_ge(piece_read[ko], no + 1)

                tt = int(name[3] if name[:2] == "q4" or name[:2] == "k4" else name[-1]) if name != "kv" else 0
                if name == "kv":
                    pe.wait_ge(c["ctx_s"], b + 2)
                    for t in range(TPB):
                        for kb in range(KB):
                            o = KB * D + kb * 2 * P
                            mm = three(pe, bank[:, t * SEQ:(t + 1) * SEQ], ctx_s[:, 0, kb, t * P:(t + 1) * P],
                                       ctx_s[:, 1, kb, t * P:(t + 1) * P], slot_block(0, 0, o, 2 * P), slot_block(0, 1, o, 2 * P),
                                       kb == 0, kb == KB - 1)
                    mm.then_inc(c["kv_ps"], 1)
                elif name[:3] == "k4T":
                    tt = int(name[3])
                    ready("kv")
                    for p in range(PAIRS):
                        tr = nc.tensor.transpose(bank[:, p * P:(p + 1) * P], k4[:, tt, 2 * p:2 * p + 2, :, :].rearrange("t g r d -> t (g r d)"),
                                                 ident[:, :])
                    tr.then_inc(c["k4T_ps"], 1)
                elif name[:2] == "hT":
                    pe.wait_ge(c["h"], 2 * (b + 1) + tt + 1)
                    for kb in range(KB):
                        tr = nc.tensor.transpose(bank[:, kb * P:(kb + 1) * P], hc[:, kb * P:(kb + 1) * P], ident[:, :])
                    tr.then_inc(c["hT_ps"], 1)
                elif name[:3] == "q4T":
                    tt, r = int(name[3]), int(name[4])
                    pe.wait_ge(c["q4"], 2 * (b + 1) + tt + 1)
                    for i in range(4):
                        n = 4 * r + i
                        tr = nc.tensor.transpose(bank[:, i * P:(i + 1) * P], q4[:, 2 * n:2 * n + 2, :, :].rearrange("t h r d -> t (h r d)"),
                                                 ident[:, :])
                    tr.then_inc(c["q4T_ps"], 1)
                elif name[:1] == "q":
                    ready(f"hT{tt}")
                    for kb in range(KB):
                        mm = three(pe, bank, hTc[:, tt, 0, kb, :], hTc[:, tt, 1, kb, :],
                                   slot_block(0, 0, kb * D, D), slot_block(0, 1, kb * D, D), kb == 0, kb == KB - 1)
                    mm.then_inc(c["q_ps"], 1)
                elif name[0] == "n":
                    n = 4 * (b - int(name[1])) + 2 * int(name[1]) + tt
                    pe.wait_ge(c["o_raw"], n + 1)
                    for i in range(4):
                        tr = nc.tensor.transpose(bank[:, i * P:(i + 1) * P], o_raw[:, tt, i * P:(i + 1) * P], ident[:, :])
                    tr.then_inc(c["n_ps"], 1)
                elif name[:2] == "oT":
                    ready("n11")
                    for kb in range(KB):
                        tr = nc.tensor.transpose(bank[:, kb * P:(kb + 1) * P], o_tok[par(b, 1)][:, tt, kb * P:(kb + 1) * P], ident[:, :])
                    tr.then_inc(c["oT_ps"], 1)
                else:
                    ready(f"oT{tt}")
                    bo = KB * (D + EXPERTS)
                    nc.tensor.matmul(bank, tri[0:1, P:2 * P], wsplit[0:1, 1, 0, bo:bo + D], start=True, stop=False)
                    nc.tensor.matmul(bank, tri[0:1, P:2 * P], wsplit[0:1, 1, 1, bo:bo + D], start=False, stop=False)
                    for kb in range(KB):
                        mm = three(pe, bank, oT[:, tt, 0, kb, :], oT[:, tt, 1, kb, :],
                                   slot_block(1, 0, kb * D, D), slot_block(1, 1, kb * D, D), False, kb == KB - 1)
                    mm.then_inc(c["wo_ps"], 1)

            parity_now = [0]

            def par(b, back):
                return (parity_now[0] + back) % 2

            def scores(b, u):
                v, heads, tile = unit_of(u)
                after(pe, c["mx"], UNITS * b + u - 1)
                rows = slice(64 * (v % 2), 64 * (v % 2) + 64)
                w = P * (tile + 1)
                for n, i in enumerate(heads):
                    mm = nc.tensor.matmul(ps[:, u % 2, n * w:(n + 1) * w], q4T[rows, par(b, 0), 4 * (v // 2) + i, tile * P:(tile + 1) * P],
                                          k4T[rows, par(b, 0), v // 2, 0:w], start=True, stop=True)
                mm.then_inc(c["S"], 1)

            def probs_t(b, u):
                pe.wait_ge(c["P"], UNITS * b + u + 1)
                after(pe, c["PT"], UNITS * b + u - 1)
                for i in range(4):
                    tr = nc.tensor.transpose(ps[:, 2 + u % 2, i * P:(i + 1) * P], sc[:, u % 4, i * P:(i + 1) * P], ident[:, :])
                tr.then_inc(c["PT_ps"], 1)

            def attend(b, u, back):
                pe.wait_ge(c["PT"], UNITS * b + u + 4)
                if u % 12 in (0, 4):
                    ends = sum(u > e for e in QUAD_ENDS)
                    after(pe, c["o_raw"], 4 * b + ends - 1)
                _, heads, tile = unit_of(u)
                for m in range(tile + 1):
                    for j in range(4):
                        v = unit_of(u + j)[0]
                        p_in = pt[:, (u + j) % PT_PLACES, :].rearrange("p (n m t) -> p m n t", m=tile + 1, t=P)
                        mm = nc.tensor.matmul(ps[32 * j:32 * j + 32, 4 + tile, heads[0] * P:(heads[-1] + 1) * P],
                                              v32[:, par(b, back), m, v, :], p_in[:, m, :, :], start=(m == 0), stop=(m == tile))
                mm.then_inc(c["O"], 1)

            def pass_c(b, sides, units=UNITS):
                first = isinstance(b, int) and b == 0
                for u in range(UNITS):
                    if not units and u == 9:
                        hT_d(0)
                    if units:
                        for name in {0: ["q4T02", "q4T03"], 4: ["q4T12", "q4T13"]}.get(u, []):
                            k, n = piece_turn(name, b - 1)
                            pe.wait_ge(piece_read[k], n + 1)
                        scores(b, u)
                    if u in PIECES:
                        piece(PIECES[u], b, sides)
                    if units or u < 3:
                        if u >= 2 or not first:
                            if units or u < 2:
                                probs_t(b, u - 2)
                        if u == 2 and not first:
                            attend(b - 1, UNITS - 4, 1)
                        if u >= 6 and u % 4 == 2:
                            attend(b, u - 6, 0)

            def hT_d(cc):
                if cc:
                    pe.wait_ge(d["copied"], cc)
                after(pe, mlp[1]["acc"], TPC * (cc - 2))
                for t in range(TPC):
                    pe.wait_ge(d["h"], TPC * cc + t + 1)
                    for k in range(KB):
                        tr = nc.tensor.transpose(ps[:, t + 4 * (cc > 0), k * P:(k + 1) * P], hd[:, t, k * P:(k + 1) * P], ident[:, :])
                    tr.then_inc(d["hT_ps"], 1)

            pe.wait_ge(w_ready[0], SLOT_X // 2 + 1)
            pe.wait_ge(mlp[0]["acc"], TPC * CHUNKS * MLP_GROUPS)
            for name in ORDER:
                parity_now[0] = 1
                piece(name, -1, ("in",))
            parity_now[0] = 0
            pass_c(0, ("in", "own"))
            pe.wait_ge(w_ready[1], SLOT_X // 2 + 1)
            with pe.Fori(0, BATCH // 2 - 1) as i:
                for half in range(2):
                    parity_now[0] = (1 + half) % 2
                    pass_c(2 * i + (1 + half), ("in", "own", "out"))
            pe.sem_inc(w_free[0], 1)
            parity_now[0] = (BATCH - 1) % 2
            pass_c(BATCH - 1, ("own", "out"))
            parity_now[0] = BATCH % 2
            pass_c(BATCH, ("out",), 0)

            def logits(cc):
                pe.wait_ge(d["hT"], TPC * (cc + 1))
                for k in range(KB):
                    for part in range(2):
                        mm = nc.tensor.matmul(ps[0:2 * EXPERTS, 7, :], router_w[:, k, :, :].rearrange("p a e -> p (a e)"),
                                              feat[:, part, k, cc * CHUNK:(cc + 1) * CHUNK], start=(k + part == 0), stop=(k + part == KB))
                mm.then_inc(d["logit"], 1)

            def logits_t(cc):
                pe.wait_ge(d["logits_f"], cc + 1)
                after(pe, mlp[1]["acc"], TPC * (cc - 2) + 1)
                for t in range(TPC):
                    tr = nc.tensor.transpose(ps[:, 4, t * 2 * EXPERTS:(t + 1) * 2 * EXPERTS], logits_f[:, t * P:(t + 1) * P],
                                             ident[0:2 * EXPERTS, 0:2 * EXPERTS])
                tr.then_inc(d["logit_ps"], 1)

            k, n = piece_turn("wo1", BATCH)
            pe.wait_ge(piece_read[k], n + 1)
            pe.wait_ge(d["router"], 1)
            pe.sem_inc(w_free[1], 1)
            up, down, steps = run_mlp(mlp[1])
            logits(0)
            logits_t(0)
            for cc in range(CHUNKS):
                more = cc + 1 < CHUNKS
                up(cc, 0, cc, cc == 0, SLOT_MOE // 2 + 1, cc == 0, (lambda: hT_d(cc + 1)) if more else None)
                if more:
                    logits(cc + 1)
                if cc:
                    pe.wait_ge(d["logits_f"], min(cc + 2, CHUNKS))
                    pe.wait_ge(d["copied"], min(cc + 1, CHUNKS))
                    down(cc - 1, 0, cc - 1, cc == 1)
                if more:
                    logits_t(cc + 1)
            steps(CHUNKS - 1, 1, SLOT_MOE // 2, 0, False, CHUNKS - 1)
            with pe.Fori(0, EXPERTS // 2 - 1) as i:
                steps(i * (2 * CHUNKS) + CHUNKS, 2, i + SLOT_MOE // 2, 1, False)
            i = EXPERTS // 2 - 1
            steps(i * 2 * CHUNKS + CHUNKS, 2, i + SLOT_MOE // 2, 1, True)

        def mlp_act(act, s_):
            def act_step(s, ch, static0, js=range(JB)):
                for j in js:
                    act.wait_ge(s_["up"], JB * s + j + 1)
                    nc.scalar.activation(sg[:, j, :], ps[:, 2 * j + 1, :], ACT.Silu).then_inc(s_["silu"], 1)
                    act.wait_ge(s_["m"], JB * s + j + 1)
                    if not (isinstance(s, int) and s < 2):
                        act.wait_ge(s_["down"], TPC * s - TPC)
                    nc.scalar.copy(m_s[:, ch % 2, 0, j, :], m_f[:, j, :]).then_inc(s_["hi"], 1)
            return act_step

        @block.scalar
        def _(act):
            def hT_hi(b, tt):
                t = 2 * b + tt
                act.wait_ge(a["hT_ps"], t + 1)
                after(act, a["v"], t - 1)
                nc.scalar.copy(hTa[:, tt, 0, :, :], ps[:, 7 * tt, :]).then_inc(a["hT_hi"], 1)

            def squares(b, pb, tt, i, out_):
                t = 2 * b + tt
                act.wait_ge(a[("q", "k")[i]], t + 1)
                nc.scalar.activation(out_, ps[:, 1 + i, :], ACT.Square, accum_out=sums[:, i:i + 1]).then_inc(a["ssq"], 1)

            def exp_q(b, pb, tt, between=None):
                t = 2 * b + tt
                if tt == 1:
                    after(act, a["scan"], 2 * b)
                squares(b, pb, tt, 0, e_q[:, place_a(pb, tt), :])
                if between:
                    between()
                act.wait_ge(a["rms"], 2 * t + 1)
                nc.scalar.activation(e_q[:, place_a(pb, tt), :], ps[:, 1, :], ACT.Exp, scale=rq[:, 0:1]).then_inc(a["e"], 1)

            def exp_k(b, pb, tt, between=None):
                t = 2 * b + tt
                after(act, a["split"], t)
                squares(b, pb, tt, 1, w_k[:, :])
                if between:
                    between()
                act.wait_ge(a["rms"], 2 * t + 2)
                nc.scalar.activation(w_k[:, :], ps[:, 2, :], ACT.Exp, scale=rq[:, 1:2]).then_inc(a["w"], 1)
                act.wait_ge(a["w"], t + 1)
                nc.scalar.activation(wv_s[:, place_a(pb, tt), 0, 0, :], w_k[:, :], ACT.Copy).then_inc(a["w_hi"], 1)

            def wv_hi(b, pb, tt):
                act.wait_ge(a["wv"], 2 * b + tt + 1)
                nc.scalar.copy(wv_s[:, place_a(pb, tt), 1, 0, :], wv_f[:, :]).then_inc(a["wv_hi"], 1)

            def w_cum(b, half):
                s = 2 * b + half
                act.wait_ge(a["w_sum"], s + 1)
                nc.scalar.activation(wce[:, :], ps[:, 5, :], ACT.Copy, bias=1e-6).then_inc(a["wce"], 1)

            def y_hi(b, half):
                act.wait_ge(a["y"], 2 * b + half + 1)
                cols = slice(b * SEQ, (b + 1) * SEQ) if isinstance(b, int) else bass.ds(b * SEQ, SEQ)
                nc.scalar.copy(feat[:, 0, 2 * half:2 * half + 2, cols], den[:, :].rearrange("p (k n) -> p k n", k=2)).then_inc(a["yhi"], 1)

            def batch_a(b, pb, first, last):
                exp_q(b, pb, 0)
                hT_hi(b, 1)
                exp_k(b, pb, 0, None if first else lambda: w_cum(b - 1, 0))
                if not first:
                    y_hi(b - 1, 0)
                wv_hi(b, pb, 0)
                if not last:
                    hT_hi(b + 1, 0)
                exp_q(b, pb, 1, None if first else lambda: w_cum(b - 1, 1))
                exp_k(b, pb, 1)
                if not first:
                    y_hi(b - 1, 1)
                wv_hi(b, pb, 1)

            for n in range(2 * SLOT // PIECE_A):
                s, at_ = divmod(n * PIECE_A, SLOT)
                if n == 2:
                    hT_hi(0, 0)
                act.wait_ge(piece_loaded[n], 16)
                nc.scalar.copy(wsplit[:, s, 0, at_:at_ + PIECE_A], qkv_raw[:, n * PIECE_A:(n + 1) * PIECE_A]).then_inc(a["w_hi_piece"], 1)
            batch_a(0, 0, True, False)
            with act.Fori(0, BATCH // 2 - 1) as i:
                for r in range(2):
                    batch_a(2 * i + (1 + r), (1 + r) % 2, False, False)
            batch_a(BATCH - 1, (BATCH - 1) % 2, False, True)
            act.wait_ge(raw_loaded[0], 16)
            act.wait_ge(w_free[0], 1)
            nc.scalar.copy(wsplit[:, 0, 0, :], wraw[:, 0, :]).then_inc(a["w2_hi"], 1)
            for half in range(2):
                w_cum(BATCH - 1, half)
                y_hi(BATCH - 1, half)
            act.wait_ge(a["yT"], 2 * BATCH)

            step = mlp_act(act, mlp[0])
            for s in range(2 * CHUNKS):
                step(s, s % CHUNKS, s == 0)
            with act.Fori(1, MLP_GROUPS // 2) as i:
                for r in range(2 * CHUNKS):
                    step(i * (2 * CHUNKS) + r, r % CHUNKS, False)

            def piece(name, b, pb):
                k, n = piece_turn(name, b)
                bank = ps[:, 6 + k, :]
                if name[:3] == "k4T":
                    t = int(name[3])
                    act.wait_ge(c["k4T_ps"], 2 * (b + 1) + t + 1)
                    nc.scalar.copy(k4T[:, pb, :, t * P:(t + 1) * P], bank.rearrange("p (k n) -> p k n", k=PAIRS)).then_inc(piece_read[k], 1)
                elif name[:3] == "q4T":
                    t, r = int(name[3]), int(name[4])
                    act.wait_ge(c["q4T_ps"], 8 * (b + 1) + 4 * t + r + 1)
                    nc.scalar.copy(q4T[:, pb, 4 * r:4 * r + 4, t * P:(t + 1) * P], bank.rearrange("p (k n) -> p k n", k=4)).then_inc(piece_read[k], 1)

            def exps(b, u):
                _, heads, tile = unit_of(u)
                act.wait_ge(c["mx"], UNITS * b + u + 1)
                w = P * (tile + 1)
                for n in range(len(heads)):
                    cols = sc[:, u % 4, n * w:(n + 1) * w]
                    ins = nc.scalar.activation(cols, cols, ACT.Exp, bias=mxs[:, u % 4, n:n + 1], scale=-1.0)
                ins.then_inc(c["P"], 1)

            def pt_read(b, u):
                act.wait_ge(c["PT_ps"], UNITS * b + u + 1)
                after(act, c["O"], UNITS // 4 * b + (u - PT_PLACES) // 4 + 1)
                nc.scalar.copy(pt[:, u % PT_PLACES, :], ps[:, 2 + u % 2, :]).then_inc(c["PT"], 1)

            def copy_out(b, end):
                n = QUAD_ENDS.index(end)
                act.wait_ge(c["O"], UNITS // 4 * b + (end + 1) // 4)
                after(act, c["n_ps"], 4 * b + n - 1)
                nc.scalar.copy(o_raw[:, n % 2, :], ps[:, 4 + n % 2, :]).then_inc(c["o_raw"], 1)

            def pass_c(b, pb, sides, units=UNITS):
                first = isinstance(b, int) and b == 0
                for u in range(UNITS):
                    if u in PIECES and piece_side(PIECES[u]) in sides:
                        piece(PIECES[u], b, pb)
                    if (units or u < 2) and (u >= 2 or not first):
                        pt_read(b, u - 2)
                    if units and u - 4 in QUAD_ENDS:
                        copy_out(b, u - 4)
                    if u == 3 and not first:
                        copy_out(b - 1, UNITS - 1)
                    if units:
                        exps(b, u)

            act.wait_ge(mlp[0]["down"], TPC * CHUNKS * MLP_GROUPS)
            act.wait_ge(c["ctx"], 16)
            nc.scalar.copy(ctx_s[:, 0, :, :], ctx_raw[:, :, :]).then_inc(c["ctx_hi"], 1)
            act.wait_ge(raw_loaded[1], 16 * (SLOT_O // 2))
            act.wait_ge(w_free[1], SLOT_O // 2)
            nc.scalar.copy(wsplit[:, 1, 0, :], wraw[:, 1, :]).then_inc(c["wo_hi"], 1)
            for name in ORDER:
                if piece_side(name) == "in":
                    piece(name, -1, 0)
            act.wait_ge(w_ready[1], SLOT_X // 2 + 1)
            pass_c(0, 1, ("in", "own"))
            with act.Fori(0, BATCH // 2 - 1) as i:
                for half in range(2):
                    pass_c(2 * i + (1 + half), half, ("in", "own", "out"))
            pass_c(BATCH - 1, 0, ("own", "out"))
            pass_c(BATCH, 1, ("out",), 0)

            def hT_hi_d(cc):
                for t in range(TPC):
                    g = TPC * cc + t
                    act.wait_ge(d["hT_ps"], g + 1)
                    nc.scalar.copy(feat[:, 0, :, g * P:(g + 1) * P], ps[:, t + 4 * (cc > 0), :].rearrange("p (k n) -> p k n", k=KB)).then_inc(d["hT_hi"], 1)

            def logits_out(cc):
                act.wait_ge(d["logit"], cc + 1)
                after(act, d["logit_ps"], cc)
                nc.scalar.copy(logits_f[:, :], ps[0:2 * EXPERTS, 7, :]).then_inc(d["logits_f"], 1)

            def exps_d(cc):
                act.wait_ge(d["shifted"], cc + 1)
                nc.scalar.activation(gl[:, 2, :, :], gl[:, 1, :, :], ACT.Exp).then_inc(d["ex"], 1)

            step = mlp_act(act, mlp[1])
            hT_hi_d(0)
            logits_out(0)
            exps_d(0)
            for cc in range(CHUNKS):
                more = cc + 1 < CHUNKS
                step(cc, cc, cc == 0, [0])
                if more:
                    hT_hi_d(cc + 1)
                step(cc, cc, cc == 0, [1])
                if more:
                    logits_out(cc + 1)
                    exps_d(cc + 1)
            with act.Fori(0, EXPERTS // 2) as i:
                for r in range(2 * CHUNKS):
                    step(i * (2 * CHUNKS) + (CHUNKS + r), r % CHUNKS, False)

        def mlp_dve(dve, s_, scale_of):
            def hidden(s, j, ch):
                dve.wait_ge(s_["silu"], JB * s + j + 1)
                nc.vector.tensor_tensor(m_f[:, j, :], ps[:, 2 * j, :], sg[:, j, :], ALU.mult).then_inc(s_["m"], 1)

            def low(s, j, ch):
                dve.wait_ge(s_["hi"], JB * s + j + 1)
                nc.vector.tensor_tensor(m_s[:, ch % 2, 1, j, :], m_f[:, j, :], m_s[:, ch % 2, 0, j, :], ALU.subtract).then_inc(s_["lo"], 1)

            def sums_(s, t, tile, scale):
                dve.wait_ge(s_["down"], TPC * s + t + 1)
                if scale is None:
                    nc.vector.tensor_tensor(acc[:, tile, :], ps[:, 4 + t, :], acc[:, tile, :], ALU.add).then_inc(s_["acc"], 1)
                else:
                    nc.vector.scalar_tensor_tensor(out=acc[:, tile, :], in0=ps[:, 4 + t, :], scalar=scale, in1=acc[:, tile, :],
                                                   op0=ALU.mult, op1=ALU.add).then_inc(s_["acc"], 1)

            def head(s, ch, js=range(JB)):
                for j in js:
                    hidden(s, j, ch)
                    low(s, j, ch)

            def steps(s0, groups, last, expert, ch0=0, before_end=None):
                for g in range(groups):
                    for ch in range(ch0, CHUNKS):
                        s = s0 + (g * CHUNKS + ch - ch0)
                        if before_end and g == groups - 1 and ch == CHUNKS - 1:
                            before_end()
                        if not (last and g == groups - 1 and ch == CHUNKS - 1):
                            head(s + 1, (ch + 1) % CHUNKS)
                        if not (isinstance(s, int) and s < CHUNKS):
                            dve.wait_ge(s_["acc"], TPC * s + TPC - TPC * CHUNKS)
                        for t in range(TPC):
                            tile = ch * TPC + t
                            scale = None
                            if expert is not None:
                                e = expert + g
                                scale = comb[:, tile, e:e + 1] if isinstance(e, int) else comb[:, tile, bass.ds(e, 1)]
                            sums_(s, t, tile, scale)
            return head, steps

        @block.vector
        def _(dve):
            def accs(b, tt):
                return acc[:, 2 * b + tt, :] if isinstance(b, int) else acc[:, bass.ds(2 * b + tt, 1), :].rearrange("p o d -> p (o d)")

            def norm_stats(b, s_, ch):
                for t in range(TPB):
                    ch.mark(nc.vector.bn_stats(stats[:, t, :], accs(b, t)))
                hold(dve, ch.sem, ch.base + ch.n, dve_held)
                for t in range(TPB):
                    ins = nc.vector.bn_aggr(mv[:, t, :], stats[:, t, :])
                    ch.mark(ins)
                ch.wait(ch.n)
                dve.sem_inc(s_, 1)

            def h_a(b, tt):
                after(dve, a["hT_ps"], 2 * b + tt)
                dve.wait_ge(a["rstd"], b + 1)
                nc.vector.tensor_scalar(ha[:, :], accs(b, tt), mv[:, tt, 0:1], ln[:, tt, 1:2], ALU.subtract, ALU.mult).then_inc(a["h"], 1)

            def residual_a(b):
                dve.wait_ge(a["h"], 2 * b + TPB)
                for tt in range(TPB):
                    nc.vector.tensor_scalar(accs(b, tt), accs(b, tt), ln[:, tt, 2:3], ln[:, tt, 3:4], ALU.mult, ALU.add).then_inc(a["acc"], 1)

            def hT_lo(b, tt):
                dve.wait_ge(a["hT_hi"], 2 * b + tt + 1)
                hi, lo = (hTa[:, tt, part, :, :].rearrange("p k n -> p (k n)") for part in range(2))
                nc.vector.tensor_tensor(lo, ps[:, 7 * tt, :], hi, ALU.subtract).then_inc(a["hT"], 1)

            def w_times_v(b, tt):
                t = 2 * b + tt
                dve.wait_ge(a["v"], t + 1)
                dve.wait_ge(a["w"], t + 1)
                after(dve, a["split"], t)
                nc.vector.tensor_tensor(wv_f[:, :], ps[:, 3, :], w_k[:, :], ALU.mult).then_inc(a["wv"], 1)

            def y_a(b, half):
                s = 2 * b + half
                dve.wait_ge(a["scan"], s + 1)
                dve.wait_ge(a["wce"], s + 1)
                if half == 1:
                    dve.wait_ge(a["yT"], s)
                nc.vector.scalar_tensor_tensor(out=den[:, :], in0=ps[:, 6, :], scalar=1.0, in1=wce[:, :], op0=ALU.add,
                                               op1=ALU.mult).then_inc(a["den"], 1)
                dve.wait_ge(a["den"], s + 1)
                nc.vector.reciprocal(den[:, :], den[:, :]).then_inc(a["rec"], 1)
                dve.wait_ge(a["rec"], s + 1)
                nc.vector.tensor_tensor(den[:, :], ps[:, 4, :], den[:, :], ALU.mult).then_inc(a["y"], 1)

            def y_lo(b, half):
                dve.wait_ge(a["yhi"], 2 * b + half + 1)
                cols = slice(b * SEQ, (b + 1) * SEQ) if isinstance(b, int) else bass.ds(b * SEQ, SEQ)
                nc.vector.tensor_tensor(feat[:, 1, 2 * half:2 * half + 2, cols], den[:, :].rearrange("p (k n) -> p k n", k=2),
                                        feat[:, 0, 2 * half:2 * half + 2, cols], ALU.subtract).then_inc(a["yT"], 1)

            def batch_a(b, first, last):
                residual_a(b)
                if not last:
                    norm_stats(b + 1, a["stats"], Chain(dve, a["dve"], 4 * b + 4))
                hT_lo(b, 1)
                if not first:
                    y_a(b - 1, 0)
                if not last:
                    h_a(b + 1, 0)
                w_times_v(b, 0)
                if not last:
                    hT_lo(b + 1, 0)
                if not first:
                    y_lo(b - 1, 0)
                if not last:
                    h_a(b + 1, 1)
                if not first:
                    y_a(b - 1, 1)
                w_times_v(b, 1)
                if not first:
                    y_lo(b - 1, 1)
                    dve.wait_ge(a["yT"], 2 * b)

            dve.wait_ge(x_first, 16)
            norm_stats(0, a["stats"], Chain(dve, a["dve"], 0))
            for n in range(2 * SLOT // PIECE_A):
                s, at_ = divmod(n * PIECE_A, SLOT)
                if n == 1:
                    h_a(0, 0)
                if n == 2:
                    hT_lo(0, 0)
                    h_a(0, 1)
                dve.wait_ge(a["w_hi_piece"], n + 1)
                nc.vector.tensor_tensor(wsplit[:, s, 1, at_:at_ + PIECE_A], qkv_raw[:, n * PIECE_A:(n + 1) * PIECE_A],
                                        wsplit[:, s, 0, at_:at_ + PIECE_A], ALU.subtract).then_inc(a["w_piece"], 1)
            dve.wait_ge(a["w_piece"], 2 * SLOT // PIECE_A)
            dve.sem_inc(w_ready[0], 1)
            dve.sem_inc(w_ready[1], 1)
            dve.wait_ge(x_rest, 16)
            batch_a(0, True, False)
            with dve.Fori(0, BATCH // 2 - 1) as i:
                for r in range(2):
                    batch_a(2 * i + (1 + r), False, False)
            batch_a(BATCH - 1, False, True)
            for half in range(2):
                y_a(BATCH - 1, half)
                y_lo(BATCH - 1, half)

            def norm_c(b, t):
                nc.vector.bn_stats(stats[:, t, :], accs(b, t)).then_inc(c["dve"], 1)
                hold(dve, c["dve"], 4 * b + 2 * t + 1, dve_held)
                nc.vector.bn_aggr(mv[:, t, :], stats[:, t, :]).then_inc(c["dve"], 1)
                dve.wait_ge(c["dve"], 4 * b + 2 * t + 2)
                if t == TPB - 1:
                    dve.sem_inc(c["stats"], 1)

            def h_c(b, t):
                dve.wait_ge(c["rstd"], b + 1)
                after(dve, c["hT_ps"], 2 * b + t)
                nc.vector.tensor_scalar(hc[:, :], accs(b, t), mv[:, t, 0:1], ln[:, t, 0:1], ALU.subtract, ALU.mult).then_inc(c["h"], 1)

            def first_norm():
                dve.wait_ge(mlp[0]["acc"], TPC * CHUNKS * (MLP_GROUPS - 1) + TPB)
                dve.wait_ge(w_ready[0], SLOT_X // 2 + 1)
                norm_c(0, 0)
                norm_c(0, 1)

            head, steps = mlp_dve(dve, mlp[0], None)
            head(0, 0)
            steps(0, 2, False, None)
            with dve.Fori(1, MLP_GROUPS // 2 - 1) as i:
                steps(i * (2 * CHUNKS), 2, False, None)
            steps((MLP_GROUPS // 2 - 1) * 2 * CHUNKS, 2, True, None, before_end=first_norm)
            h_c(0, 0)
            dve.wait_ge(mlp[0]["acc"], TPC * CHUNKS * MLP_GROUPS)

            dve.wait_ge(c["ctx_hi"], 1)
            nc.vector.tensor_tensor(ctx_s[:, 1, :, :], ctx_raw[:, :, :], ctx_s[:, 0, :, :], ALU.subtract).then_inc(c["ctx_s"], 1)
            nc.vector.memset(v32[:, :, :, :, HD:2 * HD], 0.0).then_inc(c["ones"], 1)
            dve.wait_ge(c["ones"], 1)
            nc.vector.memset(v32[:, :, :, :, HD:HD + 1], 1.0).then_inc(c["ones"], 1)
            dve.wait_ge(c["ones"], 2)

            def masks(b, pb):
                dve.wait_ge(c["mask_i"], 16 * b + 16)
                nc.vector.tensor_scalar(pad[:, :], msk_i[:, :], 0.0, MASKED, ALU.is_equal, ALU.mult).then_inc(c["pad"], 1)
                dve.wait_ge(c["pad"], b + 1)
                nc.vector.tensor_tensor(msk[:, pb, 0, :], pad[:, 0:P], causal[:, P:SEQ], ALU.add)
                nc.vector.tensor_tensor(msk[:, pb, 1:3, :].rearrange("p a n -> p (a n)"), pad[:, :],
                                        causal[:, :], ALU.add).then_inc(c["mask"], 1)

            def piece(name, b, pb):
                k, n = piece_turn(name, b)
                bank = ps[:, 6 + k, :]
                if name == "kv":
                    dve.wait_ge(c["kv_ps"], b + 2)
                    kv_in = bank.rearrange("p (t n) -> p t n", t=TPB)
                    for t in range(TPB):
                        k_in = kv_in[:, t, 0:P].rearrange("p (g o d) -> p g o d", g=KVG, o=1).broadcast_to([P, KVG, 2, HD])
                        ins = nc.vector.tensor_copy(k4[:, t, :, 0:2, :].bitcast(F32R), k_in)
                    ins.then_inc(c["kv_hi"], 1)
                    after(dve, c["O"], UNITS // 4 * b)
                    for t in range(TPB):
                        nc.vector.tensor_copy(v32[:, 1 - pb, t, :, 0:HD], kv_in[:, t, P:SEQ].rearrange("p (g d) -> p g d", g=KVG))
                    dve.wait_ge(c["kv_hi"], b + 2)
                    for t in range(TPB):
                        k_in = kv_in[:, t, 0:P].rearrange("p (g o d) -> p g o d", g=KVG, o=1).broadcast_to([P, KVG, 2, HD])
                        ins = nc.vector.tensor_tensor(k4[:, t, :, 2:4, :].bitcast(F32R), k_in, k4[:, t, :, 0:2, :], ALU.subtract)
                    ins.then_inc(piece_read[k], 1)
                elif name[:2] in ("hT", "oT"):
                    t = int(name[2])
                    tile, which, i = (hTc, "hT", b + 1) if name[0] == "h" else (oT, "oT", b - 1)
                    hi, lo = (tile[:, t, part, :, :].rearrange("p k n -> p (k n)") for part in range(2))
                    dve.wait_ge(c[which + "_ps"], 2 * i + t + 1)
                    nc.vector.tensor_copy(hi, bank).then_inc(c[which + "_hi"], 1)
                    dve.wait_ge(c[which + "_hi"], 2 * i + t + 1)
                    nc.vector.tensor_tensor(lo, bank, hi, ALU.subtract).then_inc(piece_read[k], 1)
                elif name in ("q0", "q1"):
                    t = int(name[1])
                    dve.wait_ge(c["q_ps"], 2 * (b + 1) + t + 1)
                    after(dve, c["q4T_ps"], 8 * (b + 1) + 4 * t)
                    q_in = bank.rearrange("p (h d) -> p h d", h=HEADS)
                    nc.vector.tensor_copy(q4[:, :, 0, :].bitcast(F32R), q_in).then_inc(c["q_hi"], 1)
                    dve.wait_ge(c["q_hi"], 2 * (b + 1) + t + 1)
                    nc.vector.tensor_tensor(q4[:, :, 1, :].bitcast(F32R), q_in, q4[:, :, 0, :], ALU.subtract).then_inc(piece_read[k], 1)
                    if isinstance(b, int) and b == -1:
                        dve.wait_ge(piece_read[k], n + 1)
                        nc.vector.tensor_copy(q4[:, :, 2:4, :], q4[:, :, 0:2, :]).then_inc(c["q4"], 1)
                elif name[0] == "n":
                    quad, t = int(name[1]), int(name[2])
                    n = 4 * (b - quad) + 2 * quad + t
                    dve.wait_ge(c["n_ps"], n + 1)
                    o32 = bank.rearrange("p (i j d) -> p i j d", i=4, j=4)
                    r = rden[:, :].rearrange("p (i j o) -> p i j o", i=4, j=4)
                    nc.vector.reciprocal(r, o32[:, :, :, HD:HD + 1]).then_inc(c["rden"], 1)
                    dve.wait_ge(c["rden"], n + 1)
                    dst = o_tok[(pb + quad) % 2][:, t, quad * SEQ:(quad + 1) * SEQ].rearrange("p (j i d) -> p i j d", i=4, j=4)
                    nc.vector.tensor_tensor(dst, o32[:, :, :, 0:HD], r.broadcast_to([P, 4, 4, HD]), ALU.mult).then_inc(piece_read[k], 1)
                elif name[:2] == "wo":
                    t = int(name[2])
                    dve.wait_ge(c["wo_ps"], 2 * (b - 1) + t + 1)
                    nc.vector.tensor_tensor(accs(b - 1, t), bank, accs(b - 1, t), ALU.add).then_inc(piece_read[k], 1)

            def maxes(b, u, pb):
                _, heads, tile = unit_of(u)
                hold(dve, c["S"], UNITS * b + u + 1, dve_held)
                if not (isinstance(b, int) and b == 0 and u < 4):
                    hold(dve, c["PT_ps"], UNITS * b + u - 3, dve_held)
                w = P * (tile + 1)
                m_in = msk[:, pb, 0, :] if tile == 0 else msk[:, pb, 1:3, :].rearrange("p a n -> p (a n)")
                for n in range(len(heads)):
                    ins = nc.vector.tensor_tensor_reduce(sc[:, u % 4, n * w:(n + 1) * w], ps[:, u % 2, n * w:(n + 1) * w], m_in, -0.25, 3e38,
                                                         ALU.add, ALU.min, mxs[:, u % 4, n:n + 1])
                ins.then_inc(c["mx"], 1)

            def pass_c(b, pb, sides, units=UNITS):
                first = isinstance(b, int) and b == 0
                for u in range(UNITS):
                    if not units and u == 4:
                        dve.wait_ge(c["O"], UNITS // 4 * BATCH)
                        h_d(0)
                        for part in range(2):
                            ins = nc.vector.tensor_copy(router_w[:, :, part, :], wsplit[:, 1, part, KB * D:KB * (D + EXPERTS)].rearrange("p (k e) -> p k e", k=KB))
                        ins.then_inc(d["router"], 1)
                    if not units and u == 20:
                        dve.wait_ge(c["wo_ps"], TPB * BATCH)
                        hT_lo_d(0)
                    if "in" in sides:
                        if u < TPB:
                            norm_c(b + 1, u)
                        if u == 9:
                            masks(b + 1, 1 - pb)
                        if u == 2:
                            h_c(b + 1, 0)
                        if u == 4:
                            h_c(b + 1, 1)
                    if u - 1 in PIECES and piece_side(PIECES[u - 1]) in sides:
                        piece(PIECES[u - 1], b, pb)
                    if units:
                        maxes(b, u, pb)

            masks(0, 0)
            for name in ORDER:
                if piece_side(name) == "in":
                    if name == "k4T0":
                        h_c(0, 1)
                    if name == "q0":
                        dve.wait_ge(c["wo_hi"], 1)
                        nc.vector.tensor_tensor(wsplit[:, 1, 1, :], wraw[:, 1, :], wsplit[:, 1, 0, :], ALU.subtract).then_inc(w_ready[1], 1)
                    piece(name, -1, 1)
            dve.wait_ge(w_ready[1], SLOT_X // 2 + 1)
            pass_c(0, 0, ("in", "own"))
            with dve.Fori(0, BATCH // 2 - 1) as i:
                for half in range(2):
                    pass_c(2 * i + (1 + half), (1 + half) % 2, ("in", "own", "out"))
            pass_c(BATCH - 1, 1, ("own", "out"))
            chd = Chain(dve, d["dve"])

            def stats_chunk(cc):
                for t in range(TPC):
                    chd.mark(nc.vector.bn_stats(stats_d[:, t, :], acc[:, TPC * cc + t, :]))
                chd.wait(chd.n)
                for t in range(TPC):
                    chd.mark(nc.vector.bn_aggr(mv_d[:, t, :], stats_d[:, t, :]))
                chd.wait(chd.n)
                dve.sem_inc(d["stats"], 1)

            def h_d(cc):
                dve.wait_ge(d["rstd"], cc + 1)
                after(dve, d["hT_ps"], TPC * cc)
                for t in range(TPC):
                    nc.vector.tensor_scalar(hd[:, t, :], acc[:, TPC * cc + t, :], mv_d[:, t, 0:1], ln_d[:, t, 1:2], ALU.subtract,
                                            ALU.mult).then_inc(d["h"], 1)

            def hT_lo_d(cc):
                for t in range(TPC):
                    g = TPC * cc + t
                    dve.wait_ge(d["hT_hi"], g + 1)
                    cols = slice(g * P, (g + 1) * P)
                    nc.vector.tensor_tensor(feat[:, 1, :, cols], ps[:, t + 4 * (cc > 0), :].rearrange("p (k n) -> p k n", k=KB), feat[:, 0, :, cols],
                                            ALU.subtract).then_inc(d["hT"], 1)

            stats_chunk(0)
            pass_c(BATCH, 0, ("out",), 0)
            k, n = piece_turn("wo1", BATCH)
            dve.wait_ge(piece_read[k], n + 1)

            dve.wait_ge(d["iota"], 1)

            def router(cc):
                dve.wait_ge(d["logit_ps"], cc + 1)
                by_part = ps[:, 4, 0:TPC * 2 * EXPERTS].rearrange("p (t a e) -> p t a e", t=TPC, a=2)
                chd.link(nc.vector.tensor_copy(gl[:, 0, :, :], by_part[:, :, 0, :]))
                chd.link(nc.vector.tensor_tensor(gl[:, 0, :, :], by_part[:, :, 1, :], gl[:, 0, :, :], ALU.add))
                dve.sem_inc(d["copied"], 1)
                chd.link(nc.vector.tensor_reduce(gs[:, 0, :], gl[:, 0, :, :], AX.X, ALU.max))

                def per_tile(x):
                    return x.rearrange("p (t o) -> p t o", o=1).broadcast_to([P, TPC, EXPERTS])

                nc.vector.tensor_tensor(gl[:, 1, :, :], gl[:, 0, :, :], per_tile(gs[:, 0, :]), ALU.subtract).then_inc(d["shifted"], 1)
                dve.wait_ge(d["ex"], cc + 1)
                chd.link(nc.vector.tensor_reduce(gs[:, 1, :], gl[:, 2, :, :], AX.X, ALU.add))
                chd.link(nc.vector.reciprocal(gs[:, 2, :], gs[:, 1, :]))
                chd.link(nc.vector.tensor_tensor(gl[:, 3, :, :], gl[:, 2, :, :], per_tile(gs[:, 2, :]), ALU.mult))
                for t in range(TPC):
                    chd.mark(nc.vector.max(gl[:, 4, t, :], gl[:, 3, t, :]))
                chd.wait(chd.n)
                for t in range(TPC):
                    chd.mark(nc.vector.max_index(gi[:, t, :], gl[:, 4, t, :], gl[:, 3, t, :]))
                chd.wait(chd.n)
                chd.link(nc.vector.tensor_copy(gl[:, 5, :, :], gi[:, :, :]))
                iota = iota8[:, :].rearrange("p (o e) -> p o e", o=1).broadcast_to([P, TPC, EXPERTS])
                for j in range(2):
                    chd.mark(nc.vector.tensor_tensor(gl[:, 6 + j, :, :], iota, gl[:, 5, :, j:j + 1].broadcast_to([P, TPC, EXPERTS]), ALU.is_equal))
                chd.wait(chd.n)
                for j in range(2):
                    chd.mark(nc.vector.tensor_tensor(gl[:, 6 + j, :, :], gl[:, 6 + j, :, :],
                                                     gl[:, 4, :, j:j + 1].broadcast_to([P, TPC, EXPERTS]), ALU.mult))
                chd.wait(chd.n)
                chd.link(nc.vector.tensor_tensor(comb[:, TPC * cc:TPC * cc + TPC, :], gl[:, 6, :, :], gl[:, 7, :, :], ALU.add))

            head, steps = mlp_dve(dve, mlp[1], comb)
            stats_chunk(1)
            h_d(1)
            router(0)
            for cc in range(CHUNKS):
                if cc + 2 < CHUNKS:
                    stats_chunk(cc + 2)
                head(cc, cc, [0])
                if cc + 1 < CHUNKS:
                    hT_lo_d(cc + 1)
                head(cc, cc, [1])
                if cc + 2 < CHUNKS:
                    h_d(cc + 2)
                if cc:
                    for t in range(TPC):
                        tile = (cc - 1) * TPC + t
                        dve.wait_ge(mlp[1]["down"], TPC * (cc - 1) + t + 1)
                        nc.vector.tensor_tensor(acc[:, tile, :], ps[:, 4 + t, :], acc[:, tile, :], ALU.add).then_inc(mlp[1]["acc"], 1)
                if cc + 1 < CHUNKS:
                    router(cc + 1)
            steps(CHUNKS - 1, 1, False, None, CHUNKS - 1)
            with dve.Fori(0, EXPERTS // 2 - 1) as i:
                steps(i * (2 * CHUNKS) + CHUNKS, 2, False, 2 * i)
            i = EXPERTS // 2 - 1
            steps(i * 2 * CHUNKS + CHUNKS, 2, True, 2 * i)


def blocks(w_t):
    k, n = w_t.shape
    return w_t.reshape(k // P, P, n).transpose(1, 0, 2).reshape(P, k // P * n)


def group_slot(up, gate, down):
    import numpy as np

    cols = []
    for w in (up, gate):
        t = w.T.reshape(KB, P, JB, P)
        cols.append(t.transpose(1, 2, 0, 3).reshape(P, JB * KB * P))
    cols.append(blocks(down.T))
    return np.concatenate(cols, axis=1)


def kernel(**inputs):
    import numpy as np
    import concourse.bacc as bacc
    from concourse.bass_utils import run_bass_kernel_spmd

    f = {k: np.asarray(v) for k, v in inputs.items()}
    qkv = f["L0_attn_w_qkv"]
    a_w = np.concatenate([blocks(qkv[i * D:(i + 1) * D].T) for i in range(3)], axis=1)
    slots = [a_w[:, :SLOT], a_w[:, SLOT:]]
    sw, wo = f["L0_attn_w_swiglu"], f["L0_attn_w_out"]
    for g in range(MLP_GROUPS):
        u = slice(g * GROUP, (g + 1) * GROUP)
        slots.append(group_slot(sw[:DFF][u], sw[DFF:][u], wo[:, u]))
    order = [(2 * p + half) * (HEADS // KVG) + i for p in range(PAIRS) for i in range(HEADS // KVG) for half in range(2)]
    rows = np.concatenate([np.arange(h * HD, (h + 1) * HD) for h in order])
    kv = np.concatenate([f["L0_xattn_w_k"], f["L0_xattn_w_v"]])
    slots.append(np.concatenate([blocks(f["L0_xattn_w_q"][rows].T), blocks(kv.T)], axis=1))
    o_slot = np.zeros((P, SLOT), np.float32)
    o_slot[:, :KB * D] = blocks(f["L0_xattn_w_o"].T)
    o_slot[:, KB * D:KB * (D + EXPERTS)] = blocks(f["L0_ffn_gate_w"].T)
    o_slot[0, KB * (D + EXPERTS):KB * (D + EXPERTS) + D] = f["L0_xattn_b_o"]
    slots.append(o_slot)
    slots.append(group_slot(f["L0_ffn_ws3"], f["L0_ffn_ws1"], f["L0_ffn_ws2"]))
    for e in range(EXPERTS):
        slots.append(group_slot(f["L0_ffn_w3"][e], f["L0_ffn_w1"][e], f["L0_ffn_w2"][e]))
    arrays = {
        "x": np.ascontiguousarray(f["x"].reshape(BATCH * SEQ, D)),
        "weights": np.ascontiguousarray(np.stack(slots)),
        "ctx_t": np.ascontiguousarray(f["ctx_2048"].reshape(BATCH, SEQ, KB, P).transpose(0, 3, 2, 1)),
        "mask": np.ascontiguousarray(f["mask_BxS2_if1"]),
    }
    nc = bacc.Bacc("TRN2", target_bir_lowering=False, num_devices=1)
    args = [nc.dram_tensor(n, v.shape, mybir.dt.from_np(v.dtype), kind="ExternalInput").ap() for n, v in arrays.items()]
    out = nc.dram_tensor("out", (BATCH * SEQ, D), F32, kind="ExternalOutput").ap()
    decoder_layer(nc, *args, out)
    r = run_bass_kernel_spmd(nc, [arrays], core_ids=[0])
    return r.results[0]["out"].reshape(BATCH, SEQ, D)
```
